# Optimizing a Trainium2 kernel written in Bass

```python
import numpy as np
import jax
import jax.numpy as jnp

def _softmax(x, axis=-1):
    return jax.nn.softmax(x, axis=axis)

def _gelu(x):
    return jax.nn.gelu(x, approximate=True)

def _silu(x):
    return jax.nn.silu(x)

def _sigmoid(x):
    return jax.nn.sigmoid(x)

def _layernorm(x, axis=-1, eps=1e-05):
    m = jnp.mean(x, axis=axis, keepdims=True)
    v = jnp.var(x, axis=axis, keepdims=True)
    return (x - m) / jnp.sqrt(v + eps)

def _scatter_add(tgt, idx, src, axis=0):
    return tgt.at[idx].add(src)

def _segment_sum(src, seg, n):
    return jax.ops.segment_sum(src, seg, n)
kernel_name = 'mk_gnn_preln_d4_gnn_r8_b4bd47'

def setup_inputs(seed: int=0):
    np.random.seed(seed)
    _w = jnp.asarray

    def _rec_inputs():
        import jax
        import jax.numpy as jnp
        _gk = jax.random.key(seed)
        x = 0.5001 + 0.2887 * jax.random.normal(jax.random.fold_in(_gk, 1), (12500, 64), jnp.float32)
        src = jax.random.randint(jax.random.fold_in(_gk, 2), (200000,), 0, 12500, jnp.int32)
        dst = jax.random.randint(jax.random.fold_in(_gk, 3), (200000,), 0, 12500, jnp.int32)
        _o = jnp.argsort(dst, stable=True)
        src = src[_o]
        dst = dst[_o]
        edge_attr_32 = 0.000196303 + 1.00016 * jax.random.normal(jax.random.fold_in(_gk, 12), (200000, 32), jnp.float32)
        edge_type_9 = jax.random.randint(jax.random.fold_in(_gk, 14), (200000,), 0, 9, jnp.int32)
        return (x, src, dst, edge_attr_32, edge_type_9)
    x, src, dst, edge_attr_32, edge_type_9 = _rec_inputs()

    def _L0_gnn_setup():
        import jax, jax.numpy as jnp
        import numpy as np
        N_NODES = 12500
        HIDDEN = 64
        N_REL = 9
        N_LAYERS = 3
        N_EDGES = 125000
        key = jax.random.key(seed)
        k1, k2, k3, k4, k5 = jax.random.split(key, 5)
        edge_index = jax.random.randint(k1, (2, N_EDGES), 0, N_NODES, dtype=jnp.int64)
        edge_type = jax.random.randint(k2, (N_EDGES,), 0, N_REL, dtype=jnp.int64)
        embeddings = jax.random.uniform(k3, (N_NODES, HIDDEN), dtype=jnp.float32)
        weights = jax.random.uniform(k4, (N_LAYERS, 2 * N_REL, HIDDEN, HIDDEN), dtype=jnp.float32)
        biases = jax.random.uniform(k5, (N_LAYERS, 2 * N_REL, HIDDEN), dtype=jnp.float32)
        return {'edge_index': edge_index, 'edge_type': edge_type, 'embeddings': embeddings, 'weights': weights, 'biases': biases}
    _L0_gnn_all = _L0_gnn_setup()
    _L0_gnn_in = {k: v for k, v in _L0_gnn_all.items() if k in ('weights', 'biases')}
    del _L0_gnn_all

    def _L1_gnn_setup():
        import jax, jax.numpy as jnp
        import numpy as np
        N_NODES = 6250
        N_EDGES = 100000
        F_DIM = 64
        AVG_D_LOG = 2.833
        EPS_STD = 1e-05
        EPS_BN = 1e-05
        key = jax.random.key(seed)
        k = jax.random.split(key, 5)
        h = jax.random.normal(k[0], (N_NODES, F_DIM), dtype=jnp.float32)
        src = jax.random.randint(k[1], (N_EDGES,), 0, N_NODES)
        dst = jax.random.randint(k[2], (N_EDGES,), 0, N_NODES)
        W = jax.random.normal(k[3], (12 * F_DIM, F_DIM), dtype=jnp.float32) * 0.02
        b = jnp.zeros((F_DIM,), dtype=jnp.float32)
        gamma = jnp.ones((F_DIM,), dtype=jnp.float32)
        beta = jnp.zeros((F_DIM,), dtype=jnp.float32)
        return {'h': h, 'src': src, 'dst': dst, 'W': W, 'b': b, 'gamma': gamma, 'beta': beta}
    _L1_gnn_all = _L1_gnn_setup()
    _L1_gnn_in = {k: v for k, v in _L1_gnn_all.items() if k in ('W', 'b', 'gamma', 'beta')}
    del _L1_gnn_all

    def _L2_gnn_setup():
        import jax, jax.numpy as jnp
        import numpy as np
        N_NODES = 12500
        key = jax.random.key(seed)
        k1, k2 = jax.random.split(key)
        x = jax.random.normal(k1, (N_NODES, 64), dtype=jnp.float32)
        edge_index = jax.random.randint(k2, (2, 200000), 0, N_NODES, dtype=jnp.int64)
        return {'x': x, 'edge_index': edge_index}
    _L2_gnn_all = _L2_gnn_setup()
    _L2_gnn_in = {k: v for k, v in _L2_gnn_all.items() if k in ()}
    del _L2_gnn_all

    def _L3_gnn_setup():
        import jax, jax.numpy as jnp
        import numpy as np
        N_NODES = 6250
        N_EDGES = 100000
        IN_CH = 64
        OUT_CH = 64
        EDGE_CH = 32
        key = jax.random.key(seed)
        ks = jax.random.split(key, 9)
        s = lambda d: 1.0 / np.sqrt(d)
        return {'x': jax.random.normal(ks[0], (N_NODES, IN_CH), dtype=jnp.float32), 'edge_index': jax.random.randint(ks[1], (2, N_EDGES), 0, N_NODES, dtype=jnp.int64 if jax.config.jax_enable_x64 else jnp.int32), 'edge_attr': jax.random.normal(ks[2], (N_EDGES, EDGE_CH), dtype=jnp.float32), 'We': jax.random.normal(ks[3], (IN_CH, EDGE_CH), dtype=jnp.float32) * s(EDGE_CH), 'be': jax.random.normal(ks[4], (IN_CH,), dtype=jnp.float32) * s(EDGE_CH), 'W1': jax.random.normal(ks[5], (OUT_CH, IN_CH), dtype=jnp.float32) * s(IN_CH), 'b1': jax.random.normal(ks[6], (OUT_CH,), dtype=jnp.float32) * s(IN_CH), 'W2': jax.random.normal(ks[7], (OUT_CH, OUT_CH), dtype=jnp.float32) * s(OUT_CH), 'b2': jax.random.normal(ks[8], (OUT_CH,), dtype=jnp.float32) * s(OUT_CH)}
    _L3_gnn_all = _L3_gnn_setup()
    _L3_gnn_in = {k: v for k, v in _L3_gnn_all.items() if k in ('We', 'be', 'W1', 'b1', 'W2', 'b2')}
    del _L3_gnn_all
    return {'x': x, 'src': src, 'dst': dst, 'edge_attr_32': edge_attr_32, 'edge_type_9': edge_type_9, 'L0_gnn_weights': _L0_gnn_in['weights'], 'L0_gnn_biases': _L0_gnn_in['biases'], 'L1_gnn_W': _L1_gnn_in['W'], 'L1_gnn_b': _L1_gnn_in['b'], 'L1_gnn_gamma': _L1_gnn_in['gamma'], 'L1_gnn_beta': _L1_gnn_in['beta'], 'L3_gnn_We': _L3_gnn_in['We'], 'L3_gnn_be': _L3_gnn_in['be'], 'L3_gnn_W1': _L3_gnn_in['W1'], 'L3_gnn_b1': _L3_gnn_in['b1'], 'L3_gnn_W2': _L3_gnn_in['W2'], 'L3_gnn_b2': _L3_gnn_in['b2']}

def reference(x, src, dst, edge_attr_32, edge_type_9, L0_gnn_weights, L0_gnn_biases, L1_gnn_W, L1_gnn_b, L1_gnn_gamma, L1_gnn_beta, L3_gnn_We, L3_gnn_be, L3_gnn_W1, L3_gnn_b1, L3_gnn_W2, L3_gnn_b2):
    import jax
    import jax.numpy as jnp

    def _L0_gnn_ref(edge_index, edge_type, embeddings, weights, biases):
        import jax, jax.numpy as jnp
        import numpy as np
        N_NODES = 12500
        HIDDEN = 64
        N_REL = 9
        N_LAYERS = 3
        N_EDGES = 125000
        N, E = embeddings.shape
        L = weights.shape[0]
        R = weights.shape[1] // 2
        idx0 = edge_index[0]
        idx1 = edge_index[1]
        rel0 = edge_type
        rel1 = edge_type + R
        output = embeddings
        for l in range(L):
            T = jnp.einsum('ne,reo->rno', embeddings, weights[l])
            m0 = T[rel0, idx0] + biases[l][rel0]
            m1 = T[rel1, idx1] + biases[l][rel1]
            m = jnp.concatenate([m0, m1], axis=0)
            d = jnp.concatenate([idx0, idx1], axis=0)
            s = jax.ops.segment_sum(m, d, num_segments=N)
            cnt = jax.ops.segment_sum(jnp.ones((d.shape[0],), m.dtype), d, num_segments=N)
            hidden = jnp.where(cnt[:, None] > 0, s / jnp.maximum(cnt, 1.0)[:, None], 0.0)
            if l + 1 < L:
                hidden = jax.nn.relu(hidden)
            output = hidden
        return output

    def _L1_gnn_ref(h, src, dst, W, b, gamma, beta):
        import jax, jax.numpy as jnp
        import numpy as np
        N_NODES = 6250
        N_EDGES = 100000
        F_DIM = 64
        AVG_D_LOG = 2.833
        EPS_STD = 1e-05
        EPS_BN = 1e-05
        N = h.shape[0]
        m = h[src]
        ones = jnp.ones((src.shape[0],), dtype=h.dtype)
        deg = jax.ops.segment_sum(ones, dst, num_segments=N)
        s = jax.ops.segment_sum(m, dst, num_segments=N)
        s2 = jax.ops.segment_sum(m * m, dst, num_segments=N)
        mx = jax.ops.segment_max(m, dst, num_segments=N)
        mn = jax.ops.segment_min(m, dst, num_segments=N)
        degc = jnp.maximum(deg, 1.0)[:, None]
        mean = s / degc
        var = jax.nn.relu(s2 / degc - mean * mean)
        std = jnp.sqrt(var + EPS_STD)
        agg = jnp.concatenate([mean, mx, mn, std], axis=1)
        has = (deg > 0)[:, None]
        agg = jnp.where(has, agg, 0.0)
        logD = jnp.log(deg + 1.0)[:, None]
        amp = agg * (logD / AVG_D_LOG)
        att = agg * jnp.where(has, AVG_D_LOG / jnp.maximum(logD, 1e-12), 0.0)
        x = jnp.concatenate([agg, amp, att], axis=1)
        x = x @ W + b
        mu = jnp.mean(x, axis=0)
        v = jnp.var(x, axis=0)
        x = gamma * (x - mu) / jnp.sqrt(v + EPS_BN) + beta
        x = jax.nn.relu(x)
        x = h + x
        return x

    def _L2_gnn_ref(x, edge_index):
        import jax, jax.numpy as jnp
        import numpy as np
        N_NODES = 12500
        dst, src = (edge_index[0], edge_index[1])
        msgs = x[src]
        out = jax.ops.segment_sum(msgs, dst, num_segments=x.shape[0])
        return out

    def _L3_gnn_ref(x, edge_index, edge_attr, We, be, W1, b1, W2, b2):
        import jax, jax.numpy as jnp
        import numpy as np
        N_NODES = 6250
        N_EDGES = 100000
        IN_CH = 64
        OUT_CH = 64
        EDGE_CH = 32
        eps = jnp.float32(0.0)
        row, col = (edge_index[0], edge_index[1])
        edge_embedding = edge_attr @ We.T + be
        messages = jax.nn.relu(x[row] + edge_embedding)
        aggregated = jax.ops.segment_sum(messages, col, num_segments=x.shape[0])
        h = (1.0 + eps) * x + aggregated
        h = jax.nn.relu(h @ W1.T + b1)
        return h @ W2.T + b2
    edge_index = jnp.stack([src, dst])
    h = jnp.maximum(_layernorm(x, axis=-1), 0.0)
    x = x + _L0_gnn_ref(edge_index, edge_type_9, h, L0_gnn_weights, L0_gnn_biases)
    h = jnp.maximum(_layernorm(x, axis=-1), 0.0)
    x = x + _L1_gnn_ref(h, src, dst, L1_gnn_W, L1_gnn_b, L1_gnn_gamma, L1_gnn_beta)
    h = jnp.maximum(_layernorm(x, axis=-1), 0.0)
    x = x + _L2_gnn_ref(h, edge_index)
    h = jnp.maximum(_layernorm(x, axis=-1), 0.0)
    x = x + _L3_gnn_ref(h, edge_index, edge_attr_32, L3_gnn_We, L3_gnn_be, L3_gnn_W1, L3_gnn_b1, L3_gnn_W2, L3_gnn_b2)
    return x

_drawn_inputs = setup_inputs


def setup_inputs(seed=0):
    import zlib

    import numpy as np

    out = dict(_drawn_inputs(seed))
    spreads = {'L1_gnn_b': (0.0, 0.8), 'L1_gnn_gamma': (1.0, 0.2), 'L1_gnn_beta': (0.0, 0.272)}
    factors = {'L3_gnn_b1': 8.0, 'L3_gnn_b2': 8.0}
    for name, (base, spread) in spreads.items():
        noise = np.random.default_rng([zlib.crc32(name.encode()), seed]).standard_normal(out[name].shape)
        drawn = base * np.exp(spread * noise) if base else spread * noise
        out[name] = jnp.asarray(drawn.astype(out[name].dtype))
    for name, factor in factors.items():
        out[name] = (out[name] * factor).astype(out[name].dtype)
    return out
```

```python
import concourse.bass as bass
from concourse import mybir
from contextlib import ExitStack

FP32 = mybir.dt.float32
BF16 = mybir.dt.bfloat16
FP16 = mybir.dt.float16
I32 = mybir.dt.int32
ALU = mybir.AluOpType
ACT = mybir.ActivationFunctionType
AX = mybir.AxisListType

P = 128
NODES, F, EDGES, EDGE_F, REL = 12500, 64, 200000, 32, 9
NT = -(-NODES // P)
NPAD = NT * P
LAST = NPAD - 1
TILES = 1568
EPAD = TILES * P
BODY = 8
GRP = 4
ITERS = TILES // BODY
KEYS = NT * REL
KH = KEYS // 2
REPS = 4
REP_ROWS = NPAD + P
E_ROWS = EPAD + NPAD
ZW = REP_ROWS * F // P
ZE = E_ROWS * F // P // 17
CH = 14
NCH = NT // CH
AVG_D_LOG = 2.833
EPS = 1e-5
BIG = 1e30


def build(nc, x3, srcT, dstT, dstprevT, typeT, heads, attrT, w0, w1, b1r, gam, bet,
          weT, bec, g1T, g1b, g2T, g2b, out):
    ctx = ExitStack()
    with ctx:
        def sb(name, shape, dt=FP32):
            return ctx.enter_context(nc.sbuf_tensor(name, shape, dt))

        names = {}

        def unique(name):
            names[name] = names.get(name, 0) + 1
            return f"{name}_{names[name]}"

        def sem(name):
            return ctx.enter_context(nc.semaphore(name))

        def sems(name, n):
            return [sem(f"{name}{i}") for i in range(n)]

        bank = [ctx.enter_context(nc.psum_tensor(f"bank{i}", [P, 512], FP32)) for i in range(8)]

        htab = [nc.dram_tensor(f"htab{i}", [NPAD, w], FP32).ap() for i, w in enumerate((2 * F, F, F))]
        r1 = nc.dram_tensor("r1", [EPAD, 4 * F], FP32).ap()
        r3 = nc.dram_tensor("r3", [EPAD, F], FP32).ap()
        first_rows = nc.dram_tensor("first_rows", [E_ROWS, F], FP32).ap()
        rep = [nc.dram_tensor(f"rep{i}", [REP_ROWS, F], FP32).ap() for i in range(REPS)]

        X = sb("X", [P, NT, F])
        H = sb("H", [P, NT, F])
        Y = sb("Y", [P, NT, F])
        Z = sb("Z", [P, ZW])
        SQ = Z[:, 0:NT * F].rearrange("p (a f) -> p a f", f=F)
        src_i = sb("src_i", [P, TILES + BODY], I32)
        src_f = sb("src_f", [P, TILES])
        dst_f = sb("dst_f", [P, TILES])
        key_src = sb("key_src", [P, TILES])
        key_dst = sb("key_dst", [P, TILES])
        src_hi, src_lo, dst_hi, dst_lo, gate_sum, gate_max = (
            sb(n, [P, TILES], BF16) for n in ("src_hi", "src_lo", "dst_hi", "dst_lo", "gate_sum", "gate_max"))
        ident = sb("ident", [P, P])
        ident_b = sb("ident_b", [P, P], BF16)
        ones = sb("ones", [P, P])
        upto = sb("upto", [P, P])
        before = sb("before", [P, P])
        spare_row = sb("spare_row", [P, 1])
        real = sb("real", [P, 1])
        eps_c = sb("eps_c", [P, 1])
        C = sb("C", [P, NT, 2 * REL])
        col = {n: sb("col_" + n, [P, NT]) for n in
               ("cnt", "deg", "rcnt", "has", "neghas", "rdeg", "end", "amp", "att", "t0", "t1", "mean", "rstd")}
        end_i = sb("end_i", [P, NT], I32)
        start_i = sb("start_i", [P, NT], I32)
        heads_i = sb("heads_i", [P, 13], I32)

        ldx, ldi, cst, prep = sem("ldx"), sems("ldi", 5), sem("cst"), sem("prep")
        pool_passed, pe_passed = sem("pool_passed"), sem("pe_passed")
        with ExitStack() as st:
            def tmp(name, shape, dt=FP32):
                return st.enter_context(nc.sbuf_tensor(unique(name), shape, dt))
            dst_i = tmp("dst_i", [P, TILES], I32)
            dstprev_i = tmp("dstprev_i", [P, TILES], I32)
            type_i = tmp("type_i", [P, TILES], I32)
            ia = tmp("ia", [P, TILES], I32)
            ib = tmp("ib", [P, TILES], I32)
            with nc.Block() as block:
                @block.sync
                def _(sp):
                    sp.dma_start(src_i[:, 0:TILES], srcT).then_inc(ldi[0], 16)
                    sp.dma_start(dst_i[:, :], dstT).then_inc(ldi[1], 16)
                    sp.dma_start(type_i[:, :], typeT).then_inc(ldi[2], 16)
                    sp.dma_start(dstprev_i[:, :], dstprevT).then_inc(ldi[3], 16)
                    sp.dma_start(heads_i[:, :], heads).then_inc(ldi[4], 16)
                    sp.dma_start(X[:, :, :], x3).then_inc(ldx, 16)
                    sp.wait_ge(ldx, 16)
                    sp.wait_ge(ldi[4], 16)

                @block.gpsimd
                def _(pool):
                    pool.memset(ident[:, :], 0.0).then_inc(cst, 1)
                    pool.memset(ones[:, :], 1.0).then_inc(cst, 1)
                    pool.memset(real[:, :], 1.0).then_inc(cst, 1)
                    pool.memset(eps_c[:, :], EPS).then_inc(cst, 1)
                    pool.iota(spare_row[:, :], [[0, 1]], base=NPAD, channel_multiplier=1,
                              allow_small_or_imprecise_dtypes=True).then_inc(cst, 1)
                    pool.wait_ge(cst, 5)
                    pool.affine_select(out=ident[:, :], in_=ident[:, :], compare_op=ALU.not_equal, fill=1.0,
                                       base=0, pattern=[[-1, P]], channel_multiplier=1).then_inc(cst, 1)
                    pool.affine_select(out=upto[:, :], in_=ones[:, :], compare_op=ALU.is_ge, fill=0.0,
                                       base=0, pattern=[[1, P]], channel_multiplier=-1).then_inc(cst, 1)
                    pool.affine_select(out=before[:, :], in_=ones[:, :], compare_op=ALU.is_gt, fill=0.0,
                                       base=0, pattern=[[-1, P]], channel_multiplier=1).then_inc(cst, 1)
                    pool.affine_select(out=real[:, :], in_=real[:, :], compare_op=ALU.is_gt, fill=0.0,
                                       base=NODES - (NT - 1) * P, pattern=[[0, 1]],
                                       channel_multiplier=-1).then_inc(cst, 1)

                @block.vector
                def _(dve):
                    n = [0]

                    def step(ins):
                        ins.then_inc(prep, 1)
                        n[0] += 1

                    def seen():
                        dve.wait_ge(prep, n[0])

                    step(dve.memset(src_i[:, TILES:TILES + BODY], 0))
                    for s in ldi[:4]:
                        dve.wait_ge(s, 16)
                    step(dve.tensor_copy(src_f[:, :], src_i[:, 0:TILES]))
                    step(dve.tensor_copy(dst_f[:, :], dst_i[:, :]))
                    step(dve.tensor_tensor(gate_sum[:, :], dst_i[:, :], dstprev_i[:, :], ALU.is_equal))
                    step(dve.tensor_copy(key_src[:, :], type_i[:, :]))
                    step(dve.tensor_copy(key_dst[:, :], type_i[:, :]))
                    step(dve.memset(Z[:, :], 0.0))
                    seen()
                    step(dve.tensor_scalar(gate_max[:, :], gate_sum[:, :], 1.0, BIG, ALU.subtract, ALU.mult))
                    for e_i, lo, hi, key in ((src_i[:, 0:TILES], src_lo, src_hi, key_src), (dst_i[:, :], dst_lo, dst_hi, key_dst)):
                        seen()
                        step(dve.tensor_single_scalar(ia[:, :], e_i, P - 1, ALU.bitwise_and))
                        step(dve.tensor_single_scalar(ib[:, :], e_i, 7, ALU.arith_shift_right))
                        seen()
                        step(dve.tensor_copy(lo[:, :], ia[:, :]))
                        step(dve.tensor_scalar(hi[:, :], ib[:, :], float(P), None, ALU.mult))
                        step(dve.scalar_tensor_tensor(key[:, :], ib[:, :], float(REL), key[:, :], ALU.mult, ALU.add))
                    dve.wait_ge(cst, 6)
                    step(dve.tensor_copy(ident_b[:, :], ident[:, :]))

        zdone = sems("zdone", 2)
        oh_ready, oh_used, cnt_done, hz = sem("oh_ready"), sem("oh_used"), sem("cnt_done"), sem("hz")
        with ExitStack() as st:
            def tmp(name, shape, dt=FP32):
                return st.enter_context(nc.sbuf_tensor(unique(name), shape, dt))
            iota_p = tmp("iota_p", [P, P], BF16)
            iota_k = tmp("iota_k", [P, KEYS], FP16)
            onehot_p = tmp("onehot_p", [P, 4, 2, P], BF16)
            onehot_k = tmp("onehot_k", [P, 4, 2, KEYS], BF16)
            zero_b = tmp("zero_b", [P, KH], BF16)
            with nc.Block() as block:
                @block.sync
                def _(sp):
                    ev = first_rows.rearrange("(z p n) f -> z p (n f)", p=P, z=17)
                    for z in range(17):
                        sp.dma_start(ev[z], Z[:, 0:ZE]).then_inc(zdone[0], 16)
                    for r in range(REPS):
                        sp.dma_start(rep[r].rearrange("(p n) f -> p (n f)", p=P), Z[:, :]).then_inc(zdone[1], 16)
                    sp.wait_ge(zdone[0], 17 * 16)
                    sp.wait_ge(zdone[1], REPS * 16)

                @block.gpsimd
                def _(pool):
                    pool.iota(iota_p[:, :], [[1, P]], base=0, channel_multiplier=0,
                              allow_small_or_imprecise_dtypes=True).then_inc(hz, 1)
                    pool.iota(iota_k[:, :], [[1, KEYS]], base=0, channel_multiplier=0,
                              allow_small_or_imprecise_dtypes=True).then_inc(hz, 1)
                    pool.memset(zero_b[:, :], 0.0).then_inc(hz, 1)

                @block.vector
                def _(dve):
                    dve.wait_ge(hz, 2)
                    dve.sem_inc(oh_used, 4)
                    with dve.Fori(0, TILES // 4) as i:
                        for k in range(4):
                            t = bass.ds(i * 4 + k, 1)
                            dve.wait_ge(oh_used, i * 4 + k + 1)
                            for side, lo, key in ((0, src_lo, key_src), (1, dst_lo, key_dst)):
                                dve.tensor_scalar(onehot_p[:, k, side, :], iota_p[:, :], lo[:, t], None,
                                                  ALU.is_equal).then_inc(oh_ready, 1)
                                dve.tensor_scalar(onehot_k[:, k, side, :], iota_k[:, :], key[:, t], None,
                                                  ALU.is_equal).then_inc(oh_ready, 1)
                    dve.wait_ge(cnt_done, 1)
                    for side in range(2):
                        for half in range(2):
                            dve.tensor_copy(C[:, half * 49:half * 49 + 49, side * REL:side * REL + REL],
                                            bank[2 * side + half][:, 0:KH].rearrange("p (a r) -> p a r", r=REL)
                                            ).then_inc(prep, 1)

                @block.tensor
                def _(pe):
                    pe.wait_ge(hz, 3)
                    for b in range(4):
                        pe.matmul(bank[b][:, 0:KH], zero_b[:, 0:P], zero_b[:, :], start=True, stop=False,
                                  skip_group_check=True)
                    with pe.Fori(0, TILES // 4) as i:
                        for k in range(4):
                            for side in range(2):
                                pe.wait_ge(oh_ready, (i * 4 + k) * 4 + 2 * side + 2)
                                for half in range(2):
                                    mm = pe.matmul(bank[2 * side + half][:, 0:KH], onehot_p[:, k, side, :],
                                                   onehot_k[:, k, side, half * KH:half * KH + KH],
                                                   start=False, stop=False, skip_group_check=True)
                            mm.then_inc(oh_used, 1)
                    pe.matmul(bank[3][:, 0:KH], zero_b[:, 0:P], zero_b[:, :], start=False, stop=True,
                              skip_group_check=True).then_inc(cnt_done, 1)

        nn = [0]
        nd, nd_pe, nd_io, nd_act = sem("nd"), sem("nd_pe"), sem("nd_io"), sem("nd_act")
        with ExitStack() as st:
            def tmp(name, shape, dt=FP32):
                return st.enter_context(nc.sbuf_tensor(unique(name), shape, dt))
            node_id = tmp("node_id", [P, NT])
            ta = tmp("ta", [P, NT])
            tb = tmp("tb", [P, NT])
            with nc.Block() as block:
                @block.gpsimd
                def _(pool):
                    pool.iota(node_id[:, :], [[P, NT]], base=EPAD, channel_multiplier=1,
                              allow_small_or_imprecise_dtypes=True).then_inc(nd_io, 1)

                @block.vector
                def _(dve):
                    def step(ins):
                        ins.then_inc(nd, 1)
                        nn[0] += 1
                        dve.wait_ge(nd, nn[0])
                    step(dve.tensor_reduce(col["deg"][:, :], C[:, :, REL:2 * REL], AX.X, ALU.add))
                    step(dve.tensor_reduce(col["cnt"][:, :], C[:, :, :], AX.X, ALU.add))
                    step(dve.tensor_scalar(ta[:, :], col["cnt"][:, :], 1.0, None, ALU.max))
                    step(dve.reciprocal(col["rcnt"][:, :], ta[:, :]))
                    step(dve.tensor_scalar(col["has"][:, :], col["deg"][:, :], 1.0, None, ALU.min))
                    step(dve.tensor_scalar(col["neghas"][:, :], col["has"][:, :], -1.0, None, ALU.mult))
                    step(dve.tensor_scalar(ta[:, :], col["deg"][:, :], 1.0, None, ALU.max))
                    step(dve.reciprocal(tb[:, :], ta[:, :]))
                    step(dve.tensor_tensor(col["rdeg"][:, :], tb[:, :], col["has"][:, :], ALU.mult))
                    dve.wait_ge(nd_pe, 1)
                    step(dve.tensor_copy(ta[:, :], bank[5][:, 0:NT]))
                    step(dve.tensor_tensor_scan(tb[:, :], ones[:, 0:NT], ta[:, :], 0.0, ALU.mult, ALU.add))
                    step(dve.tensor_tensor(tb[:, :], tb[:, :], ta[:, :], ALU.subtract))
                    step(dve.tensor_tensor(col["end"][:, :], bank[4][:, 0:NT], tb[:, :], ALU.add))
                    step(dve.tensor_scalar(end_i[:, :], col["end"][:, :], 1.0, 0.0, ALU.subtract, ALU.max))
                    dve.wait_ge(nd_io, 1)
                    step(dve.tensor_tensor(ta[:, :], col["end"][:, :], col["deg"][:, :], ALU.subtract))
                    step(dve.tensor_tensor(ta[:, :], ta[:, :], node_id[:, :], ALU.subtract))
                    step(dve.tensor_tensor(ta[:, :], ta[:, :], col["has"][:, :], ALU.mult))
                    step(dve.tensor_tensor(start_i[:, :], ta[:, :], node_id[:, :], ALU.add))
                    dve.wait_ge(nd_act, 1)
                    step(dve.tensor_scalar(ta[:, :], col["t0"][:, :], 1e-12, None, ALU.max))
                    step(dve.reciprocal(tb[:, :], ta[:, :]))
                    step(dve.scalar_tensor_tensor(col["att"][:, :], tb[:, :], AVG_D_LOG, col["has"][:, :],
                                                  ALU.mult, ALU.mult))
                    step(dve.tensor_scalar(col["amp"][:, :], col["t0"][:, :], 1.0 / AVG_D_LOG, None, ALU.mult))

                @block.tensor
                def _(pe):
                    pe.wait_ge(nd, 1)
                    pe.matmul(bank[4][:, 0:NT], upto[:, :], col["deg"][:, :], start=True, stop=True)
                    pe.matmul(bank[5][:, 0:NT], ones[:, :], col["deg"][:, :], start=True, stop=True
                              ).then_inc(nd_pe, 1)

                @block.scalar
                def _(act):
                    act.wait_ge(nd, 1)
                    act.activation(col["t0"][:, :], col["deg"][:, :], ACT.Ln, bias=1.0).then_inc(nd_act, 1)

        def norm(i, table, negative=False):
            v, a, d, neg = sem(f"ln_v{i}"), sem(f"ln_a{i}"), sems(f"ln_d{i}", 2), sem(f"ln_n{i}")
            n = [0]
            mean_b = col["mean"][:, :].unsqueeze(2).broadcast_to([P, NT, F])
            rstd_b = col["rstd"][:, :].unsqueeze(2).broadcast_to([P, NT, F])
            with nc.Block() as block:
                @block.vector
                def _(dve):
                    def step(ins):
                        ins.then_inc(v, 1)
                        n[0] += 1
                        dve.wait_ge(v, n[0])
                    step(dve.tensor_reduce(col["t0"][:, :], X[:, :, :], AX.X, ALU.add))
                    step(dve.tensor_scalar(col["mean"][:, :], col["t0"][:, :], 1.0 / F, None, ALU.mult))
                    step(dve.tensor_tensor(H[:, :, :], X[:, :, :], mean_b, ALU.subtract))
                    dve.wait_ge(a, 1)
                    step(dve.tensor_reduce(col["t0"][:, :], SQ, AX.X, ALU.add))
                    dve.wait_ge(a, 2)
                    step(dve.reciprocal(col["rstd"][:, :], col["t1"][:, :]))
                    step(dve.scalar_tensor_tensor(H[:, :, :], H[:, :, :], 0.0, rstd_b, ALU.max, ALU.mult))

                @block.scalar
                def _(act):
                    act.wait_ge(v, 3)
                    act.activation(SQ, H[:, :, :], ACT.Square).then_inc(a, 1)
                    act.wait_ge(v, 4)
                    act.activation(col["t1"][:, :], col["t0"][:, :], ACT.Sqrt, bias=eps_c[:, :],
                                   scale=1.0 / F).then_inc(a, 1)

                @block.gpsimd
                def _(pool):
                    if negative:
                        pool.wait_ge(v, 6)
                        pool.tensor_scalar(Y[:, :, :], H[:, :, :], -1.0, None, ALU.mult).then_inc(neg, 1)

                @block.sync
                def _(sp):
                    if table is not None:
                        tv = table.rearrange("(a p) f -> p a f", p=P)
                        sp.wait_ge(v, 6)
                        sp.dma_start(tv[:, :, 0:F], H[:, :, :]).then_inc(d[0], 16)
                        if negative:
                            sp.wait_ge(neg, 1)
                            sp.dma_start(tv[:, :, F:2 * F], Y[:, :, :]).then_inc(d[1], 16)
                            sp.wait_ge(d[1], 16)
                        sp.wait_ge(d[0], 16)

        def relational():
            hs_ready, hs_used = sem("hs_ready"), sem("hs_used")
            hT_psum, hT_ready, hT_used = sem("hT_psum"), sem("hT_ready"), sem("hT_used")
            m_ready, m_used, v, wl, on = sem("m_ready"), sem("m_used"), sem("rel_v"), sem("rel_w"), sem("rel_on")
            with ExitStack() as st:
                def tmp(name, shape, dt=FP32):
                    return st.enter_context(nc.sbuf_tensor(unique(name), shape, dt))
                W = tmp("W", [F + 1, 2 * REL * F])
                hs = tmp("hs", [P, 2, F])
                hT = tmp("hT", [F + 1, 2, P])
                prod = tmp("prod", [P, 2 * REL, F])
                res = tmp("res", [P, F])
                with nc.Block() as block:
                    @block.sync
                    def _(sp):
                        sp.dma_start(W[:, :], w0).then_inc(wl, 16)

                    @block.gpsimd
                    def _(pool):
                        pool.memset(hT[F:F + 1, :, :], 1.0).then_inc(on, 1)
                        pool.wait_ge(on, 1)
                        pool.sem_inc(hs_used, 2)
                        with pool.Fori(0, NT // 2) as i:
                            for k in range(2):
                                pool.wait_ge(hs_used, i * 2 + k + 1)
                                pool.tensor_copy(hs[:, k, :].unsqueeze(1), H[:, bass.ds(i * 2 + k, 1), :]
                                                 ).then_inc(hs_ready, 1)

                    @block.tensor
                    def _(pe):
                        pe.wait_ge(wl, 16)
                        pe.wait_ge(on, 1)
                        with pe.Fori(0, NT // 2) as i:
                            for k in range(2):
                                pe.wait_ge(hs_ready, i * 2 + k + 1)
                                pe.wait_ge(hT_used, i * 2 + k + 1)
                                pe.sem_inc(pe_passed, 1)
                                pe.transpose(bank[6 + k][0:F, 0:P], hs[:, k, :], ident[:, :]
                                             ).then_inc(hT_psum, 1)
                                pe.wait_ge(hT_ready, i * 2 + k + 1)
                                for c in range(3):
                                    pe.wait_ge(m_used, (i * 2 + k) * 3 + c + 1)
                                    pe.matmul(bank[3 * k + c][:, 0:384], hT[:, k, :],
                                              W[:, 384 * c:384 * c + 384], start=True, stop=True
                                              ).then_inc(m_ready, 1)

                    @block.scalar
                    def _(act):
                        act.sem_inc(hT_used, 2)
                        with act.Fori(0, NT // 2) as i:
                            for k in range(2):
                                act.wait_ge(hT_psum, i * 2 + k + 1)
                                act.wait_ge(m_ready, (i * 2 + k) * 3 - 3 * k)
                                act.activation(hT[0:F, k, :], bank[6 + k][0:F, 0:P], ACT.Copy
                                               ).then_inc(hT_ready, 1)
                                act.sem_inc(hT_used, 1)
                                act.sem_inc(hs_used, 1)

                    @block.vector
                    def _(dve):
                        dve.sem_inc(m_used, 6)
                        with dve.Fori(0, NT // 2) as i:
                            for k in range(2):
                                a = bass.ds(i * 2 + k, 1)
                                for c in range(3):
                                    dve.wait_ge(m_ready, (i * 2 + k) * 3 + c + 1)
                                    cb = C[:, a, 6 * c:6 * c + 6].rearrange("p a r -> p (a r)").unsqueeze(2)
                                    dve.tensor_tensor(prod[:, 6 * c:6 * c + 6, :],
                                                      bank[3 * k + c][:, 0:384].rearrange("p (r f) -> p r f", f=F),
                                                      cb.broadcast_to([P, 6, F]), ALU.mult).then_inc(m_used, 1)
                                dve.wait_ge(m_used, (i * 2 + k) * 3 + 9)
                                dve.tensor_reduce(res[:, :], prod[:, :, :].rearrange("p r f -> p f r"), AX.X,
                                                  ALU.add).then_inc(v, 1)
                                dve.wait_ge(v, (i * 2 + k) * 2 + 1)
                                dve.scalar_tensor_tensor(X[:, a, :], res[:, :].unsqueeze(1), col["rcnt"][:, a],
                                                         X[:, a, :], ALU.mult, ALU.add).then_inc(v, 1)
                                dve.wait_ge(v, (i * 2 + k) * 2 + 2)

        def pna_edges():
            win_ready, gathered = sem("pe_win_ready"), sems("pe_gathered", BODY)
            t_done, d_done, gates_done = sem("pe_t_done"), sem("pe_d_done"), sem("pe_gates_done")
            s_done, o6_done, back_done = sem("pe_s_done"), sem("pe_o6_done"), sem("pe_back_done")
            w_act, w_dve, sent = sem("pe_w_act"), sem("pe_w_dve"), sems("pe_sent", 2)
            with ExitStack() as st:
                def tmp(name, shape, dt=FP32):
                    return st.enter_context(nc.sbuf_tensor(unique(name), shape, dt))
                win = tmp("win", [P, 2, GRP], I32)
                G = tmp("G", [P, BODY, 2 * F])
                D = tmp("D", [P, 2, 2, GRP * P])
                S = tmp("S", [P, 2, 2, GRP * P])
                Wo = tmp("Wo", [P, 2, GRP, 4 * F])
                out_v = r1.rearrange("(t p) f -> p t f", p=P)
                with nc.Block() as block:
                    @block.gpsimd
                    def _(pool):
                        with pool.Fori(0, ITERS) as i:
                            for g in range(2):
                                pool.wait_ge(win_ready, i * 2 + g + 1)
                                for k in range(GRP):
                                    s = g * GRP + k
                                    pool.wait_ge(t_done, i * BODY + s + 1)
                                    pool.sem_inc(pool_passed, 1)
                                    pool.indirect_dma_start(
                                        G[:, s, :], None, htab[0],
                                        bass.IndirectOffsetOnAxis(win[:, g, k:k + 1], 0),
                                        bounds_check=NPAD - 1, oob_is_err=True).then_inc(gathered[s], 16)

                    @block.tensor
                    def _(pe):
                        pe.sem_inc(t_done, BODY)
                        pe.sem_inc(back_done, 2)

                        def front(n, i, g):
                            pe.wait_ge(d_done, n * 3 + 3)
                            for k in range(GRP):
                                s = g * GRP + k
                                pe.wait_ge(gathered[s], i * 16 + 16)
                                pe.transpose(bank[g][:, k * P:k * P + P], G[:, s, :], ident[:, :]).then_inc(t_done, 1)
                            pe.wait_ge(s_done, n * 2 + 2)
                            for b, gate in ((2, gate_sum), (4, gate_max)):
                                for k in range(GRP):
                                    mm = pe.matmul(bank[b + g][:, k * P:k * P + P],
                                                   gate[:, bass.ds(n * GRP + k, 1)].broadcast_to([P, P]),
                                                   ident_b[:, :], start=True, stop=True)
                            mm.then_inc(gates_done, 1)

                        def back(n, g):
                            pe.wait_ge(s_done, n * 2 + 6)
                            for half, read in ((0, w_act), (1, w_dve)):
                                pe.wait_ge(read, n)
                                for k in range(2):
                                    for q in range(2):
                                        c = (half * 2 + k) * P
                                        tr = pe.transpose(bank[6 + half][:, (k * 2 + q) * P:(k * 2 + q) * P + P],
                                                          S[:, g, q, c:c + P], ident[:, :])
                                tr.then_inc((o6_done, back_done)[half], 1)

                        front(0, 0, 0)
                        with pe.Fori(0, ITERS - 1) as i:
                            front(i * 2 + 1, i, 1)
                            back(i * 2, 0)
                            front(i * 2 + 2, i + 1, 0)
                            back(i * 2 + 1, 1)
                        front(2 * ITERS - 1, ITERS - 1, 1)
                        back(2 * ITERS - 2, 0)
                        back(2 * ITERS - 1, 1)

                    @block.scalar
                    def _(act):
                        act.sem_inc(d_done, 6)

                        def operands(n, g):
                            act.wait_ge(t_done, n * GRP + GRP + BODY)
                            act.wait_ge(s_done, n * 2 + 2)
                            act.activation(D[0:F, g, 0, :], bank[g][0:F, :], ACT.Copy).then_inc(d_done, 1)
                            act.activation(D[F:P, g, 0, :], bank[g][F:P, :], ACT.Square).then_inc(d_done, 1)
                            act.activation(D[:, g, 1, :], bank[g][:, :], ACT.Copy).then_inc(d_done, 1)

                        def evacuate(n, i, g):
                            act.wait_ge(o6_done, n + 1)
                            act.wait_ge(sent[g], i * 16)
                            act.activation(Wo[:, g, 0:2, :].rearrange("p k f -> p (k f)"), bank[6][:, :], ACT.Copy
                                           ).then_inc(w_act, 1)

                        operands(0, 0)
                        with act.Fori(0, ITERS - 1) as i:
                            operands(i * 2 + 1, 1)
                            evacuate(i * 2, i, 0)
                            operands(i * 2 + 2, 0)
                            evacuate(i * 2 + 1, i, 1)
                        operands(2 * ITERS - 1, 1)
                        evacuate(2 * ITERS - 2, ITERS - 1, 0)
                        evacuate(2 * ITERS - 1, ITERS - 1, 1)

                    @block.vector
                    def _(dve):
                        dve.memset(S[:, 1, :, GRP * P - 1:GRP * P], 0.0).then_inc(s_done, 4)

                        def window(n, g):
                            dve.tensor_copy(win[:, g, :], src_i[:, bass.ds(n * GRP, GRP)]).then_inc(win_ready, 1)

                        def scans(n, i, g):
                            dve.wait_ge(gates_done, n + 1)
                            dve.wait_ge(back_done, n + 1)
                            for q, b, op0, op1 in ((0, 2, ALU.mult, ALU.add), (1, 4, ALU.add, ALU.max)):
                                dve.wait_ge(d_done, n * 3 + 8 + q)
                                dve.wait_ge(s_done, n * 2 + 3 + q)
                                dve.tensor_tensor_scan(S[:, g, q, :], bank[b + g][:, :], D[:, g, q, :],
                                                       S[:, 1 - g, q, GRP * P - 1:GRP * P], op0, op1
                                                       ).then_inc(s_done, 1)
                            for k in range(GRP):
                                dve.wait_ge(gathered[g * GRP + k], i * 16 + 16)
                            window(n + 2, g)

                        def evacuate(n, i, g):
                            dve.wait_ge(back_done, n + 3)
                            dve.wait_ge(sent[g], i * 16)
                            dve.tensor_copy(Wo[:, g, 2:4, :].rearrange("p k f -> p (k f)"), bank[7][:, :]
                                            ).then_inc(w_dve, 1)

                        window(0, 0)
                        window(1, 1)
                        scans(0, 0, 0)
                        with dve.Fori(0, ITERS - 1) as i:
                            scans(i * 2 + 1, i, 1)
                            evacuate(i * 2, i, 0)
                            scans(i * 2 + 2, i + 1, 0)
                            evacuate(i * 2 + 1, i, 1)
                        scans(2 * ITERS - 1, ITERS - 1, 1)
                        evacuate(2 * ITERS - 2, ITERS - 1, 0)
                        evacuate(2 * ITERS - 1, ITERS - 1, 1)

                    @block.sync
                    def _(sp):
                        with sp.Fori(0, ITERS) as i:
                            for g in range(2):
                                n = i * 2 + g
                                sp.wait_ge(w_act, n + 1)
                                sp.wait_ge(w_dve, n + 1)
                                sp.dma_start(out_v[:, bass.ds(n * GRP, GRP), :], Wo[:, g, :, :]
                                             ).then_inc(sent[g], 16)
                        for g in range(2):
                            sp.wait_ge(sent[g], ITERS * 16)

        def pna_nodes():
            wl, win_done, fetched, r_read = sems("pn_wl", 4), sem("pn_win"), sem("pn_fetched"), sem("pn_r_read")
            v, var_done, std_done, agg_done = sem("pn_v"), sem("pn_var"), sem("pn_std"), sem("pn_agg")
            t_done, aT_done, y_done, y_read = sem("pn_t"), sem("pn_aT"), sem("pn_y"), sem("pn_yread")
            bn, bn_pe, bn_act = sem("pn_bn"), sem("pn_bn_pe"), sem("pn_bn_act")
            with ExitStack() as st:
                def tmp(name, shape, dt=FP32):
                    return st.enter_context(nc.sbuf_tensor(unique(name), shape, dt))
                win = tmp("win", [P, CH], I32)
                R = tmp("R", [P, CH, 4 * F])
                A = tmp("A", [P, CH, 4 * F])
                ms = tmp("ms", [P, CH, F])
                aT = tmp("aT", [P, 2, 2, P])
                W = tmp("W", [P, 2, 3 * F])
                bias = tmp("bias", [P, F])
                gamma = tmp("gamma", [P, F])
                beta = tmp("beta", [P, F])
                acc = tmp("acc", [P, F])
                mu = tmp("mu", [P, F])
                fac = tmp("fac", [P, F])
                fac2 = tmp("fac2", [P, F])
                with nc.Block() as block:
                    @block.sync
                    def _(sp):
                        sp.dma_start(W[:, :, :], w1).then_inc(wl[0], 16)
                        sp.dma_start(bias[:, :], b1r).then_inc(wl[1], 16)
                        sp.dma_start(gamma[:, :], gam).then_inc(wl[2], 16)
                        sp.dma_start(beta[:, :], bet).then_inc(wl[3], 16)

                    @block.gpsimd
                    def _(pool):
                        with pool.Fori(0, NCH) as c:
                            pool.wait_ge(fetched, c * (CH * 16))
                            pool.tensor_copy(win[:, :], end_i[:, bass.ds(c * CH, CH)]).then_inc(win_done, 1)
                            pool.wait_ge(win_done, c + 1)
                            pool.wait_ge(r_read, c * 5)
                            for k in range(CH):
                                pool.sem_inc(pool_passed, 1)
                                pool.indirect_dma_start(R[:, k, :], None, r1,
                                                        bass.IndirectOffsetOnAxis(win[:, k:k + 1], 0),
                                                        bounds_check=EPAD - 1, oob_is_err=True
                                                        ).then_inc(fetched, 16)

                    @block.vector
                    def _(dve):
                        for s in wl[1:]:
                            dve.wait_ge(s, 16)
                        dve.sem_inc(y_read, 6)
                        with dve.Fori(0, NCH) as c:
                            def per_node(name):
                                return col[name][:, bass.ds(c * CH, CH)].unsqueeze(2).broadcast_to([P, CH, F])
                            dve.wait_ge(fetched, c * (CH * 16) + CH * 16)
                            dve.wait_ge(t_done, c * CH)
                            dve.tensor_tensor(A[:, :, 0:F], R[:, :, 0:F], per_node("rdeg"), ALU.mult
                                              ).then_inc(r_read, 1)
                            dve.tensor_tensor(A[:, :, 3 * F:4 * F], R[:, :, F:2 * F], per_node("rdeg"), ALU.mult
                                              ).then_inc(r_read, 1)
                            dve.tensor_tensor(A[:, :, F:2 * F], R[:, :, 2 * F:3 * F], per_node("has"), ALU.mult
                                              ).then_inc(r_read, 1)
                            dve.tensor_tensor(A[:, :, 2 * F:3 * F], R[:, :, 3 * F:4 * F], per_node("neghas"),
                                              ALU.mult).then_inc(r_read, 1)
                            dve.wait_ge(r_read, c * 5 + 4)
                            dve.tensor_tensor(ms[:, :, :], A[:, :, 0:F], A[:, :, 0:F], ALU.mult
                                              ).then_inc(r_read, 1)
                            dve.wait_ge(r_read, c * 5 + 5)
                            dve.tensor_tensor(A[:, :, 3 * F:4 * F], A[:, :, 3 * F:4 * F], ms[:, :, :],
                                              ALU.subtract).then_inc(var_done, 1)
                            dve.wait_ge(var_done, c * 2 + 1)
                            dve.tensor_scalar(A[:, :, 3 * F:4 * F], A[:, :, 3 * F:4 * F], 0.0, None, ALU.max
                                              ).then_inc(var_done, 1)
                            dve.wait_ge(std_done, c + 1)
                            dve.tensor_tensor(A[:, :, 3 * F:4 * F], A[:, :, 3 * F:4 * F], per_node("has"),
                                              ALU.mult).then_inc(agg_done, 1)
                            for k in range(CH):
                                b = bank[2 + k % 2]
                                a = bass.ds(c * CH + k, 1)
                                m = c * CH + k
                                dve.wait_ge(y_done, m + 1)
                                for q, (s0, op, other) in enumerate((
                                        (col["amp"], ALU.mult, bias[:, :]),
                                        (col["att"], ALU.mult, acc[:, :]),
                                        (None, None, None))):
                                    if q:
                                        dve.wait_ge(y_read, m * 3 + q + 6)
                                    if q < 2:
                                        dve.scalar_tensor_tensor(acc[:, :], b[:, F + q * F:2 * F + q * F], s0[:, a],
                                                                 other, op, ALU.add).then_inc(y_read, 1)
                                    else:
                                        dve.tensor_tensor(Y[:, a, :], acc[:, :].unsqueeze(1),
                                                          b[:, 0:F].unsqueeze(1), ALU.add).then_inc(y_read, 1)
                                dve.wait_ge(y_read, m * 3 + 9)

                        n = [0]

                        def step(ins):
                            ins.then_inc(bn, 1)
                            n[0] += 1
                            dve.wait_ge(bn, n[0])

                        def all_nodes(t):
                            return t[:, :].unsqueeze(1).broadcast_to([P, NT, F])

                        step(dve.tensor_scalar(Y[:, NT - 1, :], Y[:, NT - 1, :], real[:, :], None, ALU.mult))
                        step(dve.tensor_reduce(acc[:, :], Y[:, :, :].rearrange("p a f -> p f a"), AX.X, ALU.add))
                        dve.wait_ge(bn_pe, 1)
                        step(dve.tensor_scalar(mu[:, :], bank[4][:, 0:F], 1.0 / NODES, None, ALU.mult))
                        step(dve.tensor_tensor(Y[:, :, :], Y[:, :, :], all_nodes(mu), ALU.subtract))
                        step(dve.tensor_scalar(Y[:, NT - 1, :], Y[:, NT - 1, :], real[:, :], None, ALU.mult))
                        dve.wait_ge(bn_act, 1)
                        step(dve.tensor_reduce(acc[:, :], SQ.rearrange("p a f -> p f a"), AX.X, ALU.add))
                        dve.wait_ge(bn_act, 2)
                        step(dve.reciprocal(fac2[:, :], fac[:, :]))
                        step(dve.tensor_tensor(fac2[:, :], fac2[:, :], gamma[:, :], ALU.mult))
                        step(dve.tensor_tensor(Y[:, :, :], Y[:, :, :], all_nodes(fac2), ALU.mult))
                        step(dve.tensor_tensor(Y[:, :, :], Y[:, :, :], all_nodes(beta), ALU.add))
                        step(dve.scalar_tensor_tensor(Y[:, :, :], Y[:, :, :], 0.0, H[:, :, :], ALU.max, ALU.add))
                        step(dve.tensor_tensor(X[:, :, :], X[:, :, :], Y[:, :, :], ALU.add))

                    @block.tensor
                    def _(pe):
                        pe.wait_ge(wl[0], 16)
                        with pe.Fori(0, NCH) as c:
                            pe.wait_ge(agg_done, c + 1)
                            for k in range(CH):
                                m = c * CH + k
                                pe.wait_ge(aT_done, m)
                                pe.transpose(bank[k % 2][:, 0:P], A[:, k, 0:P], ident[:, :])
                                pe.transpose(bank[k % 2][:, P:2 * P], A[:, k, P:2 * P], ident[:, :]
                                             ).then_inc(t_done, 1)
                                pe.wait_ge(aT_done, m + 1)
                                pe.wait_ge(y_read, m * 3 + 3)
                                for h in range(2):
                                    mm = pe.matmul(bank[2 + k % 2][:, 0:3 * F], aT[:, k % 2, h, :], W[:, h, :],
                                                   start=h == 0, stop=h == 1)
                                mm.then_inc(y_done, 1)
                        pe.wait_ge(bn, 2)
                        pe.matmul(bank[4][:, 0:F], ones[:, :], acc[:, :], start=True, stop=True).then_inc(bn_pe, 1)
                        pe.wait_ge(bn, 6)
                        pe.matmul(bank[5][:, 0:F], ones[:, :], acc[:, :], start=True, stop=True).then_inc(bn_pe, 1)

                    @block.scalar
                    def _(act):
                        with act.Fori(0, NCH) as c:
                            act.wait_ge(var_done, c * 2 + 2)
                            act.activation(A[:, :, 3 * F:4 * F], A[:, :, 3 * F:4 * F], ACT.Sqrt, bias=eps_c[:, :]
                                           ).then_inc(std_done, 1)
                            for k in range(CH):
                                m = c * CH + k
                                act.wait_ge(t_done, m + 1)
                                act.activation(aT[:, k % 2, :, :].rearrange("p h n -> p (h n)"),
                                               bank[k % 2][:, 0:2 * P], ACT.Copy).then_inc(aT_done, 1)
                        act.wait_ge(bn, 5)
                        act.activation(SQ, Y[:, :, :], ACT.Square).then_inc(bn_act, 1)
                        act.wait_ge(bn_pe, 2)
                        act.activation(fac[:, :], bank[5][:, 0:F], ACT.Sqrt, bias=eps_c[:, :],
                                       scale=1.0 / NODES).then_inc(bn_act, 1)

        def place_first_rows():
            ready, done = sem("fr_ready"), sem("fr_done")
            hd, hd_out = sem("fr_heads"), sems("fr_hout", 2)
            with ExitStack() as st:
                def tmp(name, shape, dt=FP32):
                    return st.enter_context(nc.sbuf_tensor(unique(name), shape, dt))
                win = tmp("win", [P, CH], I32)
                Hw = tmp("Hw", [P, CH, F])
                head = tmp("head", [P, 13, F])
                with nc.Block() as block:
                    @block.gpsimd
                    def _(pool):
                        for j in range(13):
                            pool.indirect_dma_start(head[:, j, :], None, htab[1],
                                                    bass.IndirectOffsetOnAxis(heads_i[:, j:j + 1], 0),
                                                    bounds_check=NPAD - 1, oob_is_err=True).then_inc(hd, 16)
                        with pool.Fori(0, NCH) as c:
                            pool.wait_ge(done, c * (CH * 16))
                            pool.tensor_copy(win[:, :], start_i[:, bass.ds(c * CH, CH)]).then_inc(ready, 1)
                            pool.tensor_copy(Hw[:, :, :], H[:, bass.ds(c * CH, CH), :]).then_inc(ready, 1)
                            pool.wait_ge(ready, c * 2 + 2)
                            for k in range(CH):
                                pool.sem_inc(pool_passed, 1)
                                pool.indirect_dma_start(first_rows, bass.IndirectOffsetOnAxis(win[:, k:k + 1], 0),
                                                        Hw[:, k, :], None, bounds_check=E_ROWS - 1,
                                                        oob_is_err=True).then_inc(done, 16)

                    @block.sync
                    def _(sp):
                        sp.wait_ge(hd, 13 * 16)
                        sp.wait_ge(done, NT * 16)
                        v = first_rows[0:12 * P * P, :].rearrange("(j p n) f -> p j n f", j=12, p=P)
                        sp.dma_start(v[:, :, 0, :], head[:, 0:12, :]).then_inc(hd_out[0], 16)
                        v = first_rows[12 * P * P:EPAD, :].rearrange("(p n) f -> p n f", n=P)
                        sp.dma_start(v[:, 0, :], head[0:TILES - 12 * P, 12, :]).then_inc(hd_out[1], 16)
                        sp.wait_ge(hd_out[0], 16)
                        sp.wait_ge(hd_out[1], 16)

        def sum_edges():
            loaded, rows_done, eq_done, idx_done = sems("se_loaded", 2), sem("se_rows"), sem("se_eq"), sem("se_idx")
            x_done, xs_done, tot_done, m_done = sem("se_x"), sem("se_xs"), sem("se_tot"), sem("se_m")
            added, own, dif_done = sems("se_added", BODY), sem("se_own"), sem("se_dif")
            with ExitStack() as st:
                def tmp(name, shape, dt=FP32):
                    return st.enter_context(nc.sbuf_tensor(unique(name), shape, dt))
                Er = tmp("Er", [P, 2, GRP, F])
                eq_dst = tmp("eq_dst", [P, 2, GRP, P])
                eq_src = tmp("eq_src", [P, 2, GRP, P])
                earlier = tmp("earlier", [P, GRP, P])
                n_earlier = tmp("n_earlier", [P, GRP])
                shift = tmp("shift", [P, GRP])
                to_spare = tmp("to_spare", [P, TILES])
                idx = tmp("idx", [P, 2, GRP], I32)
                Xs = tmp("Xs", [P, 2, GRP, F])
                M = tmp("M", [P, 2, GRP, F])
                in_v = first_rows[0:EPAD, :].rearrange("(t p) f -> p t f", p=P)
                with nc.Block() as block:
                    @block.sync
                    def _(sp):
                        with sp.Fori(0, ITERS) as i:
                            for g in range(2):
                                n = i * 2 + g
                                sp.wait_ge(x_done, n + 1)
                                sp.dma_start(Er[:, g, :, :], in_v[:, bass.ds(n * GRP, GRP), :]
                                             ).then_inc(loaded[g], 16)

                    @block.tensor
                    def _(pe):
                        pe.sem_inc(x_done, 2)
                        pe.sem_inc(tot_done, 2)

                        def rows(n, g):
                            pe.wait_ge(eq_done, n * 2 + 2)
                            for b, parts in ((0, (dst_hi, dst_lo)), (2, (src_hi, src_lo))):
                                for k in range(GRP):
                                    for q in range(2):
                                        mm = pe.matmul(bank[b + g][:, k * P:k * P + P],
                                                       parts[q][:, bass.ds(n * GRP + k, 1)].broadcast_to([P, P]),
                                                       ident_b[:, :], start=q == 0, stop=q == 1)
                            mm.then_inc(rows_done, 1)

                        def expand(n, i, g):
                            pe.wait_ge(loaded[g], i * 16 + 16)
                            pe.wait_ge(eq_done, n * 2 + 6)
                            pe.wait_ge(xs_done, n + 1)
                            for k in range(GRP):
                                mm = pe.matmul(bank[4 + g][:, k * F:k * F + F], eq_dst[:, g, k, :],
                                               Er[:, g, k, :], start=True, stop=True)
                            mm.then_inc(x_done, 1)

                        def total(n, g):
                            pe.wait_ge(xs_done, n + 3)
                            pe.wait_ge(m_done, n + 1)
                            for k in range(GRP):
                                mm = pe.matmul(bank[6 + g][:, k * F:k * F + F], eq_src[:, g, k, :],
                                               Xs[:, g, k, :], start=True, stop=True)
                            mm.then_inc(tot_done, 1)

                        rows(0, 0)
                        rows(1, 1)
                        expand(0, 0, 0)
                        with pe.Fori(0, ITERS - 1) as i:
                            rows(i * 2 + 2, 0)
                            expand(i * 2 + 1, i, 1)
                            total(i * 2, 0)
                            rows(i * 2 + 3, 1)
                            expand(i * 2 + 2, i + 1, 0)
                            total(i * 2 + 1, 1)
                        expand(2 * ITERS - 1, ITERS - 1, 1)
                        total(2 * ITERS - 2, 0)
                        total(2 * ITERS - 1, 1)

                    @block.vector
                    def _(dve):
                        dve.sem_inc(eq_done, 4)
                        dve.tensor_scalar(to_spare[:, :], src_f[:, :], -1.0, spare_row[:, :], ALU.mult, ALU.add
                                          ).then_inc(dif_done, 1)
                        dve.wait_ge(dif_done, 1)
                        with dve.Fori(0, ITERS) as i:
                            for g in range(2):
                                n = i * 2 + g
                                t = bass.ds(n * GRP, GRP)
                                dve.wait_ge(rows_done, n + 1)
                                dve.wait_ge(tot_done, n + 1)
                                for q, (eq, ids) in enumerate(((eq_dst, dst_f), (eq_src, src_f))):
                                    dve.tensor_tensor(eq[:, g, :, :],
                                                      bank[2 * q + g][:, :].rearrange("p (k e) -> p k e", k=GRP),
                                                      ids[:, t].unsqueeze(2).broadcast_to([P, GRP, P]),
                                                      ALU.is_equal).then_inc(eq_done, 1)
                                dve.wait_ge(eq_done, n * 2 + 6)
                                dve.wait_ge(own, n * 3)
                                dve.tensor_tensor(earlier[:, :, :], eq_src[:, g, :, :],
                                                  before[:, :].unsqueeze(1).broadcast_to([P, GRP, P]),
                                                  ALU.mult).then_inc(own, 1)
                                dve.wait_ge(own, n * 3 + 1)
                                dve.tensor_reduce(n_earlier[:, :], earlier[:, :, :], AX.X, ALU.add).then_inc(own, 1)
                                dve.wait_ge(own, n * 3 + 2)
                                dve.scalar_tensor_tensor(shift[:, :], n_earlier[:, :], 0.0, to_spare[:, t],
                                                         ALU.is_gt, ALU.mult).then_inc(own, 1)
                                dve.wait_ge(own, n * 3 + 3)
                                for k in range(GRP):
                                    dve.wait_ge(added[g * GRP + k], i * 16)
                                dve.tensor_tensor(idx[:, g, :], shift[:, :], src_f[:, t], ALU.add
                                                  ).then_inc(idx_done, 1)

                    @block.scalar
                    def _(act):
                        act.sem_inc(xs_done, 2)
                        act.sem_inc(m_done, 2)

                        def expanded(n, g):
                            act.wait_ge(x_done, n + 3)
                            act.wait_ge(tot_done, n + 1)
                            act.activation(Xs[:, g, :, :].rearrange("p k f -> p (k f)"), bank[4 + g][:, 0:GRP * F],
                                           ACT.Copy).then_inc(xs_done, 1)

                        def message(n, i, g):
                            act.wait_ge(tot_done, n + 3)
                            for k in range(GRP):
                                act.wait_ge(added[g * GRP + k], i * 16)
                            act.activation(M[:, g, :, :].rearrange("p k f -> p (k f)"), bank[6 + g][:, 0:GRP * F],
                                           ACT.Copy).then_inc(m_done, 1)

                        expanded(0, 0)
                        with act.Fori(0, ITERS - 1) as i:
                            expanded(i * 2 + 1, 1)
                            message(i * 2, i, 0)
                            expanded(i * 2 + 2, 0)
                            message(i * 2 + 1, i, 1)
                        expanded(2 * ITERS - 1, 1)
                        message(2 * ITERS - 2, ITERS - 1, 0)
                        message(2 * ITERS - 1, ITERS - 1, 1)

                    @block.gpsimd
                    def _(pool):
                        with pool.Fori(0, ITERS) as i:
                            for g in range(2):
                                pool.wait_ge(m_done, i * 2 + g + 3)
                                pool.wait_ge(idx_done, i * 2 + g + 1)
                                for k in range(GRP):
                                    if g == 0:
                                        pool.wait_ge(added[GRP + k], i * 16)
                                    else:
                                        pool.wait_ge(added[k], i * 16 + 16)
                                    pool.sem_inc(pool_passed, 1)
                                    pool.indirect_dma_start(rep[k], bass.IndirectOffsetOnAxis(idx[:, g, k:k + 1], 0),
                                                            M[:, g, k, :], None, bounds_check=REP_ROWS - 1,
                                                            oob_is_err=True, compute_op=ALU.add
                                                            ).then_inc(added[g * GRP + k], 16)
                        for s in added:
                            pool.wait_ge(s, ITERS * 16)

        def add_tables():
            ld, v = sems("at_ld", REPS), sem("at_v")
            with nc.Block() as block:
                @block.sync
                def _(sp):
                    for r in range(REPS):
                        if r >= 2:
                            sp.wait_ge(v, r - 1)
                        sp.dma_start((SQ, Y[:, :, :])[r % 2],
                                     rep[r][0:NPAD, :].rearrange("(a p) f -> p a f", p=P)).then_inc(ld[r], 16)

                @block.vector
                def _(dve):
                    for r in range(REPS):
                        dve.wait_ge(ld[r], 16)
                        dve.wait_ge(v, r)
                        dve.tensor_tensor(X[:, :, :], X[:, :, :], (SQ, Y[:, :, :])[r % 2], ALU.add).then_inc(v, 1)

        def gine_edges():
            wl, win_ready, gathered, attr_in = sem("ge_wl"), sem("ge_win"), sems("ge_gathered", BODY), sems("ge_attr", 2)
            t_done, d_done, gates_done, s_done = sem("ge_t"), sem("ge_d"), sem("ge_gates"), sem("ge_s")
            back_done, w_done, sent, wl2 = sem("ge_back"), sem("ge_w"), sems("ge_sent", 2), sem("ge_wl2")
            with ExitStack() as st:
                def tmp(name, shape, dt=FP32):
                    return st.enter_context(nc.sbuf_tensor(unique(name), shape, dt))
                win = tmp("win", [P, 2, GRP], I32)
                G = tmp("G", [P, BODY, F])
                attr = tmp("attr", [EDGE_F, 2, GRP * P])
                We = tmp("We", [EDGE_F, F])
                be = tmp("be", [F, 1])
                D = tmp("D", [F, 2, GRP * P])
                S = tmp("S", [F, 2, GRP * P])
                Wo = tmp("Wo", [P, 2, GRP, F])
                out_v = r3.rearrange("(t p) f -> p t f", p=P)
                with nc.Block() as block:
                    @block.gpsimd
                    def _(pool):
                        with pool.Fori(0, ITERS) as i:
                            for g in range(2):
                                pool.wait_ge(win_ready, i * 2 + g + 1)
                                pool.wait_ge(t_done, i * 2 + g + 1)
                                for k in range(GRP):
                                    s = g * GRP + k
                                    pool.sem_inc(pool_passed, 1)
                                    pool.indirect_dma_start(
                                        G[:, s, :], None, htab[2],
                                        bass.IndirectOffsetOnAxis(win[:, g, k:k + 1], 0),
                                        bounds_check=NPAD - 1, oob_is_err=True).then_inc(gathered[s], 16)

                    @block.tensor
                    def _(pe):
                        pe.sem_inc(t_done, 2)
                        pe.sem_inc(back_done, 2)
                        pe.wait_ge(wl, 16)

                        def front(n, i, g):
                            pe.wait_ge(d_done, n + 1)
                            pe.wait_ge(attr_in[g], i * 16 + 16)
                            pe.matmul(bank[g][0:F, :], We[:, :], attr[:, g, :], start=True, stop=False)
                            for k in range(GRP):
                                s = g * GRP + k
                                pe.wait_ge(gathered[s], i * 16 + 16)
                                mm = pe.matmul(bank[g][0:F, k * P:k * P + P], G[:, s, :], ident[:, :],
                                               start=False, stop=k == GRP - 1)
                            mm.then_inc(t_done, 1)
                            pe.wait_ge(s_done, n + 1)
                            for k in range(GRP):
                                mm = pe.matmul(bank[2 + g][0:F, k * P:k * P + P],
                                               gate_sum[:, bass.ds(n * GRP + k, 1)].broadcast_to([P, F]),
                                               ident_b[:, :], start=True, stop=True)
                            mm.then_inc(gates_done, 1)

                        def back(n, g):
                            pe.wait_ge(s_done, n + 3)
                            pe.wait_ge(w_done, n + 1)
                            pe.sem_inc(pe_passed, 1)
                            for k in range(GRP):
                                tr = pe.transpose(bank[4 + g][:, k * F:k * F + F], S[:, g, k * P:k * P + P],
                                                  ident[0:F, 0:F])
                            tr.then_inc(back_done, 1)

                        front(0, 0, 0)
                        with pe.Fori(0, ITERS - 1) as i:
                            front(i * 2 + 1, i, 1)
                            back(i * 2, 0)
                            front(i * 2 + 2, i + 1, 0)
                            back(i * 2 + 1, 1)
                        front(2 * ITERS - 1, ITERS - 1, 1)
                        back(2 * ITERS - 2, 0)
                        back(2 * ITERS - 1, 1)

                    @block.scalar
                    def _(act):
                        act.sem_inc(d_done, 2)
                        act.sem_inc(w_done, 2)
                        act.wait_ge(wl2, 16)

                        def message(n, g):
                            act.wait_ge(t_done, n + 3)
                            act.wait_ge(s_done, n + 1)
                            act.activation(D[:, g, :], bank[g][0:F, :], ACT.Relu, bias=be[:, :]).then_inc(d_done, 1)

                        def evacuate(n, i, g):
                            act.wait_ge(back_done, n + 3)
                            act.wait_ge(sent[g], i * 16)
                            act.activation(Wo[:, g, :, :].rearrange("p k f -> p (k f)"), bank[4 + g][:, 0:GRP * F],
                                           ACT.Copy).then_inc(w_done, 1)

                        message(0, 0)
                        with act.Fori(0, ITERS - 1) as i:
                            message(i * 2 + 1, 1)
                            evacuate(i * 2, i, 0)
                            message(i * 2 + 2, 0)
                            evacuate(i * 2 + 1, i, 1)
                        message(2 * ITERS - 1, 1)
                        evacuate(2 * ITERS - 2, ITERS - 1, 0)
                        evacuate(2 * ITERS - 1, ITERS - 1, 1)

                    @block.vector
                    def _(dve):
                        dve.memset(S[:, 1, GRP * P - 1:GRP * P], 0.0).then_inc(s_done, 2)

                        def window(n, g):
                            dve.tensor_copy(win[:, g, :], src_i[:, bass.ds(n * GRP, GRP)]).then_inc(win_ready, 1)
                        window(0, 0)
                        window(1, 1)
                        with dve.Fori(0, ITERS) as i:
                            for g in range(2):
                                n = i * 2 + g
                                dve.wait_ge(gates_done, n + 1)
                                dve.wait_ge(d_done, n + 3)
                                dve.wait_ge(back_done, n + 1)
                                dve.wait_ge(s_done, n + 2)
                                dve.tensor_tensor_scan(S[:, g, :], bank[2 + g][0:F, :], D[:, g, :],
                                                       S[:, 1 - g, GRP * P - 1:GRP * P], ALU.mult, ALU.add
                                                       ).then_inc(s_done, 1)
                                for k in range(GRP):
                                    dve.wait_ge(gathered[g * GRP + k], i * 16 + 16)
                                window(n + 2, g)

                    @block.sync
                    def _(sp):
                        sp.dma_start(We[:, :], weT).then_inc(wl, 16)
                        sp.dma_start(be[:, :], bec).then_inc(wl2, 16)

                        def load(n, g):
                            sp.wait_ge(t_done, n + 1)
                            sp.dma_start(attr[:, g, :], attrT[:, bass.ds(n * GRP * P, GRP * P)]
                                         ).then_inc(attr_in[g], 16)

                        def store(n, g):
                            sp.wait_ge(w_done, n + 3)
                            sp.dma_start(out_v[:, bass.ds(n * GRP, GRP), :], Wo[:, g, :, :]).then_inc(sent[g], 16)

                        load(0, 0)
                        load(1, 1)
                        with sp.Fori(0, ITERS - 1) as i:
                            for g in range(2):
                                load(i * 2 + g + 2, g)
                                store(i * 2 + g, g)
                        for g in range(2):
                            store(2 * ITERS - 2 + g, g)
                        for g in range(2):
                            sp.wait_ge(sent[g], ITERS * 16)

        def gine_nodes():
            wl, win_done, fetched, u = sems("gn_wl", 4), sem("gn_win"), sem("gn_fetched"), sem("gn_u")
            t_done, aT_done, h_done, hid_done, o_done, x_done = (
                sem("gn_t"), sem("gn_aT"), sem("gn_h"), sem("gn_hid"), sem("gn_o"), sem("gn_x"))
            b2_done = sem("gn_b2")
            PAIRS = CH // 2
            with ExitStack() as st:
                def tmp(name, shape, dt=FP32):
                    return st.enter_context(nc.sbuf_tensor(unique(name), shape, dt))
                win = tmp("win", [P, CH], I32)
                R = tmp("R", [P, CH, F])
                U = tmp("U", [P, CH, F])
                aT = tmp("aT", [F, 2, 2 * P])
                hid = tmp("hid", [F, 2, 2 * P])
                W1 = tmp("W1", [F, F])
                W2 = tmp("W2", [F, F])
                b1 = tmp("b1", [F, 1])
                b2 = tmp("b2", [P, F])
                with nc.Block() as block:
                    @block.sync
                    def _(sp):
                        for n, (t, d) in enumerate(((W1, g1T), (W2, g2T), (b1, g1b), (b2, g2b))):
                            sp.dma_start(t[:, :], d).then_inc(wl[n], 16)

                    @block.gpsimd
                    def _(pool):
                        with pool.Fori(0, NCH) as c:
                            pool.wait_ge(fetched, c * (CH * 16))
                            pool.tensor_copy(win[:, :], end_i[:, bass.ds(c * CH, CH)]).then_inc(win_done, 1)
                            pool.wait_ge(win_done, c + 1)
                            pool.wait_ge(u, c * 2)
                            for k in range(CH):
                                pool.sem_inc(pool_passed, 1)
                                pool.indirect_dma_start(R[:, k, :], None, r3,
                                                        bass.IndirectOffsetOnAxis(win[:, k:k + 1], 0),
                                                        bounds_check=EPAD - 1, oob_is_err=True
                                                        ).then_inc(fetched, 16)

                    @block.vector
                    def _(dve):
                        dve.wait_ge(wl[3], 16)
                        dve.tensor_tensor(X[:, :, :], X[:, :, :], b2[:, :].unsqueeze(1).broadcast_to([P, NT, F]),
                                          ALU.add).then_inc(b2_done, 1)
                        dve.wait_ge(b2_done, 1)
                        with dve.Fori(0, NCH) as c:
                            nodes = bass.ds(c * CH, CH)
                            dve.wait_ge(fetched, c * (CH * 16) + CH * 16)
                            dve.wait_ge(t_done, c * PAIRS)
                            dve.tensor_tensor(U[:, :, :], R[:, :, :],
                                              col["has"][:, nodes].unsqueeze(2).broadcast_to([P, CH, F]), ALU.mult
                                              ).then_inc(u, 1)
                            dve.wait_ge(u, c * 2 + 1)
                            dve.tensor_tensor(U[:, :, :], U[:, :, :], H[:, nodes, :], ALU.add).then_inc(u, 1)
                            for k in range(PAIRS):
                                m = c * PAIRS + k
                                a = bass.ds(c * CH + 2 * k, 2)
                                dve.wait_ge(o_done, m + 1)
                                dve.tensor_tensor(X[:, a, :], X[:, a, :],
                                                  bank[6][:, 0:2 * F].rearrange("p (k f) -> p k f", k=2), ALU.add
                                                  ).then_inc(x_done, 1)

                    @block.tensor
                    def _(pe):
                        pe.wait_ge(wl[0], 16)
                        pe.wait_ge(wl[1], 16)
                        with pe.Fori(0, NCH) as c:
                            pe.wait_ge(u, c * 2 + 2)
                            for k in range(PAIRS):
                                m = c * PAIRS + k
                                j = k % 2
                                pe.sem_inc(pe_passed, 1)
                                for q in range(2):
                                    tr = pe.transpose(bank[j][0:F, q * P:q * P + P], U[:, 2 * k + q, :], ident[:, :])
                                tr.then_inc(t_done, 1)
                                pe.wait_ge(aT_done, m + 1)
                                pe.sem_inc(pe_passed, 1)
                                pe.matmul(bank[2 + j][0:F, 0:2 * P], W1[:, :], aT[:, j, :], start=True, stop=True
                                          ).then_inc(h_done, 1)
                                pe.wait_ge(hid_done, m + 1)
                                pe.wait_ge(x_done, m)
                                for q in range(2):
                                    mm = pe.matmul(bank[6][:, q * F:q * F + F], hid[:, j, q * P:q * P + P], W2[:, :],
                                                   start=True, stop=True)
                                mm.then_inc(o_done, 1)

                    @block.scalar
                    def _(act):
                        act.wait_ge(wl[2], 16)
                        with act.Fori(0, NCH) as c:
                            for k in range(PAIRS):
                                m = c * PAIRS + k
                                j = k % 2
                                act.wait_ge(t_done, m + 1)
                                act.activation(aT[:, j, :], bank[j][0:F, 0:2 * P], ACT.Copy).then_inc(aT_done, 1)
                                act.wait_ge(h_done, m + 1)
                                act.activation(hid[:, j, :], bank[2 + j][0:F, 0:2 * P], ACT.Relu, bias=b1[:, :]
                                               ).then_inc(hid_done, 1)

        norm(0, None)
        relational()
        norm(1, htab[0], negative=True)
        pna_edges()
        pna_nodes()
        norm(2, htab[1])
        place_first_rows()
        sum_edges()
        add_tables()
        norm(3, htab[2])
        gine_edges()
        gine_nodes()

        stored = sem("stored")
        with nc.Block() as block:
            @block.sync
            def _(sp):
                sp.dma_start(out, X[:, :, :]).then_inc(stored, 16)
                sp.wait_ge(stored, 16)


def kernel(x, src, dst, edge_attr_32, edge_type_9, L0_gnn_weights, L0_gnn_biases, L1_gnn_W, L1_gnn_b,
           L1_gnn_gamma, L1_gnn_beta, L3_gnn_We, L3_gnn_be, L3_gnn_W1, L3_gnn_b1, L3_gnn_W2, L3_gnn_b2):
    import numpy as np
    import concourse.bacc as bacc
    from concourse.bass_utils import run_bass_kernel_spmd

    def edges(a, fill, more=()):
        a = np.concatenate([np.asarray(a, np.int32), np.full(EPAD - EDGES, fill, np.int32)])
        return a.reshape(TILES, P).T

    dst = np.asarray(dst)
    dst_flat = np.concatenate([dst, np.full(EPAD - EDGES, LAST, dst.dtype)])
    head = np.concatenate([dst_flat[::P], np.full(13 * P - TILES, LAST, dst.dtype)]).reshape(13, P).T
    before = np.concatenate([np.full(1, -1, dst.dtype), dst_flat[:-1]])
    x_pad = np.concatenate([np.asarray(x), np.zeros((NPAD - NODES, F), np.float32)])
    attr = np.concatenate([np.asarray(edge_attr_32), np.zeros((EPAD - EDGES, EDGE_F), np.float32)])
    w0 = np.asarray(L0_gnn_weights)[2].transpose(1, 0, 2).reshape(F, 2 * REL * F)
    b0 = np.asarray(L0_gnn_biases)[2].reshape(1, 2 * REL * F)
    w1 = np.asarray(L1_gnn_W).reshape(3, 2, P, F).transpose(2, 1, 0, 3).reshape(P, 2, 3 * F)

    def rows(v):
        return np.broadcast_to(np.asarray(v).reshape(1, F), (P, F))

    arrays = {
        "x3": x_pad.reshape(NT, P, F).transpose(1, 0, 2),
        "srcT": edges(src, LAST), "dstT": edges(dst, LAST), "dstprevT": before.reshape(TILES, P).T,
        "typeT": edges(edge_type_9, 0), "heads": head, "attrT": attr.T,
        "w0": np.concatenate([w0, b0]), "w1": w1, "b1r": rows(L1_gnn_b), "gam": rows(L1_gnn_gamma),
        "bet": rows(L1_gnn_beta), "weT": np.asarray(L3_gnn_We).T, "bec": np.asarray(L3_gnn_be).reshape(F, 1),
        "g1T": np.asarray(L3_gnn_W1).T, "g1b": np.asarray(L3_gnn_b1).reshape(F, 1),
        "g2T": np.asarray(L3_gnn_W2).T, "g2b": rows(L3_gnn_b2),
    }
    arrays = {n: np.ascontiguousarray(a) for n, a in arrays.items()}
    nc = bacc.Bacc("TRN2", target_bir_lowering=False, num_devices=1)
    args = [nc.dram_tensor(n, a.shape, mybir.dt.from_np(a.dtype), kind="ExternalInput").ap()
            for n, a in arrays.items()]
    out = nc.dram_tensor("out", (P, NT, F), FP32, kind="ExternalOutput").ap()
    build(nc, *args, out)
    r = run_bass_kernel_spmd(nc, [arrays], core_ids=[0])
    return r.results[0]["out"].transpose(1, 0, 2).reshape(NPAD, F)[:NODES]
```

```python
import concourse.bass as bass
from concourse import mybir
from contextlib import ExitStack

FP32 = mybir.dt.float32
BF16 = mybir.dt.bfloat16
FP16 = mybir.dt.float16
I32 = mybir.dt.int32
ALU = mybir.AluOpType
ACT = mybir.ActivationFunctionType
AX = mybir.AxisListType

P = 128
NODES, F, EDGES, EDGE_F, REL = 12500, 64, 200000, 32, 9
NT = -(-NODES // P)
NPAD = NT * P
LAST = NPAD - 1
TILES = 1568
EPAD = TILES * P
BODY = 16
GRP = 4
PAR = BODY // GRP
ITERS = TILES // BODY
KEYS = NT * REL
KH = KEYS // 2
REPS = 8
REP_ROWS = NPAD + P
E_ROWS = EPAD + NPAD
ZW = REP_ROWS * F // P
ZE = E_ROWS * F // P // 17
CH = 7
NCH = NT // CH
REL8 = REL - 1
AVG_D_LOG = 2.833
EPS = 1e-5
BIG = 1e30


def wait(eng, s, value):
    if not (isinstance(value, int) and value <= 0):
        eng.wait_ge(s, value)


def at(i, g):
    return i + g // PAR, g % PAR


def pipeline(eng, *stages):
    depth = len(stages) - 1

    def body(i, first=False, last=False):
        if first:
            for g in range(depth):
                for j in range(g + 1):
                    stages[j](*at(0, g - j))
        for g in range(PAR):
            for j, stage in enumerate(stages):
                if not (last and g + depth - j >= PAR):
                    stage(*at(i, g + depth - j))

    body(0, first=True)
    with eng.Fori(1, ITERS - 1) as i:
        body(i)
    body(ITERS - 1, last=True)


def chunks(eng, one):
    for q in range(2):
        one(0, q)
    with eng.Fori(1, NCH // 2) as j:
        for q in range(2):
            one(j, q)


def build(nc, x3, srcT, dstT, dstprevT, typeT, typeM, heads, attrT, w0, w1, b1r, gam, bet,
          weT, bec, g1T, g1b, g2T, g2b, out):
    ctx = ExitStack()
    with ctx:
        def sb(name, shape, dt=FP32):
            return ctx.enter_context(nc.sbuf_tensor(name, shape, dt))

        names = {}

        def unique(name):
            names[name] = names.get(name, 0) + 1
            return f"{name}_{names[name]}"

        def sem(name):
            return ctx.enter_context(nc.semaphore(name))

        def sems(name, n):
            return [sem(f"{name}{i}") for i in range(n)]

        bank = [ctx.enter_context(nc.psum_tensor(f"bank{i}", [P, 512], FP32)) for i in range(8)]

        htab = [nc.dram_tensor(f"htab{i}", [NPAD, w], FP32).ap() for i, w in enumerate((2 * F, F, F))]
        r1 = nc.dram_tensor("r1", [EPAD, 4 * F], FP32).ap()
        r3 = nc.dram_tensor("r3", [EPAD, F], FP32).ap()
        first_rows = nc.dram_tensor("first_rows", [E_ROWS, F], FP32).ap()
        type_sums = nc.dram_tensor("type_sums", [EPAD, REL8], FP32).ap()
        rep = [nc.dram_tensor(f"rep{i}", [REP_ROWS, F], FP32).ap() for i in range(REPS)]

        X = sb("X", [P, NT, F])
        HY = sb("HY", [P, 2 * NT * F])
        H = HY[:, 0:NT * F].rearrange("p (a f) -> p a f", f=F)
        Y = HY[:, NT * F:2 * NT * F].rearrange("p (a f) -> p a f", f=F)
        Z = sb("Z", [P, ZW])
        SQ = Z[:, 0:NT * F].rearrange("p (a f) -> p a f", f=F)
        row_i = sb("row_i", [P, TILES + BODY], I32)
        src_f = sb("src_f", [P, TILES])
        dst_f = sb("dst_f", [P, TILES])
        key_src = sb("key_src", [P, TILES])
        row_f = sb("row_f", [P, TILES])
        src_hi, src_lo, dst_hi, dst_lo, gate_sum, gate_max = (
            sb(n, [P, TILES], BF16) for n in ("src_hi", "src_lo", "dst_hi", "dst_lo", "gate_sum", "gate_max"))
        ident = sb("ident", [P, P])
        ident_b = sb("ident_b", [P, P], BF16)
        ones = sb("ones", [P, P])
        upto = sb("upto", [P, P])
        strict = sb("strict", [P, P])
        steps_to_counts = sb("steps_to_counts", [P, P])
        shift = sb("shift", [P, P])
        wrap = sb("wrap", [P, P])
        before = sb("before", [P, P])
        spare_row = sb("spare_row", [P, 1])
        real = sb("real", [P, 1])
        eps_c = sb("eps_c", [P, 1])
        C = sb("C", [P, NT, 2 * REL])
        col = {n: sb("col_" + n, [P, NT]) for n in
               ("cnt", "deg", "rcnt", "has", "neghas", "rdeg", "end", "some", "amp", "att", "t0", "t1", "mean", "rstd")}
        end_i = sb("end_i", [P, NT + 2 * CH], I32)
        start_i = sb("start_i", [P, NT + 2 * CH], I32)
        heads_i = sb("heads_i", [P, 13], I32)

        ldx, ldi, cst, prep = sem("ldx"), sem("ldi"), sem("cst"), sem("prep")
        pool_passed, pe_passed = sem("pool_passed"), sem("pe_passed")
        with ExitStack() as st:
            def tmp(name, shape, dt=FP32):
                return st.enter_context(nc.sbuf_tensor(unique(name), shape, dt))
            dst_i, dstprev_i, src_i, ia, ib, type_i, type_m = (
                HY[:, n * TILES:n * TILES + TILES].bitcast(I32) for n in range(7))
            src_step, dst_step, dst_astep = (tmp(n, [P, TILES], BF16) for n in ("src_step", "dst_step", "dst_astep"))
            type_b = tmp("type_b", [P, TILES], BF16)
            heads_id = tmp("heads_id", [P, 13], I32)
            heads_lo = tmp("heads_lo", [P, 13], I32)
            heads_hi = tmp("heads_hi", [P, 13], I32)
            with nc.Block() as block:
                @block.sync
                def _(sp):
                    sp.dma_start(src_i, srcT).then_inc(ldi, 16)
                    sp.dma_start(dst_i, dstT).then_inc(ldi, 16)
                    sp.dma_start(type_i, typeT).then_inc(ldi, 16)
                    sp.dma_start(dstprev_i, dstprevT).then_inc(ldi, 16)
                    sp.dma_start(type_m, typeM).then_inc(ldi, 16)
                    sp.dma_start(heads_id[:, :], heads).then_inc(ldi, 16)
                    sp.dma_start(X[:, :, :], x3).then_inc(ldx, 16)
                    sp.wait_ge(ldx, 16)

                @block.gpsimd
                def _(pool):
                    n = [0]

                    def step(ins):
                        ins.then_inc(cst, 1)
                        n[0] += 1
                        pool.wait_ge(cst, n[0])

                    def diagonal(t, fill, base):
                        step(pool.affine_select(out=t[:, :], in_=t[:, :], compare_op=ALU.not_equal, fill=fill,
                                                base=base, pattern=[[-1, P]], channel_multiplier=1))

                    for t in (ident, steps_to_counts, shift, wrap):
                        step(pool.memset(t[:, :], 0.0))
                    step(pool.memset(ones[:, :], 1.0))
                    step(pool.memset(real[:, :], 1.0))
                    step(pool.memset(eps_c[:, :], EPS))
                    step(pool.memset(end_i[:, :], 0))
                    step(pool.memset(start_i[:, :], 0))
                    step(pool.iota(spare_row[:, :], [[0, 1]], base=NPAD, channel_multiplier=1,
                                   allow_small_or_imprecise_dtypes=True))
                    diagonal(ident, 1.0, 0)
                    diagonal(steps_to_counts, 0.5, 0)
                    diagonal(steps_to_counts, -0.5, -1)
                    diagonal(steps_to_counts, 0.5, P - 1)
                    diagonal(shift, 1.0, 1)
                    diagonal(wrap, 1.0, -(P - 1))
                    step(pool.affine_select(out=upto[:, :], in_=ones[:, :], compare_op=ALU.is_ge, fill=0.0,
                                            base=0, pattern=[[1, P]], channel_multiplier=-1))
                    step(pool.affine_select(out=strict[:, :], in_=ones[:, :], compare_op=ALU.is_gt, fill=0.0,
                                            base=0, pattern=[[1, P]], channel_multiplier=-1))
                    step(pool.affine_select(out=before[:, :], in_=ones[:, :], compare_op=ALU.is_gt, fill=0.0,
                                            base=0, pattern=[[-1, P]], channel_multiplier=1))
                    step(pool.affine_select(out=real[:, :], in_=real[:, :], compare_op=ALU.is_gt, fill=0.0,
                                            base=NODES - (NT - 1) * P, pattern=[[0, 1]], channel_multiplier=-1))

                @block.vector
                def _(dve):
                    n = [0]

                    def step(ins):
                        ins.then_inc(prep, 1)
                        n[0] += 1

                    def seen():
                        dve.wait_ge(prep, n[0])

                    def split(e_id, lo_i, hi_i):
                        step(dve.tensor_single_scalar(lo_i, e_id, P - 1, ALU.bitwise_and))
                        step(dve.tensor_single_scalar(hi_i, e_id, 7, ALU.arith_shift_right))
                        seen()

                    step(dve.memset(Z[:, :], 0.0))
                    step(dve.memset(row_i[:, TILES:TILES + BODY], 0))
                    dve.wait_ge(ldi, 6 * 16)
                    step(dve.tensor_copy(src_f[:, :], src_i))
                    step(dve.tensor_copy(dst_f[:, :], dst_i))
                    step(dve.tensor_tensor(gate_sum[:, :], dst_i, dstprev_i, ALU.is_equal))
                    step(dve.tensor_copy(key_src[:, :], type_i))
                    step(dve.tensor_copy(type_b[:, :], type_m))
                    seen()
                    step(dve.tensor_scalar(gate_max[:, :], gate_sum[:, :], 1.0, BIG, ALU.subtract, ALU.mult))
                    split(src_i, ia, ib)
                    step(dve.tensor_copy(src_lo[:, :], ia))
                    step(dve.tensor_scalar(src_step[:, :], ia, 0.5, None, ALU.add))
                    step(dve.tensor_scalar(src_hi[:, :], ib, float(P), None, ALU.mult))
                    step(dve.scalar_tensor_tensor(key_src[:, :], ib, float(REL), key_src[:, :], ALU.mult, ALU.add))
                    step(dve.scalar_tensor_tensor(row_f[:, :], ia, float(NT), ib, ALU.mult, ALU.add))
                    seen()
                    step(dve.tensor_copy(row_i[:, 0:TILES], row_f[:, :]))
                    split(dst_i, ia, ib)
                    step(dve.tensor_copy(dst_lo[:, :], ia))
                    step(dve.tensor_scalar(dst_step[:, :], ia, 0.5, None, ALU.add))
                    step(dve.tensor_scalar(dst_hi[:, :], ib, float(P), None, ALU.mult))
                    step(dve.tensor_scalar(dst_astep[:, :], ib, 0.5, None, ALU.add))
                    split(heads_id[:, :], heads_lo[:, :], heads_hi[:, :])
                    step(dve.scalar_tensor_tensor(heads_i[:, :], heads_lo[:, :], float(NT), heads_hi[:, :],
                                                  ALU.mult, ALU.add))
                    dve.wait_ge(cst, 11)
                    step(dve.tensor_copy(ident_b[:, :], ident[:, :]))

            zdone, ts_out = sems("zdone", 2), sem("ts_out")
            oh_ready, step_ready, oh_used = sem("oh_ready"), sem("step_ready"), sem("oh_used")
            sums_done, hz, run, off_done, off_added = (
                sem("sums_done"), sem("hz"), sem("run"), sem("off_done"), sem("off_added"))
            iota_p = tmp("iota_p", [P, P], BF16)
            iota_k = tmp("iota_k", [P, KEYS], FP16)
            onehot_k = tmp("onehot_k", [P, 4, KEYS], BF16)
            step_src = tmp("step_src", [P, 4, P], BF16)
            step_dst = tmp("step_dst", [P, 4, P], BF16)
            step_a = tmp("step_a", [P, 4, NT], BF16)
            zero_b = tmp("zero_b", [P, KH], BF16)
            one_row = tmp("one_row", [P, TILES], BF16)
            is_type = tmp("is_type", [P, 2, TILES], BF16)
            offset = tmp("offset", [P, REL8])
            type_run = HY[:, :].rearrange("p (j r) -> p j r", r=REL8)
            with nc.Block() as block:
                @block.sync
                def _(sp):
                    ev = first_rows.rearrange("(z p n) f -> z p (n f)", p=P, z=17)
                    for z in range(17):
                        sp.dma_start(ev[z], Z[:, 0:ZE]).then_inc(zdone[0], 16)
                    for t in rep:
                        sp.dma_start(t.rearrange("(p n) f -> p (n f)", p=P), Z[:, :]).then_inc(zdone[1], 16)
                    sp.wait_ge(off_added, REL8)
                    sp.dma_start(type_sums.rearrange("(p j) r -> p (j r)", p=P), HY[:, :]).then_inc(ts_out, 16)
                    sp.wait_ge(zdone[0], 17 * 16)
                    sp.wait_ge(zdone[1], REPS * 16)
                    sp.wait_ge(ts_out, 16)

                @block.gpsimd
                def _(pool):
                    pool.iota(iota_p[:, :], [[1, P]], base=0, channel_multiplier=0,
                              allow_small_or_imprecise_dtypes=True).then_inc(hz, 1)
                    pool.iota(iota_k[:, :], [[1, KEYS]], base=0, channel_multiplier=0,
                              allow_small_or_imprecise_dtypes=True).then_inc(hz, 1)
                    pool.memset(zero_b[:, :], 0.0).then_inc(hz, 1)
                    pool.wait_ge(off_done, 2)
                    for k in range(REL8):
                        pool.tensor_scalar(type_run[:, :, k], type_run[:, :, k], offset[:, k:k + 1], None, ALU.add
                                           ).then_inc(off_added, 1)

                @block.vector
                def _(dve):
                    dve.memset(one_row[:, :], 1.0).then_inc(run, 1)
                    for k in range(REL8):
                        if k >= 2:
                            dve.wait_ge(run, 2 * k - 1)
                        dve.tensor_scalar(is_type[:, k % 2, :], type_b[:, :], float(k), None, ALU.is_equal
                                          ).then_inc(run, 1)
                        dve.wait_ge(run, 2 * k + 2)
                        dve.tensor_tensor_scan(type_run[:, :, k], one_row[:, :], is_type[:, k % 2, :], 0.0,
                                               ALU.mult, ALU.add).then_inc(run, 1)
                    dve.wait_ge(off_done, 1)
                    dve.tensor_copy(offset[:, :], bank[7][:, 0:REL8]).then_inc(off_done, 1)
                    dve.wait_ge(hz, 2)
                    with dve.Fori(0, TILES // 4) as i:
                        for k in range(4):
                            dve.wait_ge(oh_used, i * 4 + k + 1)
                            dve.tensor_scalar(onehot_k[:, k, :], iota_k[:, :], key_src[:, bass.ds(i * 4 + k, 1)],
                                              None, ALU.is_equal).then_inc(oh_ready, 1)

                @block.scalar
                def _(act):
                    act.wait_ge(hz, 1)
                    with act.Fori(0, TILES // 4) as i:
                        for k in range(4):
                            t = bass.ds(i * 4 + k, 1)
                            act.wait_ge(oh_used, i * 4 + k + 1)
                            for steps, edge, width in ((step_src, src_step, P), (step_dst, dst_step, P),
                                                       (step_a, dst_astep, NT)):
                                act.activation(steps[:, k, :], iota_p[:, 0:width], ACT.Sign, bias=edge[:, t],
                                               scale=-1.0).then_inc(step_ready, 1)

                @block.tensor
                def _(pe):
                    pe.sem_inc(oh_used, 4)
                    pe.wait_ge(hz, 3)
                    for b, width in ((0, KH), (1, KH), (2, NT)):
                        pe.matmul(bank[b][:, 0:width], zero_b[:, 0:P], zero_b[:, 0:width], start=True, stop=False,
                                  skip_group_check=True)
                    pe.wait_ge(run, 2 * REL8 + 1)
                    pe.matmul(bank[7][:, 0:REL8], strict[:, :], type_run[:, TILES - 1, :], start=True, stop=True
                              ).then_inc(off_done, 1)
                    with pe.Fori(0, TILES // 4) as i:
                        for k in range(4):
                            pe.wait_ge(step_ready, i * 12 + 3 * k + 3)
                            pe.wait_ge(oh_ready, i * 4 + k + 1)
                            for half in range(2):
                                pe.matmul(bank[half][:, 0:KH], step_src[:, k, :],
                                          onehot_k[:, k, half * KH:half * KH + KH],
                                          start=False, stop=False, skip_group_check=True)
                            pe.matmul(bank[2][:, 0:NT], step_dst[:, k, :], step_a[:, k, :],
                                      start=False, stop=False, skip_group_check=True).then_inc(oh_used, 1)
                    for b, width in ((0, KH), (1, KH), (2, NT)):
                        mm = pe.matmul(bank[b][:, 0:width], zero_b[:, 0:P], zero_b[:, 0:width], start=False,
                                       stop=True, skip_group_check=True)
                    mm.then_inc(sums_done, 1)

        nn = [0]
        nd, nd_pe, nd_io, nd_act = sem("nd"), sem("nd_pe"), sem("nd_io"), sem("nd_act")
        with ExitStack() as st:
            def tmp(name, shape, dt=FP32):
                return st.enter_context(nc.sbuf_tensor(unique(name), shape, dt))
            node_id = tmp("node_id", [P, NT])
            ta = tmp("ta", [P, NT])
            tb = tmp("tb", [P, NT])
            steps = tmp("steps", [P, KEYS + NT])
            parts = ((0, 0, KH), (1, KH, KH), (2, KEYS, NT))
            with nc.Block() as block:
                @block.gpsimd
                def _(pool):
                    pool.iota(node_id[:, :], [[P, NT]], base=EPAD, channel_multiplier=1,
                              allow_small_or_imprecise_dtypes=True).then_inc(nd_io, 1)

                @block.vector
                def _(dve):
                    def step(ins):
                        ins.then_inc(nd, 1)
                        nn[0] += 1
                        dve.wait_ge(nd, nn[0])
                    dve.wait_ge(sums_done, 1)
                    for b, at_col, width in parts:
                        step(dve.tensor_copy(steps[:, at_col:at_col + width], bank[b][:, 0:width]))
                    dve.wait_ge(nd_pe, 3)
                    for half in range(2):
                        step(dve.tensor_copy(C[:, half * 49:half * 49 + 49, 0:REL],
                                             bank[4 + half][:, 0:KH].rearrange("p (a r) -> p a r", r=REL)))
                    step(dve.tensor_copy(ta[:, :], bank[6][:, 0:NT]))
                    step(dve.tensor_tensor(tb[:, 0:NT - 1], ta[:, 0:NT - 1], ta[:, 1:NT], ALU.subtract))
                    step(dve.tensor_tensor(tb[:, NT - 1:NT], ta[:, NT - 1:NT], ta[:, 0:1], ALU.add))
                    step(dve.tensor_scalar(col["deg"][:, :], tb[:, :], 0.5, None, ALU.mult))
                    assert nn[0] == 9
                    step(dve.tensor_reduce(ta[:, :], C[:, :, 0:REL], AX.X, ALU.add))
                    step(dve.tensor_tensor(col["cnt"][:, :], ta[:, :], col["deg"][:, :], ALU.add))
                    step(dve.tensor_scalar(ta[:, :], col["cnt"][:, :], 1.0, None, ALU.max))
                    step(dve.reciprocal(col["rcnt"][:, :], ta[:, :]))
                    step(dve.tensor_scalar(col["has"][:, :], col["deg"][:, :], 1.0, None, ALU.min))
                    step(dve.tensor_scalar(col["neghas"][:, :], col["has"][:, :], -1.0, None, ALU.mult))
                    step(dve.tensor_scalar(ta[:, :], col["deg"][:, :], 1.0, None, ALU.max))
                    step(dve.reciprocal(tb[:, :], ta[:, :]))
                    step(dve.tensor_tensor(col["rdeg"][:, :], tb[:, :], col["has"][:, :], ALU.mult))
                    dve.wait_ge(nd_pe, 4)
                    step(dve.tensor_copy(ta[:, :], bank[1][:, 0:NT]))
                    step(dve.tensor_tensor_scan(tb[:, :], ones[:, 0:NT], ta[:, :], 0.0, ALU.mult, ALU.add))
                    step(dve.tensor_tensor(tb[:, :], tb[:, :], ta[:, :], ALU.subtract))
                    step(dve.tensor_tensor(col["end"][:, :], bank[0][:, 0:NT], tb[:, :], ALU.add))
                    step(dve.tensor_scalar(col["some"][:, :], col["end"][:, :], 1.0, None, ALU.min))
                    step(dve.tensor_scalar(end_i[:, 0:NT], col["end"][:, :], 1.0, 0.0, ALU.subtract, ALU.max))
                    dve.wait_ge(nd_io, 1)
                    step(dve.tensor_tensor(ta[:, :], col["end"][:, :], col["deg"][:, :], ALU.subtract))
                    step(dve.tensor_tensor(ta[:, :], ta[:, :], node_id[:, :], ALU.subtract))
                    step(dve.tensor_tensor(ta[:, :], ta[:, :], col["has"][:, :], ALU.mult))
                    step(dve.tensor_tensor(start_i[:, 0:NT], ta[:, :], node_id[:, :], ALU.add))
                    dve.wait_ge(nd_act, 1)
                    step(dve.tensor_scalar(ta[:, :], col["t0"][:, :], 1e-12, None, ALU.max))
                    step(dve.reciprocal(tb[:, :], ta[:, :]))
                    step(dve.scalar_tensor_tensor(col["att"][:, :], tb[:, :], AVG_D_LOG, col["has"][:, :],
                                                  ALU.mult, ALU.mult))
                    step(dve.tensor_scalar(col["amp"][:, :], col["t0"][:, :], 1.0 / AVG_D_LOG, None, ALU.mult))

                @block.tensor
                def _(pe):
                    for n, (b, at_col, width) in enumerate(parts):
                        pe.wait_ge(nd, n + 1)
                        pe.matmul(bank[4 + b][:, 0:width], steps_to_counts[:, :], steps[:, at_col:at_col + width],
                                  start=True, stop=True).then_inc(nd_pe, 1)
                    pe.wait_ge(nd, 9)
                    pe.matmul(bank[0][:, 0:NT], upto[:, :], col["deg"][:, :], start=True, stop=True)
                    pe.matmul(bank[1][:, 0:NT], ones[:, :], col["deg"][:, :], start=True, stop=True
                              ).then_inc(nd_pe, 1)

                @block.scalar
                def _(act):
                    act.wait_ge(nd, 9)
                    act.activation(col["t0"][:, :], col["deg"][:, :], ACT.Ln, bias=1.0).then_inc(nd_act, 1)

        def fetch(pool, table, limit, win, R, win_ready, fetched):
            def one(j, q):
                pool.wait_ge(win_ready, j * 2 + q + 1)
                pool.sem_inc(pool_passed, 1)
                for k in range(CH):
                    pool.indirect_dma_start(R[:, q, k, :], None, table,
                                            bass.IndirectOffsetOnAxis(win[:, q, k:k + 1], 0),
                                            bounds_check=limit, oob_is_err=True).then_inc(fetched[q], 16)
            chunks(pool, one)

        def window(eng, win, index, j, q, win_ready):
            eng.tensor_copy(win[:, q, :], index[:, bass.ds((j * 2 + q) * CH, CH)]).then_inc(win_ready, 1)

        def count_dst():
            win_ready, fetched, kept, v, sh = (
                sem("cd_win"), sems("cd_fetched", 2), sem("cd_kept"), sem("cd_v"), sem("cd_shift"))
            half = NT // 2
            with ExitStack() as st:
                def tmp(name, shape, dt=FP32):
                    return st.enter_context(nc.sbuf_tensor(unique(name), shape, dt))
                win = tmp("win", [P, 2, CH], I32)
                R = tmp("R", [P, 2, CH, REL8])
                upto_n = tmp("upto_n", [P, NT, REL8])
                with nc.Block() as block:
                    @block.gpsimd
                    def _(pool):
                        fetch(pool, type_sums, EPAD - 1, win, R, win_ready, fetched)

                    @block.vector
                    def _(dve):
                        def keep(j, q):
                            dve.wait_ge(fetched[q], j * (CH * 16) + CH * 16)
                            dve.tensor_copy(upto_n[:, bass.ds((j * 2 + q) * CH, CH), :], R[:, q, :, :]
                                            ).then_inc(kept, 1)
                            window(dve, win, end_i, j + 1, q, win_ready)

                        for q in range(2):
                            window(dve, win, end_i, 0, q, win_ready)
                        chunks(dve, keep)
                        dve.wait_ge(kept, NCH)
                        dve.tensor_tensor(upto_n[:, :, :], upto_n[:, :, :],
                                          col["some"][:, :].unsqueeze(2).broadcast_to([P, NT, REL8]), ALU.mult
                                          ).then_inc(v, 1)
                        dve.wait_ge(sh, 1)
                        for h in range(2):
                            a = slice(h * half, h * half + half)
                            dve.tensor_tensor(C[:, a, REL:2 * REL - 1], upto_n[:, a, :],
                                              bank[h][:, 0:half * REL8].rearrange("p (a r) -> p a r", r=REL8),
                                              ALU.subtract).then_inc(v, 1)
                        dve.wait_ge(v, 3)
                        dve.tensor_reduce(col["t0"][:, :], C[:, :, REL:2 * REL - 1], AX.X, ALU.add).then_inc(v, 1)
                        dve.wait_ge(v, 4)
                        dve.tensor_tensor(C[:, :, 2 * REL - 1:2 * REL].rearrange("p a r -> p (a r)"),
                                          col["deg"][:, :], col["t0"][:, :], ALU.subtract).then_inc(v, 1)

                    @block.tensor
                    def _(pe):
                        pe.wait_ge(v, 1)
                        for h in range(2):
                            first = 1 if h == 0 else 0
                            pe.matmul(bank[h][:, 0:half * REL8], shift[:, :],
                                      upto_n[:, h * half:h * half + half, :].rearrange("p a r -> p (a r)"),
                                      start=True, stop=False)
                            mm = pe.matmul(bank[h][:, first * REL8:half * REL8], wrap[:, :],
                                           upto_n[:, h * half + first - 1:h * half + half - 1, :]
                                           .rearrange("p a r -> p (a r)"), start=False, stop=True)
                        mm.then_inc(sh, 1)

        ln_v, ln_a, ln_neg, ln_out, ln_neg_out = sem("ln_v"), sem("ln_a"), sem("ln_neg"), sem("ln_out"), sem("ln_no")
        ln_steps = 12
        tables_out = [0]

        def norm(i, table, negative=False):
            v, a, v0, a0 = ln_v, ln_a, i * ln_steps, i * 4
            n = [v0]
            parts = (slice(0, NT // 2), slice(NT // 2, NT))

            def wide(c, h):
                return col[c][:, h].unsqueeze(2).broadcast_to([P, NT // 2, F])

            with nc.Block() as block:
                @block.vector
                def _(dve):
                    def step(ins):
                        ins.then_inc(v, 1)
                        n[0] += 1
                        dve.wait_ge(v, n[0])
                    for h in parts:
                        step(dve.tensor_reduce(col["t0"][:, h], X[:, h, :], AX.X, ALU.add))
                        step(dve.tensor_scalar(col["mean"][:, h], col["t0"][:, h], 1.0 / F, None, ALU.mult))
                        step(dve.tensor_tensor(H[:, h, :], X[:, h, :], wide("mean", h), ALU.subtract))
                    for k, h in enumerate(parts):
                        dve.wait_ge(a, a0 + k + 1)
                        step(dve.tensor_reduce(col["t0"][:, h], SQ[:, h, :], AX.X, ALU.add))
                    for k, h in enumerate(parts):
                        dve.wait_ge(a, a0 + k + 3)
                        step(dve.reciprocal(col["rstd"][:, h], col["t1"][:, h]))
                        step(dve.scalar_tensor_tensor(H[:, h, :], H[:, h, :], 0.0, wide("rstd", h), ALU.max,
                                                      ALU.mult))

                @block.scalar
                def _(act):
                    for k, h in enumerate(parts):
                        act.wait_ge(v, v0 + 3 * k + 3)
                        act.activation(SQ[:, h, :], H[:, h, :], ACT.Square).then_inc(a, 1)
                    for k, h in enumerate(parts):
                        act.wait_ge(v, v0 + 7 + k)
                        act.activation(col["t1"][:, h], col["t0"][:, h], ACT.Sqrt, bias=eps_c[:, :],
                                       scale=1.0 / F).then_inc(a, 1)

                @block.gpsimd
                def _(pool):
                    if negative:
                        for k, h in enumerate(parts):
                            pool.wait_ge(v, v0 + 10 + 2 * k)
                            pool.tensor_scalar(Y[:, h, :], H[:, h, :], -1.0, None, ALU.mult).then_inc(ln_neg, 1)

                @block.sync
                def _(sp):
                    if table is not None:
                        tv = table.rearrange("(p a) f -> p a f", p=P)
                        for k, h in enumerate(parts):
                            sp.wait_ge(v, v0 + 10 + 2 * k)
                            sp.dma_start(tv[:, h, 0:F], H[:, h, :]).then_inc(ln_out, 16)
                        tables_out[0] += 1
                        if negative:
                            for k, h in enumerate(parts):
                                sp.wait_ge(ln_neg, k + 1)
                                sp.dma_start(tv[:, h, F:2 * F], Y[:, h, :]).then_inc(ln_neg_out, 16)
                            sp.wait_ge(ln_neg_out, 2 * 16)
                        sp.wait_ge(ln_out, tables_out[0] * 2 * 16)

        def relational():
            BY_ACT = 2 * REL - 6
            hs_ready = sem("hs_ready")
            hT_psum, hT_ready = sem("hT_psum"), sem("hT_ready")
            m_ready, p_dve, p_act, v, wl, on = (
                sem("m_ready"), sem("p_dve"), sem("p_act"), sem("rel_v"), sem("rel_w"), sem("rel_on"))
            with ExitStack() as st:
                def tmp(name, shape, dt=FP32):
                    return st.enter_context(nc.sbuf_tensor(unique(name), shape, dt))
                W = tmp("W", [F + 1, 2 * REL * F])
                hs = tmp("hs", [P, 2, F])
                hT = tmp("hT", [F + 1, 2, P])
                prod = tmp("prod", [P, 2, 2 * REL, F])
                res = tmp("res", [P, F])

                def tiles(eng, one):
                    for k in range(2):
                        one(k, k)
                    with eng.Fori(1, NT // 2) as i:
                        for k in range(2):
                            one(i * 2 + k, k)

                def ahead(eng, front, back):
                    front(0, 0)
                    for k in range(2):
                        front(k + 1, 1 - k)
                        back(k, k)
                    with eng.Fori(1, NT // 2 - 1) as i:
                        for k in range(2):
                            front(i * 2 + k + 1, 1 - k)
                            back(i * 2 + k, k)
                    front(NT - 1, 1)
                    back(NT - 2, 0)
                    back(NT - 1, 1)

                with nc.Block() as block:
                    @block.sync
                    def _(sp):
                        sp.dma_start(W[:, :], w0).then_inc(wl, 16)

                    @block.gpsimd
                    def _(pool):
                        pool.memset(hT[F:F + 1, :, :], 1.0).then_inc(on, 1)
                        pool.wait_ge(on, 1)

                        def copy(m, k):
                            wait(pool, hT_psum, m - 1)
                            pool.tensor_copy(hs[:, k, :].unsqueeze(1), H[:, bass.ds(m, 1), :]).then_inc(hs_ready, 1)
                        tiles(pool, copy)

                    @block.tensor
                    def _(pe):
                        pe.wait_ge(wl, 16)
                        pe.wait_ge(on, 1)

                        def transpose(m, k):
                            pe.wait_ge(hs_ready, m + 1)
                            wait(pe, hT_ready, m - 1)
                            pe.sem_inc(pe_passed, 1)
                            pe.transpose(bank[6 + k][0:F, 0:P], hs[:, k, :], ident[:, :]).then_inc(hT_psum, 1)

                        def products(m, k):
                            pe.wait_ge(hT_ready, m + 1)
                            wait(pe, p_dve, m - 1)
                            wait(pe, p_act, (m - 1) * BY_ACT)
                            for c in range(3):
                                pe.matmul(bank[3 * k + c][:, 0:384], hT[:, k, :],
                                          W[:, 384 * c:384 * c + 384], start=True, stop=True).then_inc(m_ready, 1)
                        ahead(pe, transpose, products)

                    @block.scalar
                    def _(act):
                        def evacuate(m, k):
                            act.wait_ge(hT_psum, m + 1)
                            wait(act, m_ready, m * 3 - 3)
                            act.activation(hT[0:F, k, :], bank[6 + k][0:F, 0:P], ACT.Copy).then_inc(hT_ready, 1)

                        def scale(m, k):
                            wait(act, v, m * 2 - 3)
                            for r in range(6, 2 * REL):
                                c, o = r // 6, (r % 6) * F
                                if r % 6 == 0:
                                    act.wait_ge(m_ready, m * 3 + c + 1)
                                act.activation(prod[:, k, r, :], bank[3 * k + c][:, o:o + F], ACT.Copy,
                                               scale=C[:, bass.ds(m, 1), r:r + 1].rearrange("p a r -> p (a r)")
                                               ).then_inc(p_act, 1)
                        ahead(act, evacuate, scale)

                    @block.vector
                    def _(dve):
                        def combine(m, k):
                            a = bass.ds(m, 1)
                            dve.wait_ge(m_ready, m * 3 + 1)
                            dve.tensor_tensor(prod[:, k, 0:6, :],
                                              bank[3 * k][:, 0:6 * F].rearrange("p (r f) -> p r f", f=F),
                                              C[:, a, 0:6].rearrange("p a r -> p (a r)").unsqueeze(2)
                                              .broadcast_to([P, 6, F]), ALU.mult).then_inc(p_dve, 1)
                            dve.wait_ge(p_dve, m + 1)
                            dve.wait_ge(p_act, m * BY_ACT + BY_ACT)
                            wait(dve, v, m * 2)
                            dve.tensor_reduce(res[:, :], prod[:, k, :, :].rearrange("p r f -> p f r"), AX.X,
                                              ALU.add).then_inc(v, 1)
                            dve.wait_ge(v, m * 2 + 1)
                            dve.scalar_tensor_tensor(X[:, a, :], res[:, :].unsqueeze(1), col["rcnt"][:, a],
                                                     X[:, a, :], ALU.mult, ALU.add).then_inc(v, 1)
                        tiles(dve, combine)

        def pna_edges():
            win_ready, gathered = sem("pe_win_ready"), sems("pe_gathered", PAR)
            t_done, d_done, gates_done = sem("pe_t_done"), sem("pe_d_done"), sem("pe_gates_done")
            s_done, o6_done, back_done = sem("pe_s_done"), sem("pe_o6_done"), sem("pe_back_done")
            w_act, w_dve, sent = sem("pe_w_act"), sem("pe_w_dve"), sems("pe_sent", 2)
            with ExitStack() as st:
                def tmp(name, shape, dt=FP32):
                    return st.enter_context(nc.sbuf_tensor(unique(name), shape, dt))
                win = tmp("win", [P, PAR, GRP], I32)
                G = tmp("G", [P, BODY, 2 * F])
                D = tmp("D", [P, 2, 2, GRP * P])
                S = tmp("S", [P, 2, 2, GRP * P])
                Wo = tmp("Wo", [P, 2, GRP, 4 * F])
                out_v = r1.rearrange("(t p) f -> p t f", p=P)
                with nc.Block() as block:
                    @block.gpsimd
                    def _(pool):
                        def gather(i, g):
                            n = i * PAR + g
                            pool.wait_ge(win_ready, n + 1)
                            wait(pool, t_done, n - PAR + 1)
                            pool.sem_inc(pool_passed, 1)
                            for k in range(GRP):
                                s = g * GRP + k
                                pool.indirect_dma_start(
                                    G[:, s, :], None, htab[0], bass.IndirectOffsetOnAxis(win[:, g, k:k + 1], 0),
                                    bounds_check=NPAD - 1, oob_is_err=True).then_inc(gathered[g], 16)
                        pipeline(pool, gather)

                    @block.tensor
                    def _(pe):
                        def front(i, g):
                            n, b = i * PAR + g, g % 2
                            wait(pe, d_done, n * 3 - 3)
                            pe.wait_ge(gathered[g], i * (GRP * 16) + GRP * 16)
                            for k in range(GRP):
                                s = g * GRP + k
                                tr = pe.transpose(bank[b][:, k * P:k * P + P], G[:, s, :], ident[:, :])
                            tr.then_inc(t_done, 1)
                            wait(pe, s_done, n * 2)
                            for base, gate in ((2, gate_sum), (4, gate_max)):
                                for k in range(GRP):
                                    mm = pe.matmul(bank[base + b][:, k * P:k * P + P],
                                                   gate[:, bass.ds(n * GRP + k, 1)].broadcast_to([P, P]),
                                                   ident_b[:, :], start=True, stop=True)
                            mm.then_inc(gates_done, 1)

                        def back(i, g):
                            n, b = i * PAR + g, g % 2
                            pe.wait_ge(s_done, n * 2 + 4)
                            for half, read, done in ((0, w_act, o6_done), (1, w_dve, back_done)):
                                wait(pe, read, n)
                                for k in range(2):
                                    for q in range(2):
                                        c, o = (half * 2 + k) * P, (k * 2 + q) * P
                                        tr = pe.transpose(bank[6 + half][:, o:o + P], S[:, b, q, c:c + P],
                                                          ident[:, :])
                                tr.then_inc(done, 1)
                        pipeline(pe, front, back)

                    @block.scalar
                    def _(act):
                        def operands(i, g):
                            n, b = i * PAR + g, g % 2
                            act.wait_ge(t_done, n + 1)
                            wait(act, s_done, n * 2)
                            act.activation(D[0:F, b, 0, :], bank[b][0:F, :], ACT.Copy).then_inc(d_done, 1)
                            act.activation(D[F:P, b, 0, :], bank[b][F:P, :], ACT.Square).then_inc(d_done, 1)
                            act.activation(D[:, b, 1, :], bank[b][:, :], ACT.Copy).then_inc(d_done, 1)

                        def evacuate(i, g):
                            n, b = i * PAR + g, g % 2
                            act.wait_ge(o6_done, n + 1)
                            wait(act, sent[b], (i * 2 + g // 2) * 16)
                            act.activation(Wo[:, b, 0:2, :].rearrange("p k f -> p (k f)"), bank[6][:, :], ACT.Copy
                                           ).then_inc(w_act, 1)
                        pipeline(act, operands, evacuate)

                    @block.vector
                    def _(dve):
                        dve.memset(S[:, 1, :, GRP * P - 1:GRP * P], 0.0).then_inc(s_done, 2)

                        def sources(n, g):
                            dve.tensor_copy(win[:, g, :], row_i[:, bass.ds(n * GRP, GRP)]).then_inc(win_ready, 1)

                        def scans(i, g):
                            n, b = i * PAR + g, g % 2
                            dve.wait_ge(gates_done, n + 1)
                            wait(dve, back_done, n - 1)
                            for q, base, op0, op1 in ((0, 2, ALU.mult, ALU.add), (1, 4, ALU.add, ALU.max)):
                                dve.wait_ge(d_done, n * 3 + 2 + q)
                                dve.wait_ge(s_done, n * 2 + 1 + q)
                                dve.tensor_tensor_scan(S[:, b, q, :], bank[base + b][:, :], D[:, b, q, :],
                                                       S[:, 1 - b, q, GRP * P - 1:GRP * P], op0, op1
                                                       ).then_inc(s_done, 1)
                            dve.wait_ge(gathered[g], i * (GRP * 16) + GRP * 16)
                            sources(n + PAR, g)

                        def evacuate(i, g):
                            n, b = i * PAR + g, g % 2
                            dve.wait_ge(back_done, n + 1)
                            wait(dve, sent[b], (i * 2 + g // 2) * 16)
                            dve.tensor_copy(Wo[:, b, 2:4, :].rearrange("p k f -> p (k f)"), bank[7][:, :]
                                            ).then_inc(w_dve, 1)

                        for g in range(PAR):
                            sources(g, g)
                        pipeline(dve, scans, evacuate)

                    @block.sync
                    def _(sp):
                        def store(i, g):
                            n, b = i * PAR + g, g % 2
                            sp.wait_ge(w_act, n + 1)
                            sp.wait_ge(w_dve, n + 1)
                            sp.dma_start(out_v[:, bass.ds(n * GRP, GRP), :], Wo[:, b, :, :]).then_inc(sent[b], 16)
                        pipeline(sp, store)
                        for b in range(2):
                            sp.wait_ge(sent[b], ITERS * PAR // 2 * 16)

        def pna_nodes():
            wl, win_ready, fetched = sem("pn_wl"), sem("pn_win"), sems("pn_fetched", 2)
            raw, ms_done, var_done, std_done, agg_done = (
                sem("pn_raw"), sem("pn_ms"), sem("pn_var"), sem("pn_std"), sem("pn_agg"))
            t_done, aT_done, y_done, y_read = sem("pn_t"), sem("pn_aT"), sem("pn_y"), sem("pn_yread")
            bn, bn_pe, bn_act = sem("pn_bn"), sem("pn_bn_pe"), sem("pn_bn_act")
            with ExitStack() as st:
                def tmp(name, shape, dt=FP32):
                    return st.enter_context(nc.sbuf_tensor(unique(name), shape, dt))
                win = tmp("win", [P, 2, CH], I32)
                R = tmp("R", [P, 2, CH, 4 * F])
                A = tmp("A", [P, 2, CH, 4 * F])
                ms = tmp("ms", [P, 2, CH, F])
                aT = tmp("aT", [P, 2, 2, P])
                W = tmp("W", [P, 2, 3 * F])
                bias = tmp("bias", [P, F])
                gamma = tmp("gamma", [P, F])
                beta = tmp("beta", [P, F])
                acc = tmp("acc", [P, F])
                mu = tmp("mu", [P, F])
                fac = tmp("fac", [P, F])
                fac2 = tmp("fac2", [P, F])

                def ahead(eng, front, back):
                    front(0, 0)
                    front(0, 1)
                    back(0, 0)
                    with eng.Fori(1, NCH // 2) as j:
                        front(j, 0)
                        back(j - 1, 1)
                        front(j, 1)
                        back(j, 0)
                    back(NCH // 2 - 1, 1)

                with nc.Block() as block:
                    @block.sync
                    def _(sp):
                        sp.dma_start(W[:, :, :], w1).then_inc(wl, 16)
                        sp.dma_start(bias[:, :], b1r).then_inc(wl, 16)
                        sp.dma_start(gamma[:, :], gam).then_inc(wl, 16)
                        sp.dma_start(beta[:, :], bet).then_inc(wl, 16)

                    @block.gpsimd
                    def _(pool):
                        fetch(pool, r1, EPAD - 1, win, R, win_ready, fetched)

                    @block.vector
                    def _(dve):
                        dve.wait_ge(wl, 4 * 16)

                        def aggregate(j, q):
                            c = j * 2 + q
                            A_q, R_q, std = A[:, q], R[:, q], A[:, q, :, 3 * F:4 * F]

                            def per_node(name):
                                return col[name][:, bass.ds(c * CH, CH)].unsqueeze(2).broadcast_to([P, CH, F])
                            dve.wait_ge(fetched[q], j * (CH * 16) + CH * 16)
                            wait(dve, t_done, (c - 1) * CH)
                            for at_a, at_r, name in ((0, 0, "rdeg"), (3, 1, "rdeg"), (1, 2, "has"), (2, 3, "neghas")):
                                dve.tensor_tensor(A_q[:, :, at_a * F:at_a * F + F], R_q[:, :, at_r * F:at_r * F + F],
                                                  per_node(name), ALU.mult).then_inc(raw, 1)
                            window(dve, win, end_i, j + 1, q, win_ready)
                            dve.wait_ge(raw, c * 4 + 4)
                            dve.wait_ge(ms_done, c + 1)
                            dve.tensor_tensor(std, std, ms[:, q, :, :], ALU.subtract).then_inc(var_done, 1)
                            dve.wait_ge(var_done, c * 2 + 1)
                            dve.tensor_scalar(std, std, 0.0, None, ALU.max).then_inc(var_done, 1)
                            dve.wait_ge(std_done, c + 1)
                            dve.tensor_tensor(std, std, per_node("has"), ALU.mult).then_inc(agg_done, 1)

                        def linear(j, q):
                            c = j * 2 + q
                            for k in range(CH):
                                m = c * CH + k
                                a = bass.ds(m, 1)
                                y = bank[2 + (q * CH + k) % 2]
                                dve.wait_ge(y_done, m + 1)
                                wait(dve, y_read, m * 3)
                                dve.scalar_tensor_tensor(acc[:, :], y[:, F:2 * F], col["amp"][:, a], bias[:, :],
                                                         ALU.mult, ALU.add).then_inc(y_read, 1)
                                dve.wait_ge(y_read, m * 3 + 1)
                                dve.scalar_tensor_tensor(acc[:, :], y[:, 2 * F:3 * F], col["att"][:, a], acc[:, :],
                                                         ALU.mult, ALU.add).then_inc(y_read, 1)
                                dve.wait_ge(y_read, m * 3 + 2)
                                dve.tensor_tensor(Y[:, a, :], acc[:, :].unsqueeze(1), y[:, 0:F].unsqueeze(1),
                                                  ALU.add).then_inc(y_read, 1)

                        for q in range(2):
                            window(dve, win, end_i, 0, q, win_ready)
                        ahead(dve, aggregate, linear)

                        n = [0]

                        def step(ins):
                            ins.then_inc(bn, 1)
                            n[0] += 1
                            dve.wait_ge(bn, n[0])

                        def all_nodes(t):
                            return t[:, :].unsqueeze(1).broadcast_to([P, NT, F])

                        dve.wait_ge(y_read, NT * 3)
                        step(dve.tensor_scalar(Y[:, NT - 1, :], Y[:, NT - 1, :], real[:, :], None, ALU.mult))
                        step(dve.tensor_reduce(acc[:, :], Y[:, :, :].rearrange("p a f -> p f a"), AX.X, ALU.add))
                        dve.wait_ge(bn_pe, 1)
                        step(dve.tensor_scalar(mu[:, :], bank[4][:, 0:F], 1.0 / NODES, None, ALU.mult))
                        step(dve.tensor_tensor(Y[:, :, :], Y[:, :, :], all_nodes(mu), ALU.subtract))
                        step(dve.tensor_scalar(Y[:, NT - 1, :], Y[:, NT - 1, :], real[:, :], None, ALU.mult))
                        dve.wait_ge(bn_act, 1)
                        step(dve.tensor_reduce(acc[:, :], SQ.rearrange("p a f -> p f a"), AX.X, ALU.add))
                        dve.wait_ge(bn_act, 2)
                        step(dve.reciprocal(fac2[:, :], fac[:, :]))
                        step(dve.tensor_tensor(fac2[:, :], fac2[:, :], gamma[:, :], ALU.mult))
                        step(dve.tensor_tensor(Y[:, :, :], Y[:, :, :], all_nodes(fac2), ALU.mult))
                        step(dve.tensor_tensor(Y[:, :, :], Y[:, :, :], all_nodes(beta), ALU.add))
                        step(dve.scalar_tensor_tensor(Y[:, :, :], Y[:, :, :], 0.0, H[:, :, :], ALU.max, ALU.add))
                        step(dve.tensor_tensor(X[:, :, :], X[:, :, :], Y[:, :, :], ALU.add))

                    @block.tensor
                    def _(pe):
                        pe.wait_ge(wl, 4 * 16)

                        def one(j, q):
                            c = j * 2 + q

                            def transpose(k):
                                m, b = c * CH + k, (q * CH + k) % 2
                                wait(pe, aT_done, m - 1)
                                pe.transpose(bank[b][:, 0:P], A[:, q, k, 0:P], ident[:, :])
                                pe.transpose(bank[b][:, P:2 * P], A[:, q, k, P:2 * P], ident[:, :]
                                             ).then_inc(t_done, 1)

                            def product(k):
                                m, b = c * CH + k, (q * CH + k) % 2
                                pe.wait_ge(aT_done, m + 1)
                                wait(pe, y_read, m * 3 - 3)
                                for h in range(2):
                                    mm = pe.matmul(bank[2 + b][:, 0:3 * F], aT[:, b, h, :], W[:, h, :],
                                                   start=h == 0, stop=h == 1)
                                mm.then_inc(y_done, 1)

                            pe.wait_ge(agg_done, c + 1)
                            transpose(0)
                            for k in range(CH):
                                if k + 1 < CH:
                                    transpose(k + 1)
                                product(k)
                        chunks(pe, one)
                        pe.wait_ge(bn, 2)
                        pe.matmul(bank[4][:, 0:F], ones[:, :], acc[:, :], start=True, stop=True).then_inc(bn_pe, 1)
                        pe.wait_ge(bn, 6)
                        pe.matmul(bank[5][:, 0:F], ones[:, :], acc[:, :], start=True, stop=True).then_inc(bn_pe, 1)

                    @block.scalar
                    def _(act):
                        def deviate(j, q):
                            c = j * 2 + q
                            act.wait_ge(raw, c * 4 + 1)
                            wait(act, var_done, (c - 1) * 2)
                            act.activation(ms[:, q, :, :], A[:, q, :, 0:F], ACT.Square).then_inc(ms_done, 1)
                            act.wait_ge(var_done, c * 2 + 2)
                            act.activation(A[:, q, :, 3 * F:4 * F], A[:, q, :, 3 * F:4 * F], ACT.Sqrt,
                                           bias=eps_c[:, :]).then_inc(std_done, 1)

                        def evacuate(j, q):
                            for k in range(CH):
                                m, b = (j * 2 + q) * CH + k, (q * CH + k) % 2
                                act.wait_ge(t_done, m + 1)
                                wait(act, y_done, m - 1)
                                act.activation(aT[:, b, :, :].rearrange("p h n -> p (h n)"), bank[b][:, 0:2 * P],
                                               ACT.Copy).then_inc(aT_done, 1)
                        ahead(act, deviate, evacuate)
                        act.wait_ge(bn, 5)
                        act.activation(SQ, Y[:, :, :], ACT.Square).then_inc(bn_act, 1)
                        act.wait_ge(bn_pe, 2)
                        act.activation(fac[:, :], bank[5][:, 0:F], ACT.Sqrt, bias=eps_c[:, :],
                                       scale=1.0 / NODES).then_inc(bn_act, 1)

        def place_first_rows():
            ready, placed = sem("fr_ready"), sems("fr_placed", 2)
            hd, hd_out = sem("fr_heads"), sems("fr_hout", 2)
            with ExitStack() as st:
                def tmp(name, shape, dt=FP32):
                    return st.enter_context(nc.sbuf_tensor(unique(name), shape, dt))
                win = tmp("win", [P, 2, CH], I32)
                Hw = tmp("Hw", [P, 2, CH, F])
                head = tmp("head", [P, 13, F])
                with nc.Block() as block:
                    @block.vector
                    def _(dve):
                        def one(j, q):
                            c = j * 2 + q
                            wait(dve, placed[q], j * (CH * 16))
                            window(dve, win, start_i, j, q, ready)
                            dve.tensor_copy(Hw[:, q, :, :], H[:, bass.ds(c * CH, CH), :]).then_inc(ready, 1)
                        chunks(dve, one)

                    @block.gpsimd
                    def _(pool):
                        def one(j, q):
                            pool.wait_ge(ready, (j * 2 + q) * 2 + 2)
                            pool.sem_inc(pool_passed, 1)
                            for k in range(CH):
                                pool.indirect_dma_start(first_rows, bass.IndirectOffsetOnAxis(win[:, q, k:k + 1], 0),
                                                        Hw[:, q, k, :], None, bounds_check=E_ROWS - 1,
                                                        oob_is_err=True).then_inc(placed[q], 16)
                        for j in range(13):
                            pool.indirect_dma_start(head[:, j, :], None, htab[1],
                                                    bass.IndirectOffsetOnAxis(heads_i[:, j:j + 1], 0),
                                                    bounds_check=NPAD - 1, oob_is_err=True).then_inc(hd, 16)
                        chunks(pool, one)

                    @block.sync
                    def _(sp):
                        sp.wait_ge(hd, 13 * 16)
                        for q in range(2):
                            sp.wait_ge(placed[q], NT // 2 * 16)
                        v = first_rows[0:12 * P * P, :].rearrange("(j p n) f -> p j n f", j=12, p=P)
                        sp.dma_start(v[:, :, 0, :], head[:, 0:12, :]).then_inc(hd_out[0], 16)
                        v = first_rows[12 * P * P:EPAD, :].rearrange("(p n) f -> p n f", n=P)
                        sp.dma_start(v[:, 0, :], head[0:TILES - 12 * P, 12, :]).then_inc(hd_out[1], 16)
                        sp.wait_ge(hd_out[0], 16)
                        sp.wait_ge(hd_out[1], 16)

        def sum_edges():
            loaded, rows_done, eq_done, idx_done = sems("se_loaded", 2), sem("se_rows"), sem("se_eq"), sem("se_idx")
            x_done, xs_done, tot_done, m_done = sem("se_x"), sem("se_xs"), sem("se_tot"), sem("se_m")
            added, own, dif_done = sems("se_added", BODY), sem("se_own"), sem("se_dif")
            with ExitStack() as st:
                def tmp(name, shape, dt=FP32):
                    return st.enter_context(nc.sbuf_tensor(unique(name), shape, dt))
                Er = tmp("Er", [P, 2, GRP, F])
                eq_dst = tmp("eq_dst", [P, 2, GRP, P])
                eq_src = tmp("eq_src", [P, 2, GRP, P])
                earlier = tmp("earlier", [P, GRP, P])
                n_earlier = tmp("n_earlier", [P, GRP])
                shifts = tmp("shifts", [P, GRP])
                to_spare = tmp("to_spare", [P, TILES])
                idx = tmp("idx", [P, PAR, GRP], I32)
                Xs = tmp("Xs", [P, 2, GRP, F])
                M = tmp("M", [P, PAR, GRP, F])
                in_v = first_rows[0:EPAD, :].rearrange("(t p) f -> p t f", p=P)
                with nc.Block() as block:
                    @block.sync
                    def _(sp):
                        def load(i, g):
                            n, b = i * PAR + g, g % 2
                            wait(sp, x_done, n - 1)
                            sp.dma_start(Er[:, b, :, :], in_v[:, bass.ds(n * GRP, GRP), :]).then_inc(loaded[b], 16)
                        pipeline(sp, load)

                    @block.tensor
                    def _(pe):
                        def rows(i, g):
                            n, b = i * PAR + g, g % 2
                            wait(pe, eq_done, n * 2 - 2)
                            for base, parts in ((0, (dst_hi, dst_lo)), (2, (src_hi, src_lo))):
                                for k in range(GRP):
                                    for q in range(2):
                                        mm = pe.matmul(bank[base + b][:, k * P:k * P + P],
                                                       parts[q][:, bass.ds(n * GRP + k, 1)].broadcast_to([P, P]),
                                                       ident_b[:, :], start=q == 0, stop=q == 1)
                            mm.then_inc(rows_done, 1)

                        def expand(i, g):
                            n, b = i * PAR + g, g % 2
                            pe.wait_ge(loaded[b], (i * 2 + g // 2) * 16 + 16)
                            pe.wait_ge(eq_done, n * 2 + 1)
                            wait(pe, xs_done, n - 1)
                            for k in range(GRP):
                                mm = pe.matmul(bank[4 + b][:, k * F:k * F + F], eq_dst[:, b, k, :],
                                               Er[:, b, k, :], start=True, stop=True)
                            mm.then_inc(x_done, 1)

                        def total(i, g):
                            n, b = i * PAR + g, g % 2
                            pe.wait_ge(eq_done, n * 2 + 2)
                            pe.wait_ge(xs_done, n + 1)
                            wait(pe, m_done, n - 1)
                            for k in range(GRP):
                                mm = pe.matmul(bank[6 + b][:, k * F:k * F + F], eq_src[:, b, k, :],
                                               Xs[:, b, k, :], start=True, stop=True)
                            mm.then_inc(tot_done, 1)
                        pipeline(pe, rows, expand, total)

                    @block.vector
                    def _(dve):
                        dve.tensor_scalar(to_spare[:, :], row_f[:, :], -1.0, spare_row[:, :], ALU.mult, ALU.add
                                          ).then_inc(dif_done, 1)
                        dve.wait_ge(dif_done, 1)

                        def compare(i, g):
                            n, b = i * PAR + g, g % 2
                            t = bass.ds(n * GRP, GRP)
                            dve.wait_ge(rows_done, n + 1)
                            for q, (eq, ids, used) in enumerate(((eq_dst, dst_f, x_done), (eq_src, src_f, tot_done))):
                                wait(dve, used, n - 1)
                                dve.tensor_tensor(eq[:, b, :, :],
                                                  bank[2 * q + b][:, :].rearrange("p (k e) -> p k e", k=GRP),
                                                  ids[:, t].unsqueeze(2).broadcast_to([P, GRP, P]),
                                                  ALU.is_equal).then_inc(eq_done, 1)
                            dve.wait_ge(eq_done, n * 2 + 2)
                            wait(dve, own, n * 3)
                            dve.tensor_tensor(earlier[:, :, :], eq_src[:, b, :, :],
                                              before[:, :].unsqueeze(1).broadcast_to([P, GRP, P]),
                                              ALU.mult).then_inc(own, 1)
                            dve.wait_ge(own, n * 3 + 1)
                            dve.tensor_reduce(n_earlier[:, :], earlier[:, :, :], AX.X, ALU.add).then_inc(own, 1)
                            dve.wait_ge(own, n * 3 + 2)
                            wait(dve, idx_done, n)
                            dve.scalar_tensor_tensor(shifts[:, :], n_earlier[:, :], 0.0, to_spare[:, t],
                                                     ALU.is_gt, ALU.mult).then_inc(own, 1)
                            dve.wait_ge(own, n * 3 + 3)
                            for k in range(GRP):
                                wait(dve, added[g * GRP + k], i * 16)
                            dve.tensor_tensor(idx[:, g, :], shifts[:, :], row_f[:, t], ALU.add
                                              ).then_inc(idx_done, 1)
                        pipeline(dve, compare)

                    @block.scalar
                    def _(act):
                        def expanded(i, g):
                            n, b = i * PAR + g, g % 2
                            act.wait_ge(x_done, n + 1)
                            wait(act, tot_done, n - 1)
                            act.activation(Xs[:, b, :, :].rearrange("p k f -> p (k f)"), bank[4 + b][:, 0:GRP * F],
                                           ACT.Copy).then_inc(xs_done, 1)

                        def message(i, g):
                            n, b = i * PAR + g, g % 2
                            act.wait_ge(tot_done, n + 1)
                            for k in range(GRP):
                                wait(act, added[g * GRP + k], i * 16)
                            act.activation(M[:, g, :, :].rearrange("p k f -> p (k f)"), bank[6 + b][:, 0:GRP * F],
                                           ACT.Copy).then_inc(m_done, 1)
                        pipeline(act, expanded, message)

                    @block.gpsimd
                    def _(pool):
                        def add(i, g):
                            n, b = i * PAR + g, g % 2
                            pool.wait_ge(m_done, n + 1)
                            pool.wait_ge(idx_done, n + 1)
                            for k in range(GRP):
                                if g < 2:
                                    wait(pool, added[(g + 2) * GRP + k], i * 16)
                                else:
                                    wait(pool, added[(g - 2) * GRP + k], i * 16 + 16)
                                pool.sem_inc(pool_passed, 1)
                                pool.indirect_dma_start(rep[b * GRP + k],
                                                        bass.IndirectOffsetOnAxis(idx[:, g, k:k + 1], 0),
                                                        M[:, g, k, :], None, bounds_check=REP_ROWS - 1,
                                                        oob_is_err=True, compute_op=ALU.add
                                                        ).then_inc(added[g * GRP + k], 16)
                        pipeline(pool, add)
                        for s in added:
                            pool.wait_ge(s, ITERS * 16)

        def add_tables():
            ld, v = sems("at_ld", REPS), sem("at_v")
            bufs = (SQ, H, Y)
            with nc.Block() as block:
                @block.sync
                def _(sp):
                    for k in range(REPS):
                        wait(sp, v, k - 2)
                        sp.dma_start(bufs[k % 3], rep[k][0:NPAD, :].rearrange("(p a) f -> p a f", p=P)
                                     ).then_inc(ld[k], 16)

                @block.vector
                def _(dve):
                    for k in range(REPS):
                        dve.wait_ge(ld[k], 16)
                        wait(dve, v, k)
                        dve.tensor_tensor(X[:, :, :], X[:, :, :], bufs[k % 3], ALU.add).then_inc(v, 1)

        def gine_edges():
            wl, win_ready, gathered, attr_in = (
                sem("ge_wl"), sem("ge_win"), sems("ge_gathered", PAR), sems("ge_attr", 2))
            t_done, d_done, gates_done, s_done = sem("ge_t"), sem("ge_d"), sem("ge_gates"), sem("ge_s")
            back_done, w_done, sent = sem("ge_back"), sem("ge_w"), sems("ge_sent", 2)
            with ExitStack() as st:
                def tmp(name, shape, dt=FP32):
                    return st.enter_context(nc.sbuf_tensor(unique(name), shape, dt))
                win = tmp("win", [P, PAR, GRP], I32)
                G = tmp("G", [P, BODY, F])
                attr = tmp("attr", [EDGE_F, 2, GRP * P])
                We = tmp("We", [EDGE_F, F])
                be = tmp("be", [F, 1])
                D = tmp("D", [F, 2, GRP * P])
                S = tmp("S", [F, 2, GRP * P])
                Wo = tmp("Wo", [P, 2, GRP, F])
                out_v = r3.rearrange("(t p) f -> p t f", p=P)
                with nc.Block() as block:
                    @block.gpsimd
                    def _(pool):
                        def gather(i, g):
                            n = i * PAR + g
                            pool.wait_ge(win_ready, n + 1)
                            wait(pool, t_done, n - PAR + 1)
                            pool.sem_inc(pool_passed, 1)
                            for k in range(GRP):
                                s = g * GRP + k
                                pool.indirect_dma_start(
                                    G[:, s, :], None, htab[2], bass.IndirectOffsetOnAxis(win[:, g, k:k + 1], 0),
                                    bounds_check=NPAD - 1, oob_is_err=True).then_inc(gathered[g], 16)
                        pipeline(pool, gather)

                    @block.tensor
                    def _(pe):
                        pe.wait_ge(wl, 2 * 16)

                        def front(i, g):
                            n, b = i * PAR + g, g % 2
                            wait(pe, d_done, n - 1)
                            pe.wait_ge(attr_in[b], (i * 2 + g // 2) * 16 + 16)
                            pe.matmul(bank[b][0:F, :], We[:, :], attr[:, b, :], start=True, stop=False)
                            pe.wait_ge(gathered[g], i * (GRP * 16) + GRP * 16)
                            for k in range(GRP):
                                s = g * GRP + k
                                mm = pe.matmul(bank[b][0:F, k * P:k * P + P], G[:, s, :], ident[:, :],
                                               start=False, stop=k == GRP - 1)
                            mm.then_inc(t_done, 1)
                            wait(pe, s_done, n)
                            for k in range(GRP):
                                mm = pe.matmul(bank[2 + b][0:F, k * P:k * P + P],
                                               gate_sum[:, bass.ds(n * GRP + k, 1)].broadcast_to([P, F]),
                                               ident_b[:, :], start=True, stop=True)
                            mm.then_inc(gates_done, 1)

                        def back(i, g):
                            n, b = i * PAR + g, g % 2
                            pe.wait_ge(s_done, n + 2)
                            wait(pe, w_done, n - 1)
                            pe.sem_inc(pe_passed, 1)
                            for k in range(GRP):
                                tr = pe.transpose(bank[4 + b][:, k * F:k * F + F], S[:, b, k * P:k * P + P],
                                                  ident[0:F, 0:F])
                            tr.then_inc(back_done, 1)
                        pipeline(pe, front, back)

                    @block.scalar
                    def _(act):
                        act.wait_ge(wl, 2 * 16)

                        def message(i, g):
                            n, b = i * PAR + g, g % 2
                            act.wait_ge(t_done, n + 1)
                            wait(act, s_done, n)
                            act.activation(D[:, b, :], bank[b][0:F, :], ACT.Relu, bias=be[:, :]).then_inc(d_done, 1)

                        def evacuate(i, g):
                            n, b = i * PAR + g, g % 2
                            act.wait_ge(back_done, n + 1)
                            wait(act, sent[b], (i * 2 + g // 2) * 16)
                            act.activation(Wo[:, b, :, :].rearrange("p k f -> p (k f)"), bank[4 + b][:, 0:GRP * F],
                                           ACT.Copy).then_inc(w_done, 1)
                        pipeline(act, message, evacuate)

                    @block.vector
                    def _(dve):
                        dve.memset(S[:, 1, GRP * P - 1:GRP * P], 0.0).then_inc(s_done, 1)

                        def sources(n, g):
                            dve.tensor_copy(win[:, g, :], row_i[:, bass.ds(n * GRP, GRP)]).then_inc(win_ready, 1)

                        def scan(i, g):
                            n, b = i * PAR + g, g % 2
                            dve.wait_ge(gates_done, n + 1)
                            dve.wait_ge(d_done, n + 1)
                            wait(dve, back_done, n - 1)
                            dve.wait_ge(s_done, n + 1)
                            dve.tensor_tensor_scan(S[:, b, :], bank[2 + b][0:F, :], D[:, b, :],
                                                   S[:, 1 - b, GRP * P - 1:GRP * P], ALU.mult, ALU.add
                                                   ).then_inc(s_done, 1)
                            dve.wait_ge(gathered[g], i * (GRP * 16) + GRP * 16)
                            sources(n + PAR, g)

                        for g in range(PAR):
                            sources(g, g)
                        pipeline(dve, scan)

                    @block.sync
                    def _(sp):
                        sp.dma_start(We[:, :], weT).then_inc(wl, 16)
                        sp.dma_start(be[:, :], bec).then_inc(wl, 16)

                        def load(i, g):
                            n, b = i * PAR + g, g % 2
                            wait(sp, t_done, n - 1)
                            sp.dma_start(attr[:, b, :], attrT[:, bass.ds(n * GRP * P, GRP * P)]
                                         ).then_inc(attr_in[b], 16)

                        def nothing(i, g):
                            pass

                        def store(i, g):
                            n, b = i * PAR + g, g % 2
                            sp.wait_ge(w_done, n + 1)
                            sp.dma_start(out_v[:, bass.ds(n * GRP, GRP), :], Wo[:, b, :, :]).then_inc(sent[b], 16)
                        pipeline(sp, load, nothing, store)
                        for b in range(2):
                            sp.wait_ge(sent[b], ITERS * PAR // 2 * 16)

        def gine_nodes():
            wl, win_ready, fetched, u = sem("gn_wl"), sem("gn_win"), sems("gn_fetched", 2), sem("gn_u")
            t_done, aT_done, h_done, hid_done, o_done, x_done, b2_done = (
                sem("gn_t"), sem("gn_aT"), sem("gn_h"), sem("gn_hid"), sem("gn_o"), sem("gn_x"), sem("gn_b2"))
            sets = ((0, 4), (4, 3))
            with ExitStack() as st:
                def tmp(name, shape, dt=FP32):
                    return st.enter_context(nc.sbuf_tensor(unique(name), shape, dt))
                win = tmp("win", [P, 2, CH], I32)
                R = tmp("R", [P, 2, CH, F])
                U = tmp("U", [P, 2, CH, F])
                aT = tmp("aT", [F, 2, 4 * P])
                hid = tmp("hid", [F, 2, 4 * P])
                W1 = tmp("W1", [F, F])
                W2 = tmp("W2", [F, F])
                b1 = tmp("b1", [F, 1])
                b2 = tmp("b2", [P, F])
                with nc.Block() as block:
                    @block.sync
                    def _(sp):
                        for t, d in ((W1, g1T), (W2, g2T), (b1, g1b), (b2, g2b)):
                            sp.dma_start(t[:, :], d).then_inc(wl, 16)

                    @block.gpsimd
                    def _(pool):
                        fetch(pool, r3, EPAD - 1, win, R, win_ready, fetched)

                    @block.vector
                    def _(dve):
                        def inputs(j, q):
                            c = j * 2 + q
                            nodes = bass.ds(c * CH, CH)
                            dve.wait_ge(fetched[q], j * (CH * 16) + CH * 16)
                            wait(dve, t_done, c * 2 - 2)
                            dve.tensor_tensor(U[:, q, :, :], R[:, q, :, :],
                                              col["has"][:, nodes].unsqueeze(2).broadcast_to([P, CH, F]), ALU.mult
                                              ).then_inc(u, 1)
                            window(dve, win, end_i, j + 1, q, win_ready)
                            dve.wait_ge(u, c * 2 + 1)
                            dve.tensor_tensor(U[:, q, :, :], U[:, q, :, :], H[:, nodes, :], ALU.add).then_inc(u, 1)

                        def outputs(j, q):
                            c = j * 2 + q
                            for h, (first, count) in enumerate(sets):
                                a = bass.ds(c * CH + first, count)
                                dve.wait_ge(o_done, c * 2 + h + 1)
                                dve.tensor_tensor(X[:, a, :], X[:, a, :],
                                                  bank[4 + h][:, 0:count * F].rearrange("p (k f) -> p k f", f=F),
                                                  ALU.add).then_inc(x_done, 1)

                        for q in range(2):
                            window(dve, win, end_i, 0, q, win_ready)
                        dve.wait_ge(wl, 4 * 16)
                        dve.tensor_tensor(X[:, :, :], X[:, :, :], b2[:, :].unsqueeze(1).broadcast_to([P, NT, F]),
                                          ALU.add).then_inc(b2_done, 1)
                        dve.wait_ge(b2_done, 1)
                        inputs(0, 0)
                        inputs(0, 1)
                        outputs(0, 0)
                        with dve.Fori(1, NCH // 2) as j:
                            inputs(j, 0)
                            outputs(j - 1, 1)
                            inputs(j, 1)
                            outputs(j, 0)
                        outputs(NCH // 2 - 1, 1)

                    @block.tensor
                    def _(pe):
                        pe.wait_ge(wl, 4 * 16)

                        def one(j, q):
                            c = j * 2 + q
                            pe.wait_ge(u, c * 2 + 2)
                            for h, (first, count) in enumerate(sets):
                                wait(pe, aT_done, c * 2 + h - 1)
                                pe.sem_inc(pe_passed, 1)
                                for k in range(count):
                                    tr = pe.transpose(bank[h][0:F, k * P:k * P + P], U[:, q, first + k, :],
                                                      ident[:, :])
                                tr.then_inc(t_done, 1)
                            for h, (first, count) in enumerate(sets):
                                pe.wait_ge(aT_done, c * 2 + h + 1)
                                wait(pe, hid_done, c * 2 + h - 1)
                                pe.sem_inc(pe_passed, 1)
                                pe.matmul(bank[2 + h][0:F, 0:count * P], W1[:, :], aT[:, h, 0:count * P],
                                          start=True, stop=True).then_inc(h_done, 1)
                            for h, (first, count) in enumerate(sets):
                                pe.wait_ge(hid_done, c * 2 + h + 1)
                                wait(pe, x_done, c * 2 + h - 1)
                                for k in range(count):
                                    mm = pe.matmul(bank[4 + h][:, k * F:k * F + F], hid[:, h, k * P:k * P + P],
                                                   W2[:, :], start=True, stop=True)
                                mm.then_inc(o_done, 1)
                        chunks(pe, one)

                    @block.scalar
                    def _(act):
                        act.wait_ge(wl, 4 * 16)

                        def one(j, q):
                            c = j * 2 + q
                            for h, (first, count) in enumerate(sets):
                                act.wait_ge(t_done, c * 2 + h + 1)
                                wait(act, h_done, c * 2 + h - 1)
                                act.activation(aT[:, h, 0:count * P], bank[h][0:F, 0:count * P], ACT.Copy
                                               ).then_inc(aT_done, 1)
                            for h, (first, count) in enumerate(sets):
                                act.wait_ge(h_done, c * 2 + h + 1)
                                wait(act, o_done, c * 2 + h - 1)
                                act.activation(hid[:, h, 0:count * P], bank[2 + h][0:F, 0:count * P], ACT.Relu,
                                               bias=b1[:, :]).then_inc(hid_done, 1)
                        chunks(act, one)

        count_dst()
        norm(0, None)
        relational()
        norm(1, htab[0], negative=True)
        pna_edges()
        pna_nodes()
        norm(2, htab[1])
        place_first_rows()
        sum_edges()
        add_tables()
        norm(3, htab[2])
        gine_edges()
        gine_nodes()

        stored = sem("stored")
        with nc.Block() as block:
            @block.sync
            def _(sp):
                sp.dma_start(out, X[:, :, :]).then_inc(stored, 16)
                sp.wait_ge(stored, 16)


def kernel(x, src, dst, edge_attr_32, edge_type_9, L0_gnn_weights, L0_gnn_biases, L1_gnn_W, L1_gnn_b,
           L1_gnn_gamma, L1_gnn_beta, L3_gnn_We, L3_gnn_be, L3_gnn_W1, L3_gnn_b1, L3_gnn_W2, L3_gnn_b2):
    import numpy as np
    import concourse.bacc as bacc
    from concourse.bass_utils import run_bass_kernel_spmd

    def edges(a, fill):
        a = np.asarray(a)
        a = np.concatenate([a, np.full(EPAD - EDGES, fill, a.dtype)])
        return a.reshape(TILES, P).T

    dst = np.asarray(dst)
    type_flat = np.concatenate([np.asarray(edge_type_9), np.zeros(EPAD - EDGES, np.int32)])
    dst_flat = np.concatenate([dst, np.full(EPAD - EDGES, LAST, dst.dtype)])
    head = np.concatenate([dst_flat[::P], np.full(13 * P - TILES, LAST, dst.dtype)]).reshape(13, P).T
    before = np.concatenate([np.full(1, -1, dst.dtype), dst_flat[:-1]])
    x_pad = np.concatenate([np.asarray(x), np.zeros((NPAD - NODES, F), np.float32)])
    attr = np.concatenate([np.asarray(edge_attr_32), np.zeros((EPAD - EDGES, EDGE_F), np.float32)])
    w0 = np.asarray(L0_gnn_weights)[2].transpose(1, 0, 2).reshape(F, 2 * REL * F)
    b0 = np.asarray(L0_gnn_biases)[2].reshape(1, 2 * REL * F)
    w1 = np.asarray(L1_gnn_W).reshape(3, 2, P, F).transpose(2, 1, 0, 3).reshape(P, 2, 3 * F)

    def rows(v):
        return np.broadcast_to(np.asarray(v).reshape(1, F), (P, F))

    arrays = {
        "x3": x_pad.reshape(NT, P, F).transpose(1, 0, 2),
        "srcT": edges(src, LAST), "dstT": edges(dst, LAST), "dstprevT": before.reshape(TILES, P).T,
        "typeT": edges(edge_type_9, 0), "typeM": type_flat.reshape(P, TILES), "heads": head, "attrT": attr.T,
        "w0": np.concatenate([w0, b0]), "w1": w1, "b1r": rows(L1_gnn_b), "gam": rows(L1_gnn_gamma),
        "bet": rows(L1_gnn_beta), "weT": np.asarray(L3_gnn_We).T, "bec": np.asarray(L3_gnn_be).reshape(F, 1),
        "g1T": np.asarray(L3_gnn_W1).T, "g1b": np.asarray(L3_gnn_b1).reshape(F, 1),
        "g2T": np.asarray(L3_gnn_W2).T, "g2b": rows(L3_gnn_b2),
    }
    arrays = {n: np.ascontiguousarray(a) for n, a in arrays.items()}
    nc = bacc.Bacc("TRN2", target_bir_lowering=False, num_devices=1)
    args = [nc.dram_tensor(n, a.shape, mybir.dt.from_np(a.dtype), kind="ExternalInput").ap()
            for n, a in arrays.items()]
    out = nc.dram_tensor("out", (P, NT, F), FP32, kind="ExternalOutput").ap()
    build(nc, *args, out)
    r = run_bass_kernel_spmd(nc, [arrays], core_ids=[0])
    return r.results[0]["out"].transpose(1, 0, 2).reshape(NPAD, F)[:NODES]
```

```python
import concourse.bass as bass
from concourse import mybir
from contextlib import ExitStack

FP32 = mybir.dt.float32
BF16 = mybir.dt.bfloat16
FP16 = mybir.dt.float16
I32 = mybir.dt.int32
ALU = mybir.AluOpType
ACT = mybir.ActivationFunctionType
AX = mybir.AxisListType

P = 128
NODES, F, EDGES, EDGE_F, REL = 12500, 64, 200000, 32, 9
NT = -(-NODES // P)
NPAD = NT * P
LAST = NPAD - 1
TILES = 1568
EPAD = TILES * P
BODY = 16
GRP = 4
PAR = BODY // GRP
ITERS = TILES // BODY
KEYS = NT * REL
KH = KEYS // 2
REPS = 8
REP_ROWS = NPAD + P
E_ROWS = EPAD + NPAD
ZW = REP_ROWS * F // P
ZE = E_ROWS * F // P // 17
CH = 7
NCH = NT // CH
REL8 = REL - 1
AVG_D_LOG = 2.833
EPS = 1e-5
BIG = 1e30


def wait(eng, s, value):
    if not (isinstance(value, int) and value <= 0):
        eng.wait_ge(s, value)


def at(i, g):
    return i + g // PAR, g % PAR


def pipeline(eng, *stages):
    depth = len(stages) - 1

    def body(i, first=False, last=False):
        if first:
            for g in range(depth):
                for j in range(g + 1):
                    stages[j](*at(0, g - j))
        for g in range(PAR):
            for j, stage in enumerate(stages):
                if not (last and g + depth - j >= PAR):
                    stage(*at(i, g + depth - j))

    body(0, first=True)
    with eng.Fori(1, ITERS - 1) as i:
        body(i)
    body(ITERS - 1, last=True)


def chunks(eng, one):
    for q in range(2):
        one(0, q)
    with eng.Fori(1, NCH // 2) as j:
        for q in range(2):
            one(j, q)


def build(nc, x3, srcT, dstT, dstprevT, typeT, typeM, dstM, heads, attrT, w0, w1, b1r, gam, bet,
          weT, bec, g1T, g1b, g2T, g2b, out):
    ctx = ExitStack()
    with ctx:
        def sb(name, shape, dt=FP32):
            return ctx.enter_context(nc.sbuf_tensor(name, shape, dt))

        names = {}

        def unique(name):
            names[name] = names.get(name, 0) + 1
            return f"{name}_{names[name]}"

        def sem(name):
            return ctx.enter_context(nc.semaphore(name))

        def sems(name, n):
            return [sem(f"{name}{i}") for i in range(n)]

        bank = [ctx.enter_context(nc.psum_tensor(f"bank{i}", [P, 512], FP32)) for i in range(8)]

        htab = [nc.dram_tensor(f"htab{i}", [NPAD, w], FP32).ap() for i, w in enumerate((2 * F, F, F))]
        r1 = nc.dram_tensor("r1", [EPAD, 4 * F], FP32).ap()
        r3 = nc.dram_tensor("r3", [EPAD, F], FP32).ap()
        first_rows = nc.dram_tensor("first_rows", [E_ROWS, F], FP32).ap()
        type_sums = nc.dram_tensor("type_sums", [EPAD, REL8], FP32).ap()
        rep = [nc.dram_tensor(f"rep{i}", [REP_ROWS, F], FP32).ap() for i in range(REPS)]

        X = sb("X", [P, NT, F])
        HY = sb("HY", [P, 2 * NT * F])
        H = HY[:, 0:NT * F].rearrange("p (a f) -> p a f", f=F)
        Y = HY[:, NT * F:2 * NT * F].rearrange("p (a f) -> p a f", f=F)
        Z = sb("Z", [P, ZW])
        SQ = Z[:, 0:NT * F].rearrange("p (a f) -> p a f", f=F)
        row_i = sb("row_i", [P, TILES + BODY], I32)
        src_f = sb("src_f", [P, TILES])
        dst_f = sb("dst_f", [P, TILES])
        key_src = sb("key_src", [P, TILES])
        row_f = sb("row_f", [P, TILES])
        src_hi, src_lo, dst_hi, dst_lo, gate_sum, gate_max = (
            sb(n, [P, TILES], BF16) for n in ("src_hi", "src_lo", "dst_hi", "dst_lo", "gate_sum", "gate_max"))
        ident = sb("ident", [P, P])
        ident_b = sb("ident_b", [P, P], BF16)
        ones = sb("ones", [P, P])
        upto = sb("upto", [P, P])
        strict = sb("strict", [P, P])
        steps_to_counts = sb("steps_to_counts", [P, P])
        shift = sb("shift", [P, P])
        wrap = sb("wrap", [P, P])
        before = sb("before", [P, P])
        spare_row = sb("spare_row", [P, 1])
        real = sb("real", [P, 1])
        eps_c = sb("eps_c", [P, 1])
        C = sb("C", [P, NT, 2 * REL])
        run_sums = C[:, :, REL:2 * REL]
        col = {n: sb("col_" + n, [P, NT]) for n in
               ("cnt", "deg", "rcnt", "has", "neghas", "rdeg", "end", "some", "amp", "att", "t0", "t1", "mean", "rstd")}
        end_i = sb("end_i", [P, NT + 2 * CH], I32)
        start_i = sb("start_i", [P, NT + 2 * CH], I32)
        heads_i = sb("heads_i", [P, 13], I32)

        ldx, ldi, cst, prep = sem("ldx"), sem("ldi"), sem("cst"), sem("prep")
        pool_passed, pe_passed = sem("pool_passed"), sem("pe_passed")
        with ExitStack() as st:
            def tmp(name, shape, dt=FP32):
                return st.enter_context(nc.sbuf_tensor(unique(name), shape, dt))
            dst_i, dstprev_i, src_i, ia, ib, type_i, type_m = (
                HY[:, n * TILES:n * TILES + TILES].bitcast(I32) for n in range(7))
            src_step = tmp("src_step", [P, TILES], BF16)
            type_b = tmp("type_b", [P, TILES], BF16)
            iota_p = tmp("iota_p", [P, P], BF16)
            iota_k = tmp("iota_k", [P, KEYS], FP16)
            zero_b = tmp("zero_b", [P, KH], BF16)
            node_n = tmp("node_n", [P, NT])
            hz = sem("hz")
            heads_id = tmp("heads_id", [P, 13], I32)
            heads_lo = tmp("heads_lo", [P, 13], I32)
            heads_hi = tmp("heads_hi", [P, 13], I32)
            heads_lo_b = tmp("heads_lo_b", [P, 13], BF16)
            heads_hi_b = tmp("heads_hi_b", [P, 13], BF16)
            with nc.Block() as block:
                @block.sync
                def _(sp):
                    sp.dma_start(src_i, srcT).then_inc(ldi, 16)
                    sp.dma_start(dst_i, dstT).then_inc(ldi, 16)
                    sp.dma_start(type_i, typeT).then_inc(ldi, 16)
                    sp.dma_start(dstprev_i, dstprevT).then_inc(ldi, 16)
                    sp.dma_start(type_m, typeM).then_inc(ldi, 16)
                    sp.dma_start(heads_id[:, :], heads).then_inc(ldi, 16)
                    sp.dma_start(X[:, :, :], x3).then_inc(ldx, 16)
                    sp.wait_ge(ldx, 16)

                @block.gpsimd
                def _(pool):
                    n = [0]

                    def step(ins):
                        ins.then_inc(cst, 1)
                        n[0] += 1
                        pool.wait_ge(cst, n[0])

                    def diagonal(t, fill, base):
                        step(pool.affine_select(out=t[:, :], in_=t[:, :], compare_op=ALU.not_equal, fill=fill,
                                                base=base, pattern=[[-1, P]], channel_multiplier=1))

                    for t in (ident, steps_to_counts, shift, wrap):
                        step(pool.memset(t[:, :], 0.0))
                    step(pool.memset(ones[:, :], 1.0))
                    step(pool.memset(real[:, :], 1.0))
                    step(pool.memset(eps_c[:, :], EPS))
                    step(pool.memset(end_i[:, :], 0))
                    step(pool.memset(start_i[:, :], 0))
                    step(pool.iota(spare_row[:, :], [[0, 1]], base=NPAD, channel_multiplier=1,
                                   allow_small_or_imprecise_dtypes=True))
                    diagonal(ident, 1.0, 0)
                    diagonal(steps_to_counts, 0.5, 0)
                    diagonal(steps_to_counts, -0.5, -1)
                    diagonal(steps_to_counts, 0.5, P - 1)
                    diagonal(shift, 1.0, 1)
                    diagonal(wrap, 1.0, -(P - 1))
                    step(pool.affine_select(out=upto[:, :], in_=ones[:, :], compare_op=ALU.is_ge, fill=0.0,
                                            base=0, pattern=[[1, P]], channel_multiplier=-1))
                    step(pool.affine_select(out=strict[:, :], in_=ones[:, :], compare_op=ALU.is_gt, fill=0.0,
                                            base=0, pattern=[[1, P]], channel_multiplier=-1))
                    step(pool.affine_select(out=before[:, :], in_=ones[:, :], compare_op=ALU.is_gt, fill=0.0,
                                            base=0, pattern=[[-1, P]], channel_multiplier=1))
                    step(pool.affine_select(out=real[:, :], in_=real[:, :], compare_op=ALU.is_gt, fill=0.0,
                                            base=NODES - (NT - 1) * P, pattern=[[0, 1]], channel_multiplier=-1))
                    pool.iota(iota_p[:, :], [[1, P]], base=0, channel_multiplier=0,
                              allow_small_or_imprecise_dtypes=True).then_inc(hz, 1)
                    pool.iota(iota_k[:, :], [[1, KEYS]], base=0, channel_multiplier=0,
                              allow_small_or_imprecise_dtypes=True).then_inc(hz, 1)
                    pool.memset(zero_b[:, :], 0.0).then_inc(hz, 1)
                    pool.iota(node_n[:, :], [[P, NT]], base=0, channel_multiplier=1,
                              allow_small_or_imprecise_dtypes=True).then_inc(hz, 1)

                @block.vector
                def _(dve):
                    n = [0]

                    def step(ins):
                        ins.then_inc(prep, 1)
                        n[0] += 1

                    def seen():
                        dve.wait_ge(prep, n[0])

                    def split(e_id, lo_i, hi_i):
                        step(dve.tensor_single_scalar(lo_i, e_id, P - 1, ALU.bitwise_and))
                        step(dve.tensor_single_scalar(hi_i, e_id, 7, ALU.arith_shift_right))
                        seen()

                    step(dve.memset(Z[:, :], 0.0))
                    step(dve.memset(row_i[:, TILES:TILES + BODY], 0))
                    dve.wait_ge(ldi, 6 * 16)
                    step(dve.tensor_copy(src_f[:, :], src_i))
                    step(dve.tensor_copy(dst_f[:, :], dst_i))
                    step(dve.tensor_tensor(gate_sum[:, :], dst_i, dstprev_i, ALU.is_equal))
                    step(dve.tensor_copy(key_src[:, :], type_i))
                    step(dve.tensor_copy(type_b[:, :], type_m))
                    seen()
                    step(dve.tensor_scalar(gate_max[:, :], gate_sum[:, :], 1.0, BIG, ALU.subtract, ALU.mult))
                    split(src_i, ia, ib)
                    step(dve.tensor_copy(src_lo[:, :], ia))
                    step(dve.tensor_scalar(src_step[:, :], ia, 0.5, None, ALU.add))
                    step(dve.tensor_scalar(src_hi[:, :], ib, float(P), None, ALU.mult))
                    step(dve.scalar_tensor_tensor(key_src[:, :], ib, float(REL), key_src[:, :], ALU.mult, ALU.add))
                    step(dve.scalar_tensor_tensor(row_f[:, :], ia, float(NT), ib, ALU.mult, ALU.add))
                    seen()
                    step(dve.tensor_copy(row_i[:, 0:TILES], row_f[:, :]))
                    split(dst_i, ia, ib)
                    step(dve.tensor_copy(dst_lo[:, :], ia))
                    step(dve.tensor_scalar(dst_hi[:, :], ib, float(P), None, ALU.mult))
                    split(heads_id[:, :], heads_lo[:, :], heads_hi[:, :])
                    step(dve.scalar_tensor_tensor(heads_i[:, :], heads_lo[:, :], float(NT), heads_hi[:, :],
                                                  ALU.mult, ALU.add))
                    step(dve.tensor_copy(heads_lo_b[:, :], heads_lo[:, :]))
                    step(dve.tensor_copy(heads_hi_b[:, :], heads_hi[:, :]))
                    dve.wait_ge(cst, 11)
                    step(dve.tensor_copy(ident_b[:, :], ident[:, :]))

            zdone, ts_out = sems("zdone", 2), sem("ts_out")
            oh_ready, step_ready, oh_used = sem("oh_ready"), sem("step_ready"), sem("oh_used")
            sums_done, run, off_done, off_added = (
                sem("sums_done"), sem("run"), sem("off_done"), sem("off_added"))
            heads_pe, tiles_found = sem("heads_pe"), sem("tiles_found")
            asked, rows_in, counted, sums_in = sem("asked"), sems("rows_in", 2), sem("counted"), sems("sums_in", 2)
            onehot_k = tmp("onehot_k", [P, 4, KEYS], BF16)
            step_src = tmp("step_src", [P, 4, P], BF16)
            heads_is_lo = tmp("heads_is_lo", [P, 13, P], BF16)
            heads_is_hi = tmp("heads_is_hi", [P, 13, NT], BF16)
            is_type = tmp("is_type", [P, 2, TILES], BF16)
            offset = tmp("offset", [P, REL8])
            at_head, ha, hb = col["t0"], col["t1"], col["mean"]
            tile_f = col["rstd"]
            tile_i = tmp("tile_i", [P, NT], I32)
            in_tile = tmp("in_tile", [P, NT])
            win = tmp("win", [P, 2, CH], I32)
            dst_rows = tmp("dst_rows", [P, 2, CH, P], I32)
            up_to = tmp("up_to", [P, CH, P])
            R = tmp("R", [P, 2, CH, REL8])
            type_run = HY[:, :].rearrange("p (j r) -> p j r", r=REL8)
            with nc.Block() as block:
                @block.sync
                def _(sp):
                    ev = first_rows.rearrange("(z p n) f -> z p (n f)", p=P, z=17)
                    for z in range(17):
                        sp.dma_start(ev[z], Z[:, 0:ZE]).then_inc(zdone[0], 16)
                    for t in rep:
                        sp.dma_start(t.rearrange("(p n) f -> p (n f)", p=P), Z[:, :]).then_inc(zdone[1], 16)
                    sp.wait_ge(off_added, REL8)
                    sp.dma_start(type_sums.rearrange("(p j) r -> p (j r)", p=P), HY[:, :]).then_inc(ts_out, 16)
                    sp.wait_ge(zdone[0], 17 * 16)
                    sp.wait_ge(zdone[1], REPS * 16)
                    sp.wait_ge(ts_out, 16)

                @block.gpsimd
                def _(pool):
                    pool.wait_ge(hz, 4)
                    pool.wait_ge(off_done, 2)
                    for k in range(1, REL8):
                        pool.tensor_scalar(type_run[:, :, k], type_run[:, :, k], offset[:, k:k + 1], None, ALU.add
                                           ).then_inc(off_added, 1)
                    pool.wait_ge(tiles_found, 1)

                    def ask(j, q, index, rows, table, limit, arrived, before):
                        c = j * 2 + q
                        pool.tensor_copy(win[:, q, :], index[:, bass.ds(c * CH, CH)]).then_inc(asked, 1)
                        pool.wait_ge(asked, c + before + 1)
                        pool.sem_inc(pool_passed, 1)
                        for k in range(CH):
                            pool.indirect_dma_start(rows[:, q, k, :], None, table,
                                                    bass.IndirectOffsetOnAxis(win[:, q, k:k + 1], 0),
                                                    bounds_check=limit, oob_is_err=True).then_inc(arrived[q], 16)

                    def behind(front, back):
                        front(0, 0)
                        front(0, 1)
                        back(0, 0)
                        with pool.Fori(1, NCH // 2) as j:
                            front(j, 0)
                            back(j - 1, 1)
                            front(j, 1)
                            back(j, 0)
                        back(NCH // 2 - 1, 1)

                    OPS = 10

                    def ask_edges(j, q):
                        ask(j, q, tile_i, dst_rows, dstM, TILES - 1, rows_in, 0)

                    def count(j, q):
                        c = j * 2 + q
                        nodes = bass.ds(c * CH, CH)
                        pool.wait_ge(rows_in[q], j * (CH * 16) + CH * 16)
                        wait(pool, counted, c * OPS)
                        pool.sem_inc(pool_passed, 1)
                        pool.tensor_copy(up_to[:, :, :], dst_rows[:, q, :, :]).then_inc(counted, 1)
                        pool.wait_ge(counted, c * OPS + 1)
                        pool.tensor_tensor(up_to[:, :, :], up_to[:, :, :],
                                           node_n[:, nodes].unsqueeze(2).broadcast_to([P, CH, P]), ALU.subtract
                                           ).then_inc(counted, 1)
                        pool.wait_ge(counted, c * OPS + 2)
                        pool.sem_inc(pool_passed, 1)
                        pool.tensor_scalar(up_to[:, :, :], up_to[:, :, :], 0.0, None, ALU.is_le
                                           ).then_inc(counted, 1)
                        for h in range(7):
                            w = P >> h + 1
                            total = up_to[:, :, 0:w] if w > 1 else in_tile[:, nodes].unsqueeze(2)
                            pool.wait_ge(counted, c * OPS + 3 + h)
                            pool.tensor_tensor(total, up_to[:, :, 0:w], up_to[:, :, w:2 * w], ALU.add
                                               ).then_inc(counted, 1)
                    behind(ask_edges, count)

                    pool.wait_ge(counted, NCH * OPS)
                    pool.tensor_scalar(tile_f[:, :], tile_f[:, :], float(P), None, ALU.mult).then_inc(counted, 1)
                    pool.wait_ge(counted, NCH * OPS + 1)
                    pool.tensor_tensor(col["end"][:, :], tile_f[:, :], in_tile[:, :], ALU.add).then_inc(counted, 1)
                    pool.wait_ge(counted, NCH * OPS + 2)
                    pool.tensor_scalar(end_i[:, 0:NT], col["end"][:, :], 1.0, 0.0, ALU.subtract, ALU.max
                                       ).then_inc(counted, 1)
                    pool.tensor_copy(run_sums[:, :, REL8:REL].rearrange("p a r -> p (a r)"), col["end"][:, :]
                                     ).then_inc(counted, 1)
                    pool.wait_ge(counted, NCH * OPS + 3)
                    pool.wait_ge(ts_out, 16)

                    def ask_sums(j, q):
                        ask(j, q, end_i, R, type_sums, EPAD - 1, sums_in, NCH)

                    def keep(j, q):
                        c = j * 2 + q
                        pool.wait_ge(sums_in[q], j * (CH * 16) + CH * 16)
                        pool.tensor_copy(run_sums[:, bass.ds(c * CH, CH), 0:REL8], R[:, q, :, :]
                                         ).then_inc(counted, 1)
                        pool.wait_ge(counted, c + NCH * OPS + 5)
                    behind(ask_sums, keep)

                @block.vector
                def _(dve):
                    n = [0]

                    def step(ins):
                        ins.then_inc(run, 1)
                        n[0] += 1
                        return n[0]

                    dve.wait_ge(hz, 2)
                    step(dve.tensor_tensor(heads_is_lo[:, :, :], iota_p[:, :].unsqueeze(1).broadcast_to([P, 13, P]),
                                           heads_lo_b[:, :].unsqueeze(2).broadcast_to([P, 13, P]), ALU.is_equal))
                    step(dve.tensor_tensor(heads_is_hi[:, :, :],
                                           iota_p[:, 0:NT].unsqueeze(1).broadcast_to([P, 13, NT]),
                                           heads_hi_b[:, :].unsqueeze(2).broadcast_to([P, 13, NT]), ALU.is_equal))
                    assert n[0] == 2

                    scanned = []
                    for k in range(REL8):
                        if k == REL8 // 2:
                            dve.wait_ge(heads_pe, 1)
                            assert step(dve.tensor_copy(at_head[:, :], bank[3][:, 0:NT])) == 11
                        if k >= 2:
                            dve.wait_ge(run, scanned[k - 2])
                        now = step(dve.tensor_scalar(is_type[:, k % 2, :], type_b[:, :], float(k), None,
                                                     ALU.is_equal))
                        dve.wait_ge(run, now)
                        scanned.append(step(dve.tensor_tensor_scan(type_run[:, :, k], ones[:, 0:1].broadcast_to([P, TILES]),
                                                                   is_type[:, k % 2, :], 0.0, ALU.mult, ALU.add)))
                    assert n[0] == 19
                    dve.wait_ge(heads_pe, 2)
                    dve.wait_ge(run, step(dve.tensor_copy(ha[:, :], bank[5][:, 0:NT])))
                    dve.wait_ge(run, step(dve.tensor_tensor_scan(hb[:, :], ones[:, 0:NT], ha[:, :], 0.0,
                                                                 ALU.mult, ALU.add)))
                    dve.wait_ge(run, step(dve.tensor_tensor(hb[:, :], hb[:, :], ha[:, :], ALU.subtract)))
                    dve.wait_ge(run, step(dve.tensor_tensor(hb[:, :], bank[4][:, 0:NT], hb[:, :], ALU.add)))
                    dve.wait_ge(run, step(dve.tensor_scalar(hb[:, :], hb[:, :], 1.0, 0.0, ALU.subtract, ALU.max)))
                    dve.wait_ge(run, step(dve.tensor_scalar(tile_f[:, :], hb[:, :], float(TILES - 1), None,
                                                            ALU.min)))
                    dve.tensor_copy(tile_i[:, :], tile_f[:, :]).then_inc(tiles_found, 1)
                    dve.wait_ge(off_done, 1)
                    dve.tensor_copy(offset[:, :], bank[7][:, 0:REL8]).then_inc(off_done, 1)
                    with dve.Fori(0, ITERS) as i:
                        for k in range(BODY):
                            s = k % 4
                            dve.wait_ge(oh_used, i * BODY + k + 1)
                            dve.tensor_scalar(onehot_k[:, s, :], iota_k[:, :], key_src[:, bass.ds(i * BODY + k, 1)],
                                              None, ALU.is_equal).then_inc(oh_ready, 1)

                @block.scalar
                def _(act):
                    act.wait_ge(off_done, 2)
                    act.activation(type_run[:, :, 0], type_run[:, :, 0], ACT.Identity, bias=offset[:, 0:1]
                                   ).then_inc(off_added, 1)
                    act.wait_ge(hz, 1)
                    with act.Fori(0, ITERS) as i:
                        for k in range(BODY):
                            s = k % 4
                            act.wait_ge(oh_used, i * BODY + k + 1)
                            act.activation(step_src[:, s, :], iota_p[:, :], ACT.Sign,
                                           bias=src_step[:, bass.ds(i * BODY + k, 1)], scale=-1.0
                                           ).then_inc(step_ready, 1)

                @block.tensor
                def _(pe):
                    pe.sem_inc(oh_used, 4)
                    pe.wait_ge(hz, 3)
                    for b in range(2):
                        pe.matmul(bank[b][:, 0:KH], zero_b[:, 0:P], zero_b[:, 0:KH], start=True, stop=False,
                                  skip_group_check=True)
                    pe.wait_ge(run, 2)
                    for j in range(13):
                        mm = pe.matmul(bank[3][:, 0:NT], heads_is_lo[:, j, :], heads_is_hi[:, j, :],
                                       start=j == 0, stop=j == 12)
                    mm.then_inc(heads_pe, 1)
                    pe.wait_ge(run, 11)
                    pe.matmul(bank[4][:, 0:NT], upto[:, :], at_head[:, :], start=True, stop=True)
                    pe.matmul(bank[5][:, 0:NT], ones[:, :], at_head[:, :], start=True, stop=True
                              ).then_inc(heads_pe, 1)
                    pe.wait_ge(run, 19)
                    pe.matmul(bank[7][:, 0:REL8], strict[:, :], type_run[:, TILES - 1, :], start=True, stop=True
                              ).then_inc(off_done, 1)
                    with pe.Fori(0, ITERS) as i:
                        for k in range(BODY):
                            s = k % 4
                            pe.wait_ge(step_ready, i * BODY + k + 1)
                            pe.wait_ge(oh_ready, i * BODY + k + 1)
                            for half in range(2):
                                mm = pe.matmul(bank[half][:, 0:KH], step_src[:, s, :],
                                               onehot_k[:, s, half * KH:half * KH + KH],
                                               start=False, stop=False, skip_group_check=True)
                            mm.then_inc(oh_used, 1)
                    for b in range(2):
                        mm = pe.matmul(bank[b][:, 0:KH], zero_b[:, 0:P], zero_b[:, 0:KH], start=False,
                                       stop=True, skip_group_check=True)
                    mm.then_inc(sums_done, 1)

        nn = [0]
        nd, nd_pe, nd_io, nd_act = sem("nd"), sem("nd_pe"), sem("nd_io"), sem("nd_act")
        with ExitStack() as st:
            def tmp(name, shape, dt=FP32):
                return st.enter_context(nc.sbuf_tensor(unique(name), shape, dt))
            node_id = tmp("node_id", [P, NT])
            ta = tmp("ta", [P, NT])
            tb = tmp("tb", [P, NT])
            steps = tmp("steps", [P, KEYS])
            half = NT // 2
            with nc.Block() as block:
                @block.gpsimd
                def _(pool):
                    pool.iota(node_id[:, :], [[P, NT]], base=EPAD, channel_multiplier=1,
                              allow_small_or_imprecise_dtypes=True).then_inc(nd_io, 1)

                @block.vector
                def _(dve):
                    def step(ins):
                        ins.then_inc(nd, 1)
                        nn[0] += 1
                        dve.wait_ge(nd, nn[0])
                    step(dve.tensor_scalar(col["some"][:, :], col["end"][:, :], 1.0, None, ALU.min))
                    step(dve.tensor_tensor(run_sums[:, :, :], run_sums[:, :, :],
                                           col["some"][:, :].unsqueeze(2).broadcast_to([P, NT, REL]), ALU.mult))
                    dve.wait_ge(sums_done, 1)
                    for b in range(2):
                        step(dve.tensor_copy(steps[:, b * KH:b * KH + KH], bank[b][:, 0:KH]))
                    dve.wait_ge(nd_pe, 1)
                    for b in range(2):
                        a = slice(b * half, b * half + half)
                        step(dve.tensor_tensor(run_sums[:, a, :], run_sums[:, a, :],
                                               bank[2 + b][:, 0:KH].rearrange("p (a r) -> p a r", r=REL),
                                               ALU.subtract))
                    step(dve.tensor_copy(col["deg"][:, :], C[:, :, 2 * REL - 1:2 * REL].rearrange("p a r -> p (a r)")))
                    assert nn[0] == 7
                    dve.wait_ge(nd_pe, 3)
                    for b in range(2):
                        step(dve.tensor_copy(C[:, b * half:b * half + half, 0:REL],
                                             bank[4 + b][:, 0:KH].rearrange("p (a r) -> p a r", r=REL)))
                    step(dve.tensor_reduce(ta[:, :], C[:, :, REL:2 * REL - 1], AX.X, ALU.add))
                    step(dve.tensor_tensor(C[:, :, 2 * REL - 1:2 * REL].rearrange("p a r -> p (a r)"),
                                           col["deg"][:, :], ta[:, :], ALU.subtract))
                    step(dve.tensor_reduce(ta[:, :], C[:, :, 0:REL], AX.X, ALU.add))
                    step(dve.tensor_tensor(col["cnt"][:, :], ta[:, :], col["deg"][:, :], ALU.add))
                    step(dve.tensor_scalar(ta[:, :], col["cnt"][:, :], 1.0, None, ALU.max))
                    step(dve.reciprocal(col["rcnt"][:, :], ta[:, :]))
                    step(dve.tensor_scalar(col["has"][:, :], col["deg"][:, :], 1.0, None, ALU.min))
                    step(dve.tensor_scalar(col["neghas"][:, :], col["has"][:, :], -1.0, None, ALU.mult))
                    step(dve.tensor_scalar(ta[:, :], col["deg"][:, :], 1.0, None, ALU.max))
                    step(dve.reciprocal(tb[:, :], ta[:, :]))
                    step(dve.tensor_tensor(col["rdeg"][:, :], tb[:, :], col["has"][:, :], ALU.mult))
                    dve.wait_ge(nd_io, 1)
                    step(dve.tensor_tensor(ta[:, :], col["end"][:, :], col["deg"][:, :], ALU.subtract))
                    step(dve.tensor_tensor(ta[:, :], ta[:, :], node_id[:, :], ALU.subtract))
                    step(dve.tensor_tensor(ta[:, :], ta[:, :], col["has"][:, :], ALU.mult))
                    step(dve.tensor_tensor(start_i[:, 0:NT], ta[:, :], node_id[:, :], ALU.add))
                    dve.wait_ge(nd_act, 1)
                    step(dve.tensor_scalar(ta[:, :], col["t0"][:, :], 1e-12, None, ALU.max))
                    step(dve.reciprocal(tb[:, :], ta[:, :]))
                    step(dve.scalar_tensor_tensor(col["att"][:, :], tb[:, :], AVG_D_LOG, col["has"][:, :],
                                                  ALU.mult, ALU.mult))
                    step(dve.tensor_scalar(col["amp"][:, :], col["t0"][:, :], 1.0 / AVG_D_LOG, None, ALU.mult))

                @block.tensor
                def _(pe):
                    pe.wait_ge(nd, 2)
                    for b in range(2):
                        first = 1 if b == 0 else 0
                        pe.matmul(bank[2 + b][:, 0:KH].rearrange("p (a r) -> p a r", r=REL), shift[:, :],
                                  run_sums[:, b * half:b * half + half, :], start=True, stop=False)
                        mm = pe.matmul(bank[2 + b][:, first * REL:KH].rearrange("p (a r) -> p a r", r=REL),
                                       wrap[:, :], run_sums[:, b * half + first - 1:b * half + half - 1, :],
                                       start=False, stop=True)
                    mm.then_inc(nd_pe, 1)
                    for b in range(2):
                        pe.wait_ge(nd, b + 3)
                        pe.matmul(bank[4 + b][:, 0:KH], steps_to_counts[:, :], steps[:, b * KH:b * KH + KH],
                                  start=True, stop=True).then_inc(nd_pe, 1)

                @block.scalar
                def _(act):
                    act.wait_ge(nd, 7)
                    act.activation(col["t0"][:, :], col["deg"][:, :], ACT.Ln, bias=1.0).then_inc(nd_act, 1)

        def fetch(pool, table, limit, win, R, win_ready, fetched):
            def one(j, q):
                pool.wait_ge(win_ready, j * 2 + q + 1)
                pool.sem_inc(pool_passed, 1)
                for k in range(CH):
                    pool.indirect_dma_start(R[:, q, k, :], None, table,
                                            bass.IndirectOffsetOnAxis(win[:, q, k:k + 1], 0),
                                            bounds_check=limit, oob_is_err=True).then_inc(fetched[q], 16)
            chunks(pool, one)

        def window(eng, win, index, j, q, win_ready):
            eng.tensor_copy(win[:, q, :], index[:, bass.ds((j * 2 + q) * CH, CH)]).then_inc(win_ready, 1)

        ln_v, ln_a, ln_neg, ln_out, ln_neg_out = sem("ln_v"), sem("ln_a"), sem("ln_neg"), sem("ln_out"), sem("ln_no")
        ln_steps = 12
        tables_out = [0]

        def norm(i, table, negative=False, await_table=True, on_pool=None, on_sync=None):
            v, a, v0, a0 = ln_v, ln_a, i * ln_steps, i * 4
            n = [v0]
            parts = (slice(0, NT // 2), slice(NT // 2, NT))

            def wide(c, h):
                return col[c][:, h].unsqueeze(2).broadcast_to([P, NT // 2, F])

            with nc.Block() as block:
                @block.vector
                def _(dve):
                    def step(ins):
                        ins.then_inc(v, 1)
                        n[0] += 1
                        dve.wait_ge(v, n[0])
                    for h in parts:
                        step(dve.tensor_reduce(col["t0"][:, h], X[:, h, :], AX.X, ALU.add))
                        step(dve.tensor_scalar(col["mean"][:, h], col["t0"][:, h], 1.0 / F, None, ALU.mult))
                        step(dve.tensor_tensor(H[:, h, :], X[:, h, :], wide("mean", h), ALU.subtract))
                    for k, h in enumerate(parts):
                        dve.wait_ge(a, a0 + k + 1)
                        step(dve.tensor_reduce(col["t0"][:, h], SQ[:, h, :], AX.X, ALU.add))
                    for k, h in enumerate(parts):
                        dve.wait_ge(a, a0 + k + 3)
                        step(dve.reciprocal(col["rstd"][:, h], col["t1"][:, h]))
                        step(dve.scalar_tensor_tensor(H[:, h, :], H[:, h, :], 0.0, wide("rstd", h), ALU.max,
                                                      ALU.mult))

                @block.scalar
                def _(act):
                    for k, h in enumerate(parts):
                        act.wait_ge(v, v0 + 3 * k + 3)
                        act.activation(SQ[:, h, :], H[:, h, :], ACT.Square).then_inc(a, 1)
                    for k, h in enumerate(parts):
                        act.wait_ge(v, v0 + 7 + k)
                        act.activation(col["t1"][:, h], col["t0"][:, h], ACT.Sqrt, bias=eps_c[:, :],
                                       scale=1.0 / F).then_inc(a, 1)
                    if negative:
                        for k, h in enumerate(parts):
                            act.wait_ge(v, v0 + 10 + 2 * k)
                            act.activation(Y[:, h, :], H[:, h, :], ACT.Copy, scale=-1.0).then_inc(ln_neg, 1)

                @block.sync
                def _(sp):
                    if table is not None:
                        tv = table.rearrange("(p a) f -> p a f", p=P)
                        for k, h in enumerate(parts):
                            sp.wait_ge(v, v0 + 10 + 2 * k)
                            sp.dma_start(tv[:, h, 0:F], H[:, h, :]).then_inc(ln_out, 16)
                        tables_out[0] += 1
                        if negative:
                            for k, h in enumerate(parts):
                                sp.wait_ge(ln_neg, k + 1)
                                sp.dma_start(tv[:, h, F:2 * F], Y[:, h, :]).then_inc(ln_neg_out, 16)
                            sp.wait_ge(ln_neg_out, 2 * 16)
                        if await_table:
                            sp.wait_ge(ln_out, tables_out[0] * 2 * 16)
                    if on_sync:
                        on_sync(sp)

                @block.gpsimd
                def _(pool):
                    if on_pool:
                        on_pool(pool)

        def relational():
            BY_ACT = REL
            hs_ready, split_w, w_in = sem("hs_ready"), sem("split_w"), sem("rel_w")
            hT_psum, hT_ready = sem("hT_psum"), sem("hT_ready")
            m_ready, p_dve, p_act, v, on = sem("m_ready"), sem("p_dve"), sem("p_act"), sem("rel_v"), sem("rel_on")
            summed = sem("rel_summed")
            with ExitStack() as st:
                def tmp(name, shape, dt=FP32):
                    return st.enter_context(nc.sbuf_tensor(unique(name), shape, dt))
                W = tmp("W", [P, 2 * REL * F])
                rest_w = tmp("rest_w", [P, 2 * REL * F])
                w_00, w_11, w_20 = (tmp(n, [P, 2 * REL * F], BF16) for n in ("w_00", "w_11", "w_20"))
                B = tmp("B", [P, 2 * REL * F])
                b_parts = tmp("b_parts", [P, 2 * REL * F], BF16)
                b_1 = tmp("b_1", [P, 2 * REL * F], BF16)
                ones_b = tmp("ones_b", [P, P], BF16)
                rest = tmp("rest", [P, F])
                hp = tmp("hp", [P, 2, 3, F], BF16)
                hT = tmp("hT", [P, 2, 2, P], BF16)
                prod = tmp("prod", [P, 2, 2 * REL, F])
                res = tmp("res", [P, 2, F])

                def tiles(eng, one):
                    for k in range(2):
                        one(k, k)
                    with eng.Fori(1, NT // 2) as i:
                        for k in range(2):
                            one(i * 2 + k, k)

                def ahead(eng, front, back):
                    front(0, 0)
                    for k in range(2):
                        front(k + 1, 1 - k)
                        back(k, k)
                    with eng.Fori(1, NT // 2 - 1) as i:
                        for k in range(2):
                            front(i * 2 + k + 1, 1 - k)
                            back(i * 2 + k, k)
                    front(NT - 1, 1)
                    back(NT - 2, 0)
                    back(NT - 1, 1)

                def load_weights(sp):
                    for h in range(2):
                        sp.dma_start(W[h * F:h * F + F, :], w0[0:F, :]).then_inc(w_in, 16)
                    sp.wait_ge(on, 1)
                    for row in (0, 32, 64):
                        sp.dma_start(B[row:row + 1, :], w0[F:F + 1, :]).then_inc(w_in, 16)

                def split_weights(pool):
                    n = [0]

                    def step(ins):
                        ins.then_inc(split_w, 1)
                        n[0] += 1
                        pool.wait_ge(split_w, n[0])

                    pool.memset(B[:, :], 0.0).then_inc(on, 1)
                    pool.memset(ones_b[:, :], 1.0).then_inc(on, 1)
                    pool.wait_ge(w_in, 5 * 16)
                    step(pool.tensor_copy(w_00[:, :], W[:, :]))
                    step(pool.tensor_tensor(rest_w[:, :], W[:, :], w_00[:, :], ALU.subtract))
                    step(pool.tensor_copy(w_11[:, :], rest_w[:, :]))
                    step(pool.tensor_tensor(w_20[0:F, :], rest_w[0:F, :], w_11[0:F, :], ALU.subtract))
                    step(pool.tensor_copy(w_20[F:P, :], w_00[F:P, :]))
                    step(pool.tensor_copy(b_parts[:, :], B[:, :]))
                    step(pool.tensor_tensor(rest_w[:, :], B[:, :], b_parts[:, :], ALU.subtract))
                    step(pool.tensor_copy(b_1[:, :], rest_w[:, :]))
                    step(pool.tensor_copy(b_parts[32:33, :], b_1[32:33, :]))
                    step(pool.tensor_tensor(b_parts[64:65, :], rest_w[64:65, :], b_1[64:65, :], ALU.subtract))

                norm(0, None, on_pool=split_weights, on_sync=load_weights)
                with nc.Block() as block:
                    @block.gpsimd
                    def _(pool):
                        def split(m, k):
                            h = H[:, bass.ds(m, 1), :]
                            h1, h0, h2 = (hp[:, k, q, :].unsqueeze(1) for q in range(3))
                            r = rest[:, :].unsqueeze(1)
                            wait(pool, hT_psum, m - 1)
                            pool.sem_inc(pool_passed, 1)
                            pool.tensor_copy(h0, h).then_inc(hs_ready, 1)
                            pool.wait_ge(hs_ready, m * 4 + 1)
                            pool.sem_inc(pool_passed, 1)
                            pool.tensor_tensor(r, h, h0, ALU.subtract).then_inc(hs_ready, 1)
                            pool.wait_ge(hs_ready, m * 4 + 2)
                            pool.sem_inc(pool_passed, 1)
                            pool.tensor_copy(h1, r).then_inc(hs_ready, 1)
                            pool.wait_ge(hs_ready, m * 4 + 3)
                            pool.tensor_tensor(h2, r, h1, ALU.subtract).then_inc(hs_ready, 1)
                            pool.wait_ge(hs_ready, m * 4 + 4)
                        tiles(pool, split)

                    @block.tensor
                    def _(pe):
                        pe.wait_ge(on, 2)
                        pe.wait_ge(split_w, 10)

                        def transpose(m, k):
                            pe.wait_ge(hs_ready, m * 4 + 4)
                            wait(pe, hT_ready, m - 1)
                            pe.sem_inc(pe_passed, 1)
                            for q in range(2):
                                mm = pe.matmul(bank[6 + k][:, q * P:q * P + P],
                                               hp[:, k, q:q + 2, :].rearrange("p q f -> p (q f)"), ident_b[:, :],
                                               start=True, stop=True)
                            mm.then_inc(hT_psum, 1)

                        def products(m, k):
                            pe.wait_ge(hT_ready, m + 1)
                            wait(pe, p_dve, m * 2 - 2)
                            wait(pe, p_act, (m - 1) * BY_ACT)
                            for c in range(3):
                                cols = slice(384 * c, 384 * c + 384)
                                terms = ((ones_b[:, :], b_parts), (hT[:, k, 0, :], w_00), (hT[:, k, 0, :], w_11),
                                         (hT[:, k, 1, :], w_20))
                                for q, (left, right) in enumerate(terms):
                                    mm = pe.matmul(bank[3 * k + c][:, 0:384], left, right[:, cols],
                                                   start=q == 0, stop=q == 3)
                                mm.then_inc(m_ready, 1)
                        ahead(pe, transpose, products)

                    @block.scalar
                    def _(act):
                        def evacuate(m, k):
                            act.wait_ge(hT_psum, m + 1)
                            wait(act, m_ready, m * 3 - 3)
                            act.activation(hT[:, k, :, :].rearrange("p q n -> p (q n)"), bank[6 + k][:, 0:2 * P],
                                           ACT.Copy).then_inc(hT_ready, 1)

                        def scale(m, k):
                            wait(act, summed, m - 1)
                            for r in range(REL, 2 * REL):
                                c, o = r // 6, (r % 6) * F
                                if r in (REL, 12):
                                    act.wait_ge(m_ready, m * 3 + c + 1)
                                act.activation(prod[:, k, r, :], bank[3 * k + c][:, o:o + F], ACT.Copy,
                                               scale=C[:, bass.ds(m, 1), r:r + 1].rearrange("p a r -> p (a r)")
                                               ).then_inc(p_act, 1)
                        ahead(act, evacuate, scale)

                    @block.vector
                    def _(dve):
                        def multiply(m, k):
                            for c, lo, hi in ((0, 0, 6), (1, 6, REL)):
                                dve.wait_ge(m_ready, m * 3 + c + 1)
                                if c == 1:
                                    dve.wait_ge(p_act, m * BY_ACT + 3)
                                dve.tensor_tensor(prod[:, k, lo:hi, :],
                                                  bank[3 * k + c][:, 0:(hi - lo) * F]
                                                  .rearrange("p (r f) -> p r f", f=F),
                                                  C[:, bass.ds(m, 1), lo:hi].rearrange("p a r -> p (a r)")
                                                  .unsqueeze(2).broadcast_to([P, hi - lo, F]), ALU.mult
                                                  ).then_inc(p_dve, 1)

                        def add_mean(m, k):
                            a = bass.ds(m, 1)
                            dve.wait_ge(summed, m + 1)
                            dve.scalar_tensor_tensor(X[:, a, :], res[:, k, :].unsqueeze(1), col["rcnt"][:, a],
                                                     X[:, a, :], ALU.mult, ALU.add).then_inc(v, 1)

                        def total(m, k):
                            dve.wait_ge(p_dve, m * 2 + 2)
                            dve.wait_ge(p_act, m * BY_ACT + BY_ACT)
                            wait(dve, v, m - 1)
                            dve.tensor_reduce(res[:, k, :], prod[:, k, :, :].rearrange("p r f -> p f r"), AX.X,
                                              ALU.add).then_inc(summed, 1)

                        multiply(0, 0)
                        total(0, 0)
                        multiply(1, 1)
                        add_mean(0, 0)
                        total(1, 1)
                        with dve.Fori(1, NT // 2) as i:
                            for k in range(2):
                                multiply(i * 2 + k, k)
                                add_mean(i * 2 + k - 1, 1 - k)
                                total(i * 2 + k, k)
                        add_mean(NT - 1, 1)

        def pna_edges():
            win_ready, gathered = sem("pe_win_ready"), sems("pe_gathered", PAR)
            t_done, d_done, gates_done = sem("pe_t_done"), sem("pe_d_done"), sem("pe_gates_done")
            s_done, o6_done, back_done = sem("pe_s_done"), sem("pe_o6_done"), sem("pe_back_done")
            w_act, w_dve, sent = sem("pe_w_act"), sem("pe_w_dve"), sems("pe_sent", 2)
            with ExitStack() as st:
                def tmp(name, shape, dt=FP32):
                    return st.enter_context(nc.sbuf_tensor(unique(name), shape, dt))
                win = tmp("win", [P, PAR, GRP], I32)
                G = tmp("G", [P, BODY, 2 * F])
                D = tmp("D", [P, 2, 2, GRP * P])
                S = tmp("S", [P, 2, 2, GRP * P])
                Wo = tmp("Wo", [P, 2, GRP, 4 * F])
                out_v = r1.rearrange("(t p) f -> p t f", p=P)
                with nc.Block() as block:
                    @block.gpsimd
                    def _(pool):
                        def gather(i, g):
                            n = i * PAR + g
                            pool.wait_ge(win_ready, n + 1)
                            wait(pool, t_done, n - PAR + 1)
                            pool.sem_inc(pool_passed, 1)
                            for k in range(GRP):
                                s = g * GRP + k
                                pool.indirect_dma_start(
                                    G[:, s, :], None, htab[0], bass.IndirectOffsetOnAxis(win[:, g, k:k + 1], 0),
                                    bounds_check=NPAD - 1, oob_is_err=True).then_inc(gathered[g], 16)
                        pipeline(pool, gather)

                    @block.tensor
                    def _(pe):
                        def front(i, g):
                            n, b = i * PAR + g, g % 2
                            wait(pe, d_done, n * 3 - 3)
                            pe.wait_ge(gathered[g], i * (GRP * 16) + GRP * 16)
                            for k in range(GRP):
                                s = g * GRP + k
                                tr = pe.transpose(bank[b][:, k * P:k * P + P], G[:, s, :], ident[:, :])
                            tr.then_inc(t_done, 1)
                            wait(pe, s_done, n * 2)
                            for base, gate in ((2, gate_sum), (4, gate_max)):
                                for k in range(GRP):
                                    mm = pe.matmul(bank[base + b][:, k * P:k * P + P],
                                                   gate[:, bass.ds(n * GRP + k, 1)].broadcast_to([P, P]),
                                                   ident_b[:, :], start=True, stop=True)
                            mm.then_inc(gates_done, 1)

                        def back(i, g):
                            n, b = i * PAR + g, g % 2
                            pe.wait_ge(s_done, n * 2 + 4)
                            for half, read, done in ((0, w_act, o6_done), (1, w_dve, back_done)):
                                wait(pe, read, n)
                                for k in range(2):
                                    for q in range(2):
                                        c, o = (half * 2 + k) * P, (k * 2 + q) * P
                                        tr = pe.transpose(bank[6 + half][:, o:o + P], S[:, b, q, c:c + P],
                                                          ident[:, :])
                                tr.then_inc(done, 1)
                        pipeline(pe, front, back)

                    @block.scalar
                    def _(act):
                        def operands(i, g):
                            n, b = i * PAR + g, g % 2
                            act.wait_ge(t_done, n + 1)
                            wait(act, s_done, n * 2)
                            act.activation(D[0:F, b, 0, :], bank[b][0:F, :], ACT.Copy).then_inc(d_done, 1)
                            act.activation(D[F:P, b, 0, :], bank[b][F:P, :], ACT.Square).then_inc(d_done, 1)
                            act.activation(D[:, b, 1, :], bank[b][:, :], ACT.Copy).then_inc(d_done, 1)

                        def evacuate(i, g):
                            n, b = i * PAR + g, g % 2
                            act.wait_ge(o6_done, n + 1)
                            wait(act, sent[b], (i * 2 + g // 2) * 16)
                            act.activation(Wo[:, b, 0:2, :].rearrange("p k f -> p (k f)"), bank[6][:, :], ACT.Copy
                                           ).then_inc(w_act, 1)
                        pipeline(act, operands, evacuate)

                    @block.vector
                    def _(dve):
                        dve.memset(S[:, 1, :, GRP * P - 1:GRP * P], 0.0).then_inc(s_done, 2)

                        def sources(n, g):
                            dve.tensor_copy(win[:, g, :], row_i[:, bass.ds(n * GRP, GRP)]).then_inc(win_ready, 1)

                        def scans(i, g):
                            n, b = i * PAR + g, g % 2
                            dve.wait_ge(gates_done, n + 1)
                            wait(dve, back_done, n - 1)
                            for q, base, op0, op1 in ((0, 2, ALU.mult, ALU.add), (1, 4, ALU.add, ALU.max)):
                                dve.wait_ge(d_done, n * 3 + 2 + q)
                                dve.wait_ge(s_done, n * 2 + 1 + q)
                                dve.tensor_tensor_scan(S[:, b, q, :], bank[base + b][:, :], D[:, b, q, :],
                                                       S[:, 1 - b, q, GRP * P - 1:GRP * P], op0, op1
                                                       ).then_inc(s_done, 1)
                            dve.wait_ge(gathered[g], i * (GRP * 16) + GRP * 16)
                            sources(n + PAR, g)

                        def evacuate(i, g):
                            n, b = i * PAR + g, g % 2
                            dve.wait_ge(back_done, n + 1)
                            wait(dve, sent[b], (i * 2 + g // 2) * 16)
                            dve.tensor_copy(Wo[:, b, 2:4, :].rearrange("p k f -> p (k f)"), bank[7][:, :]
                                            ).then_inc(w_dve, 1)

                        for g in range(PAR):
                            sources(g, g)
                        pipeline(dve, scans, evacuate)

                    @block.sync
                    def _(sp):
                        def store(i, g):
                            n, b = i * PAR + g, g % 2
                            sp.wait_ge(w_act, n + 1)
                            sp.wait_ge(w_dve, n + 1)
                            sp.dma_start(out_v[:, bass.ds(n * GRP, GRP), :], Wo[:, b, :, :]).then_inc(sent[b], 16)
                        pipeline(sp, store)
                        for b in range(2):
                            sp.wait_ge(sent[b], ITERS * PAR // 2 * 16)

        def pna_nodes():
            wl, win_ready, fetched = sem("pn_wl"), sem("pn_win"), sems("pn_fetched", 2)
            raw, ms_done, var_done, std_done, agg_done = (
                sem("pn_raw"), sem("pn_ms"), sem("pn_var"), sem("pn_std"), sem("pn_agg"))
            t_done, aT_done, y_done = sem("pn_t"), sem("pn_aT"), sem("pn_y")
            y_1, y_2, y_read = sem("pn_y1"), sem("pn_y2"), sem("pn_yread")
            residual = sem("pn_residual")
            y_bank = (2, 3, 6, 7)
            bn, bn_pe, bn_act = sem("pn_bn"), sem("pn_bn_pe"), sem("pn_bn_act")
            with ExitStack() as st:
                def tmp(name, shape, dt=FP32):
                    return st.enter_context(nc.sbuf_tensor(unique(name), shape, dt))
                win = tmp("win", [P, 2, CH], I32)
                R = tmp("R", [P, 2, CH, 4 * F])
                A = tmp("A", [P, 2, CH, 4 * F])
                ms = tmp("ms", [P, 2, CH, F])
                aT = tmp("aT", [P, 2, 2, P])
                W = tmp("W", [P, 2, 3 * F])
                bias = tmp("bias", [P, F])
                gamma = tmp("gamma", [P, F])
                beta = tmp("beta", [P, F])
                accs = tmp("accs", [P, 3, F])
                acc = tmp("acc", [P, F])
                mu = tmp("mu", [P, F])
                fac = tmp("fac", [P, F])
                fac2 = tmp("fac2", [P, F])

                def ahead(eng, fronts, backs):
                    def both(j, q, jb, qb):
                        for front, back in zip(fronts, backs):
                            front(j, q)
                            back(jb, qb)

                    for front in fronts:
                        front(0, 0)
                    both(0, 1, 0, 0)
                    with eng.Fori(1, NCH // 2) as j:
                        both(j, 0, j - 1, 1)
                        both(j, 1, j, 0)
                    for back in backs:
                        back(NCH // 2 - 1, 1)

                with nc.Block() as block:
                    @block.sync
                    def _(sp):
                        sp.dma_start(W[:, :, :], w1).then_inc(wl, 16)
                        sp.dma_start(bias[:, :], b1r).then_inc(wl, 16)
                        sp.dma_start(gamma[:, :], gam).then_inc(wl, 16)
                        sp.dma_start(beta[:, :], bet).then_inc(wl, 16)

                    @block.gpsimd
                    def _(pool):
                        fetch(pool, r1, EPAD - 1, win, R, win_ready, fetched)
                        pool.tensor_tensor(X[:, :, :], X[:, :, :], H[:, :, :], ALU.add).then_inc(residual, 1)

                    @block.vector
                    def _(dve):
                        dve.wait_ge(wl, 4 * 16)

                        def aggregate(j, q):
                            c = j * 2 + q
                            A_q, R_q = A[:, q], R[:, q]

                            def per_node(name):
                                return col[name][:, bass.ds(c * CH, CH)].unsqueeze(2).broadcast_to([P, CH, F])
                            dve.wait_ge(fetched[q], j * (CH * 16) + CH * 16)
                            wait(dve, t_done, (c - 1) * CH)
                            for at_a, at_r, name in ((0, 0, "rdeg"), (3, 1, "rdeg"), (1, 2, "has"), (2, 3, "neghas")):
                                dve.tensor_tensor(A_q[:, :, at_a * F:at_a * F + F], R_q[:, :, at_r * F:at_r * F + F],
                                                  per_node(name), ALU.mult).then_inc(raw, 1)
                            window(dve, win, end_i, j + 1, q, win_ready)

                        def variance(j, q):
                            c, std = j * 2 + q, A[:, q, :, 3 * F:4 * F]
                            dve.wait_ge(raw, c * 4 + 4)
                            dve.wait_ge(ms_done, c + 1)
                            dve.tensor_tensor(std, std, ms[:, q, :, :], ALU.subtract).then_inc(var_done, 1)
                            dve.wait_ge(var_done, c * 2 + 1)
                            dve.tensor_scalar(std, std, 0.0, None, ALU.max).then_inc(var_done, 1)

                        def deviation(j, q):
                            c, std = j * 2 + q, A[:, q, :, 3 * F:4 * F]
                            has = col["has"][:, bass.ds(c * CH, CH)].unsqueeze(2).broadcast_to([P, CH, F])
                            dve.wait_ge(std_done, c + 1)
                            dve.tensor_tensor(std, std, has, ALU.mult).then_inc(agg_done, 1)

                        def linear(steps):
                            def run(j, q):
                                c = j * 2 + q
                                for n in steps:
                                    if n < CH:
                                        m, a = c * CH + n, bass.ds(c * CH + n, 1)
                                        dve.wait_ge(y_done, m + 1)
                                        wait(dve, y_read, m - 2 if n >= 3 else c * CH)
                                        dve.scalar_tensor_tensor(accs[:, n % 3, :], bank[y_bank[n % 4]][:, F:2 * F],
                                                                 col["amp"][:, a], bias[:, :], ALU.mult, ALU.add
                                                                 ).then_inc(y_1, 1)
                                    if 1 <= n <= CH:
                                        k = n - 1
                                        m, a = c * CH + k, bass.ds(c * CH + k, 1)
                                        dve.wait_ge(y_1, m + 1)
                                        dve.scalar_tensor_tensor(accs[:, k % 3, :],
                                                                 bank[y_bank[k % 4]][:, 2 * F:3 * F],
                                                                 col["att"][:, a], accs[:, k % 3, :],
                                                                 ALU.mult, ALU.add).then_inc(y_2, 1)
                                    if 2 <= n:
                                        k = n - 2
                                        m, a = c * CH + k, bass.ds(c * CH + k, 1)
                                        dve.wait_ge(y_2, m + 1)
                                        dve.tensor_tensor(Y[:, a, :], accs[:, k % 3, :].unsqueeze(1),
                                                          bank[y_bank[k % 4]][:, 0:F].unsqueeze(1), ALU.add
                                                          ).then_inc(y_read, 1)
                            return run

                        for q in range(2):
                            window(dve, win, end_i, 0, q, win_ready)
                        ahead(dve, (aggregate, variance, deviation),
                              (linear(range(0, 2)), linear(range(2, 6)), linear(range(6, CH + 2))))

                        n = [0]

                        def step(ins):
                            ins.then_inc(bn, 1)
                            n[0] += 1
                            dve.wait_ge(bn, n[0])

                        def all_nodes(t):
                            return t[:, :].unsqueeze(1).broadcast_to([P, NT, F])

                        dve.wait_ge(y_read, NT)
                        step(dve.tensor_scalar(Y[:, NT - 1, :], Y[:, NT - 1, :], real[:, :], None, ALU.mult))
                        step(dve.tensor_reduce(acc[:, :], Y[:, :, :].rearrange("p a f -> p f a"), AX.X, ALU.add))
                        dve.wait_ge(bn_pe, 1)
                        step(dve.tensor_scalar(mu[:, :], bank[4][:, 0:F], 1.0 / NODES, None, ALU.mult))
                        step(dve.tensor_tensor(Y[:, :, :], Y[:, :, :], all_nodes(mu), ALU.subtract))
                        step(dve.tensor_scalar(Y[:, NT - 1, :], Y[:, NT - 1, :], real[:, :], None, ALU.mult))
                        dve.wait_ge(bn_act, 1)
                        step(dve.tensor_reduce(acc[:, :], SQ.rearrange("p a f -> p f a"), AX.X, ALU.add))
                        dve.wait_ge(bn_act, 2)
                        step(dve.reciprocal(fac2[:, :], fac[:, :]))
                        step(dve.tensor_tensor(fac2[:, :], fac2[:, :], gamma[:, :], ALU.mult))
                        step(dve.tensor_tensor(Y[:, :, :], Y[:, :, :], all_nodes(fac2), ALU.mult))
                        step(dve.tensor_tensor(Y[:, :, :], Y[:, :, :], all_nodes(beta), ALU.add))
                        dve.wait_ge(residual, 1)
                        step(dve.scalar_tensor_tensor(X[:, :, :], Y[:, :, :], 0.0, X[:, :, :], ALU.max, ALU.add))

                    @block.tensor
                    def _(pe):
                        pe.wait_ge(wl, 4 * 16)

                        def one(j, q):
                            c = j * 2 + q

                            def transpose(k):
                                m, b = c * CH + k, (q * CH + k) % 2
                                wait(pe, aT_done, m - 1)
                                pe.transpose(bank[b][:, 0:P], A[:, q, k, 0:P], ident[:, :])
                                pe.transpose(bank[b][:, P:2 * P], A[:, q, k, P:2 * P], ident[:, :]
                                             ).then_inc(t_done, 1)

                            def product(k):
                                m, b = c * CH + k, (q * CH + k) % 2
                                pe.wait_ge(aT_done, m + 1)
                                wait(pe, y_read, m - (3 if k >= 4 else 2 if k < 3 else 6))
                                for h in range(2):
                                    mm = pe.matmul(bank[y_bank[k % 4]][:, 0:3 * F], aT[:, b, h, :], W[:, h, :],
                                                   start=h == 0, stop=h == 1)
                                mm.then_inc(y_done, 1)

                            pe.wait_ge(agg_done, c + 1)
                            transpose(0)
                            for k in range(CH):
                                if k + 1 < CH:
                                    transpose(k + 1)
                                product(k)
                        chunks(pe, one)
                        pe.wait_ge(bn, 2)
                        pe.matmul(bank[4][:, 0:F], ones[:, :], acc[:, :], start=True, stop=True).then_inc(bn_pe, 1)
                        pe.wait_ge(bn, 6)
                        pe.matmul(bank[5][:, 0:F], ones[:, :], acc[:, :], start=True, stop=True).then_inc(bn_pe, 1)

                    @block.scalar
                    def _(act):
                        def squares(j, q):
                            c = j * 2 + q
                            act.wait_ge(raw, c * 4 + 1)
                            wait(act, var_done, (c - 1) * 2)
                            act.activation(ms[:, q, :, :], A[:, q, :, 0:F], ACT.Square).then_inc(ms_done, 1)

                        def roots(j, q):
                            c = j * 2 + q
                            act.wait_ge(var_done, c * 2 + 2)
                            act.activation(A[:, q, :, 3 * F:4 * F], A[:, q, :, 3 * F:4 * F], ACT.Sqrt,
                                           bias=eps_c[:, :]).then_inc(std_done, 1)

                        def evacuate(tiles):
                            def run(j, q):
                                for k in tiles:
                                    m, b = (j * 2 + q) * CH + k, (q * CH + k) % 2
                                    act.wait_ge(t_done, m + 1)
                                    wait(act, y_done, m - 1)
                                    act.activation(aT[:, b, :, :].rearrange("p h n -> p (h n)"),
                                                   bank[b][:, 0:2 * P], ACT.Copy).then_inc(aT_done, 1)
                            return run
                        ahead(act, (squares, roots), (evacuate(range(0, 4)), evacuate(range(4, CH))))
                        act.wait_ge(bn, 5)
                        act.activation(SQ, Y[:, :, :], ACT.Square).then_inc(bn_act, 1)
                        act.wait_ge(bn_pe, 2)
                        act.activation(fac[:, :], bank[5][:, 0:F], ACT.Sqrt, bias=eps_c[:, :],
                                       scale=1.0 / NODES).then_inc(bn_act, 1)

        def place_first_rows():
            ready, placed = sem("fr_ready"), sems("fr_placed", 2)
            hd, hd_out = sem("fr_heads"), sems("fr_hout", 2)
            with ExitStack() as st:
                def tmp(name, shape, dt=FP32):
                    return st.enter_context(nc.sbuf_tensor(unique(name), shape, dt))
                win = tmp("win", [P, 2, CH], I32)
                Hw = tmp("Hw", [P, 2, CH, F])
                head = tmp("head", [P, 13, F])
                with nc.Block() as block:
                    @block.vector
                    def _(dve):
                        def one(j, q):
                            c = j * 2 + q
                            wait(dve, placed[q], j * (CH * 16))
                            window(dve, win, start_i, j, q, ready)
                            dve.tensor_copy(Hw[:, q, :, :], H[:, bass.ds(c * CH, CH), :]).then_inc(ready, 1)
                        chunks(dve, one)

                    @block.gpsimd
                    def _(pool):
                        def one(j, q):
                            pool.wait_ge(ready, (j * 2 + q) * 2 + 2)
                            pool.sem_inc(pool_passed, 1)
                            for k in range(CH):
                                pool.indirect_dma_start(first_rows, bass.IndirectOffsetOnAxis(win[:, q, k:k + 1], 0),
                                                        Hw[:, q, k, :], None, bounds_check=E_ROWS - 1,
                                                        oob_is_err=True).then_inc(placed[q], 16)
                        one(0, 0)
                        one(0, 1)
                        pool.wait_ge(ln_out, tables_out[0] * 2 * 16)
                        for j in range(13):
                            pool.indirect_dma_start(head[:, j, :], None, htab[1],
                                                    bass.IndirectOffsetOnAxis(heads_i[:, j:j + 1], 0),
                                                    bounds_check=NPAD - 1, oob_is_err=True).then_inc(hd, 16)
                        with pool.Fori(1, NCH // 2) as j:
                            for q in range(2):
                                one(j, q)

                    @block.sync
                    def _(sp):
                        sp.wait_ge(hd, 13 * 16)
                        for q in range(2):
                            sp.wait_ge(placed[q], NT // 2 * 16)
                        v = first_rows[0:12 * P * P, :].rearrange("(j p n) f -> p j n f", j=12, p=P)
                        sp.dma_start(v[:, :, 0, :], head[:, 0:12, :]).then_inc(hd_out[0], 16)
                        v = first_rows[12 * P * P:EPAD, :].rearrange("(p n) f -> p n f", n=P)
                        sp.dma_start(v[:, 0, :], head[0:TILES - 12 * P, 12, :]).then_inc(hd_out[1], 16)
                        sp.wait_ge(hd_out[0], 16)
                        sp.wait_ge(hd_out[1], 16)

        def sum_edges():
            loaded, rows_done, eq_done, idx_done = sems("se_loaded", 2), sem("se_rows"), sem("se_eq"), sem("se_idx")
            x_done, xs_done, tot_done, m_done = sem("se_x"), sem("se_xs"), sem("se_tot"), sem("se_m")
            added, own, dif_done = sems("se_added", BODY), sem("se_own"), sem("se_dif")
            with ExitStack() as st:
                def tmp(name, shape, dt=FP32):
                    return st.enter_context(nc.sbuf_tensor(unique(name), shape, dt))
                Er = tmp("Er", [P, 2, GRP, F])
                eq_dst = tmp("eq_dst", [P, 2, GRP, P])
                eq_src = tmp("eq_src", [P, 2, GRP, P])
                earlier = tmp("earlier", [P, GRP, P])
                n_earlier = tmp("n_earlier", [P, GRP])
                shifts = tmp("shifts", [P, GRP])
                to_spare = tmp("to_spare", [P, TILES])
                idx = tmp("idx", [P, PAR, GRP], I32)
                Xs = tmp("Xs", [P, 2, GRP, F])
                M = tmp("M", [P, PAR, GRP, F])
                in_v = first_rows[0:EPAD, :].rearrange("(t p) f -> p t f", p=P)
                with nc.Block() as block:
                    @block.sync
                    def _(sp):
                        def load(i, g):
                            n, b = i * PAR + g, g % 2
                            wait(sp, x_done, n - 1)
                            sp.dma_start(Er[:, b, :, :], in_v[:, bass.ds(n * GRP, GRP), :]).then_inc(loaded[b], 16)
                        pipeline(sp, load)

                    @block.tensor
                    def _(pe):
                        def rows(i, g):
                            n, b = i * PAR + g, g % 2
                            wait(pe, eq_done, n * 2 - 2)
                            for base, parts in ((0, (dst_hi, dst_lo)), (2, (src_hi, src_lo))):
                                for k in range(GRP):
                                    for q in range(2):
                                        mm = pe.matmul(bank[base + b][:, k * P:k * P + P],
                                                       parts[q][:, bass.ds(n * GRP + k, 1)].broadcast_to([P, P]),
                                                       ident_b[:, :], start=q == 0, stop=q == 1)
                            mm.then_inc(rows_done, 1)

                        def expand(i, g):
                            n, b = i * PAR + g, g % 2
                            pe.wait_ge(loaded[b], (i * 2 + g // 2) * 16 + 16)
                            pe.wait_ge(eq_done, n * 2 + 1)
                            wait(pe, xs_done, n - 1)
                            for k in range(GRP):
                                mm = pe.matmul(bank[4 + b][:, k * F:k * F + F], eq_dst[:, b, k, :],
                                               Er[:, b, k, :], start=True, stop=True)
                            mm.then_inc(x_done, 1)

                        def total(i, g):
                            n, b = i * PAR + g, g % 2
                            pe.wait_ge(eq_done, n * 2 + 2)
                            pe.wait_ge(xs_done, n + 1)
                            wait(pe, m_done, n - 1)
                            for k in range(GRP):
                                mm = pe.matmul(bank[6 + b][:, k * F:k * F + F], eq_src[:, b, k, :],
                                               Xs[:, b, k, :], start=True, stop=True)
                            mm.then_inc(tot_done, 1)
                        pipeline(pe, rows, expand, total)

                    @block.vector
                    def _(dve):
                        dve.tensor_scalar(to_spare[:, :], row_f[:, :], -1.0, spare_row[:, :], ALU.mult, ALU.add
                                          ).then_inc(dif_done, 1)
                        dve.wait_ge(dif_done, 1)

                        def compare(i, g):
                            n, b = i * PAR + g, g % 2
                            t = bass.ds(n * GRP, GRP)
                            dve.wait_ge(rows_done, n + 1)
                            for q, (eq, ids, used) in enumerate(((eq_dst, dst_f, x_done), (eq_src, src_f, tot_done))):
                                wait(dve, used, n - 1)
                                dve.tensor_tensor(eq[:, b, :, :],
                                                  bank[2 * q + b][:, :].rearrange("p (k e) -> p k e", k=GRP),
                                                  ids[:, t].unsqueeze(2).broadcast_to([P, GRP, P]),
                                                  ALU.is_equal).then_inc(eq_done, 1)
                            dve.wait_ge(eq_done, n * 2 + 2)
                            wait(dve, own, n * 3)
                            dve.tensor_tensor(earlier[:, :, :], eq_src[:, b, :, :],
                                              before[:, :].unsqueeze(1).broadcast_to([P, GRP, P]),
                                              ALU.mult).then_inc(own, 1)
                            dve.wait_ge(own, n * 3 + 1)
                            dve.tensor_reduce(n_earlier[:, :], earlier[:, :, :], AX.X, ALU.add).then_inc(own, 1)
                            dve.wait_ge(own, n * 3 + 2)
                            wait(dve, idx_done, n)
                            dve.scalar_tensor_tensor(shifts[:, :], n_earlier[:, :], 0.0, to_spare[:, t],
                                                     ALU.is_gt, ALU.mult).then_inc(own, 1)
                            dve.wait_ge(own, n * 3 + 3)
                            for k in range(GRP):
                                wait(dve, added[g * GRP + k], i * 16)
                            dve.tensor_tensor(idx[:, g, :], shifts[:, :], row_f[:, t], ALU.add
                                              ).then_inc(idx_done, 1)
                        pipeline(dve, compare)

                    @block.scalar
                    def _(act):
                        def expanded(i, g):
                            n, b = i * PAR + g, g % 2
                            act.wait_ge(x_done, n + 1)
                            wait(act, tot_done, n - 1)
                            act.activation(Xs[:, b, :, :].rearrange("p k f -> p (k f)"), bank[4 + b][:, 0:GRP * F],
                                           ACT.Copy).then_inc(xs_done, 1)

                        def message(i, g):
                            n, b = i * PAR + g, g % 2
                            act.wait_ge(tot_done, n + 1)
                            for k in range(GRP):
                                wait(act, added[g * GRP + k], i * 16)
                            act.activation(M[:, g, :, :].rearrange("p k f -> p (k f)"), bank[6 + b][:, 0:GRP * F],
                                           ACT.Copy).then_inc(m_done, 1)
                        pipeline(act, expanded, message)

                    @block.gpsimd
                    def _(pool):
                        def add(i, g):
                            n, b = i * PAR + g, g % 2
                            pool.wait_ge(m_done, n + 1)
                            pool.wait_ge(idx_done, n + 1)
                            for k in range(GRP):
                                if g < 2:
                                    wait(pool, added[(g + 2) * GRP + k], i * 16)
                                else:
                                    wait(pool, added[(g - 2) * GRP + k], i * 16 + 16)
                                pool.sem_inc(pool_passed, 1)
                                pool.indirect_dma_start(rep[b * GRP + k],
                                                        bass.IndirectOffsetOnAxis(idx[:, g, k:k + 1], 0),
                                                        M[:, g, k, :], None, bounds_check=REP_ROWS - 1,
                                                        oob_is_err=True, compute_op=ALU.add
                                                        ).then_inc(added[g * GRP + k], 16)
                        pipeline(pool, add)
                        for s in added:
                            pool.wait_ge(s, ITERS * 16)

        def add_tables():
            ld, v = sems("at_ld", REPS), sem("at_v")
            bufs = (SQ, H, Y)
            with nc.Block() as block:
                @block.sync
                def _(sp):
                    for k in range(REPS):
                        wait(sp, v, k - 2)
                        sp.dma_start(bufs[k % 3], rep[k][0:NPAD, :].rearrange("(p a) f -> p a f", p=P)
                                     ).then_inc(ld[k], 16)

                @block.vector
                def _(dve):
                    for k in range(REPS):
                        dve.wait_ge(ld[k], 16)
                        wait(dve, v, k)
                        dve.tensor_tensor(X[:, :, :], X[:, :, :], bufs[k % 3], ALU.add).then_inc(v, 1)

        def gine_edges():
            wl, win_ready, gathered, attr_in = (
                sem("ge_wl"), sem("ge_win"), sems("ge_gathered", PAR), sems("ge_attr", 2))
            t_done, d_done, gates_done, s_done = sem("ge_t"), sem("ge_d"), sem("ge_gates"), sem("ge_s")
            back_done, w_done, sent = sem("ge_back"), sem("ge_w"), sems("ge_sent", 2)
            with ExitStack() as st:
                def tmp(name, shape, dt=FP32):
                    return st.enter_context(nc.sbuf_tensor(unique(name), shape, dt))
                win = tmp("win", [P, PAR, GRP], I32)
                G = tmp("G", [P, BODY, F])
                attr = tmp("attr", [EDGE_F, 2, GRP * P])
                We = tmp("We", [EDGE_F, F])
                be = tmp("be", [F, 1])
                D = tmp("D", [F, 2, GRP * P])
                S = tmp("S", [F, 2, GRP * P])
                Wo = tmp("Wo", [P, 2, GRP, F])
                out_v = r3.rearrange("(t p) f -> p t f", p=P)
                with nc.Block() as block:
                    @block.gpsimd
                    def _(pool):
                        def gather(i, g):
                            n = i * PAR + g
                            pool.wait_ge(win_ready, n + 1)
                            wait(pool, t_done, n - PAR + 1)
                            pool.sem_inc(pool_passed, 1)
                            for k in range(GRP):
                                s = g * GRP + k
                                pool.indirect_dma_start(
                                    G[:, s, :], None, htab[2], bass.IndirectOffsetOnAxis(win[:, g, k:k + 1], 0),
                                    bounds_check=NPAD - 1, oob_is_err=True).then_inc(gathered[g], 16)
                        pipeline(pool, gather)

                    @block.tensor
                    def _(pe):
                        pe.wait_ge(wl, 2 * 16)

                        def front(i, g):
                            n, b = i * PAR + g, g % 2
                            wait(pe, d_done, n - 1)
                            pe.wait_ge(attr_in[b], (i * 2 + g // 2) * 16 + 16)
                            pe.matmul(bank[b][0:F, :], We[:, :], attr[:, b, :], start=True, stop=False)
                            pe.wait_ge(gathered[g], i * (GRP * 16) + GRP * 16)
                            for k in range(GRP):
                                s = g * GRP + k
                                mm = pe.matmul(bank[b][0:F, k * P:k * P + P], G[:, s, :], ident[:, :],
                                               start=False, stop=k == GRP - 1)
                            mm.then_inc(t_done, 1)
                            wait(pe, s_done, n)
                            for k in range(GRP):
                                mm = pe.matmul(bank[2 + b][0:F, k * P:k * P + P],
                                               gate_sum[:, bass.ds(n * GRP + k, 1)].broadcast_to([P, F]),
                                               ident_b[:, :], start=True, stop=True)
                            mm.then_inc(gates_done, 1)

                        def back(i, g):
                            n, b = i * PAR + g, g % 2
                            pe.wait_ge(s_done, n + 2)
                            wait(pe, w_done, n - 1)
                            pe.sem_inc(pe_passed, 1)
                            for k in range(GRP):
                                tr = pe.transpose(bank[4 + b][:, k * F:k * F + F], S[:, b, k * P:k * P + P],
                                                  ident[0:F, 0:F])
                            tr.then_inc(back_done, 1)
                        pipeline(pe, front, back)

                    @block.scalar
                    def _(act):
                        act.wait_ge(wl, 2 * 16)

                        def message(i, g):
                            n, b = i * PAR + g, g % 2
                            act.wait_ge(t_done, n + 1)
                            wait(act, s_done, n)
                            act.activation(D[:, b, :], bank[b][0:F, :], ACT.Relu, bias=be[:, :]).then_inc(d_done, 1)

                        def evacuate(i, g):
                            n, b = i * PAR + g, g % 2
                            act.wait_ge(back_done, n + 1)
                            wait(act, sent[b], (i * 2 + g // 2) * 16)
                            act.activation(Wo[:, b, :, :].rearrange("p k f -> p (k f)"), bank[4 + b][:, 0:GRP * F],
                                           ACT.Copy).then_inc(w_done, 1)
                        pipeline(act, message, evacuate)

                    @block.vector
                    def _(dve):
                        dve.memset(S[:, 1, GRP * P - 1:GRP * P], 0.0).then_inc(s_done, 1)

                        def sources(n, g):
                            dve.tensor_copy(win[:, g, :], row_i[:, bass.ds(n * GRP, GRP)]).then_inc(win_ready, 1)

                        def scan(i, g):
                            n, b = i * PAR + g, g % 2
                            dve.wait_ge(gates_done, n + 1)
                            dve.wait_ge(d_done, n + 1)
                            wait(dve, back_done, n - 1)
                            dve.wait_ge(s_done, n + 1)
                            dve.tensor_tensor_scan(S[:, b, :], bank[2 + b][0:F, :], D[:, b, :],
                                                   S[:, 1 - b, GRP * P - 1:GRP * P], ALU.mult, ALU.add
                                                   ).then_inc(s_done, 1)
                            dve.wait_ge(gathered[g], i * (GRP * 16) + GRP * 16)
                            sources(n + PAR, g)

                        for g in range(PAR):
                            sources(g, g)
                        pipeline(dve, scan)

                    @block.sync
                    def _(sp):
                        sp.dma_start(We[:, :], weT).then_inc(wl, 16)
                        sp.dma_start(be[:, :], bec).then_inc(wl, 16)

                        def load(i, g):
                            n, b = i * PAR + g, g % 2
                            wait(sp, t_done, n - 1)
                            sp.dma_start(attr[:, b, :], attrT[:, bass.ds(n * GRP * P, GRP * P)]
                                         ).then_inc(attr_in[b], 16)

                        def nothing(i, g):
                            pass

                        def store(i, g):
                            n, b = i * PAR + g, g % 2
                            sp.wait_ge(w_done, n + 1)
                            sp.dma_start(out_v[:, bass.ds(n * GRP, GRP), :], Wo[:, b, :, :]).then_inc(sent[b], 16)
                        pipeline(sp, load, nothing, store)
                        for b in range(2):
                            sp.wait_ge(sent[b], ITERS * PAR // 2 * 16)

        def gine_nodes():
            wl, win_ready, fetched, u = sem("gn_wl"), sem("gn_win"), sems("gn_fetched", 2), sem("gn_u")
            t_done, aT_done, h_done, hid_done, o_done, x_done, b2_done = (
                sem("gn_t"), sem("gn_aT"), sem("gn_h"), sem("gn_hid"), sem("gn_o"), sem("gn_x"), sem("gn_b2"))
            sets = ((0, 4), (4, 3))
            with ExitStack() as st:
                def tmp(name, shape, dt=FP32):
                    return st.enter_context(nc.sbuf_tensor(unique(name), shape, dt))
                win = tmp("win", [P, 2, CH], I32)
                R = tmp("R", [P, 2, CH, F])
                U = tmp("U", [P, 2, CH, F])
                aT = tmp("aT", [F, 2, 4 * P])
                hid = tmp("hid", [F, 2, 4 * P])
                W1 = tmp("W1", [F, F])
                W2 = tmp("W2", [F, F])
                b1 = tmp("b1", [F, 1])
                b2 = tmp("b2", [P, F])
                with nc.Block() as block:
                    @block.sync
                    def _(sp):
                        for t, d in ((W1, g1T), (W2, g2T), (b1, g1b), (b2, g2b)):
                            sp.dma_start(t[:, :], d).then_inc(wl, 16)

                    @block.gpsimd
                    def _(pool):
                        fetch(pool, r3, EPAD - 1, win, R, win_ready, fetched)

                    @block.vector
                    def _(dve):
                        def inputs(j, q):
                            c = j * 2 + q
                            nodes = bass.ds(c * CH, CH)
                            dve.wait_ge(fetched[q], j * (CH * 16) + CH * 16)
                            wait(dve, t_done, c * 2 - 2)
                            dve.tensor_tensor(U[:, q, :, :], R[:, q, :, :],
                                              col["has"][:, nodes].unsqueeze(2).broadcast_to([P, CH, F]), ALU.mult
                                              ).then_inc(u, 1)
                            window(dve, win, end_i, j + 1, q, win_ready)
                            dve.wait_ge(u, c * 2 + 1)
                            dve.tensor_tensor(U[:, q, :, :], U[:, q, :, :], H[:, nodes, :], ALU.add).then_inc(u, 1)

                        def outputs(j, q):
                            c = j * 2 + q
                            for h, (first, count) in enumerate(sets):
                                a = bass.ds(c * CH + first, count)
                                dve.wait_ge(o_done, c * 2 + h + 1)
                                dve.tensor_tensor(X[:, a, :], X[:, a, :],
                                                  bank[4 + h][:, 0:count * F].rearrange("p (k f) -> p k f", f=F),
                                                  ALU.add).then_inc(x_done, 1)

                        for q in range(2):
                            window(dve, win, end_i, 0, q, win_ready)
                        dve.wait_ge(wl, 4 * 16)
                        dve.tensor_tensor(X[:, :, :], X[:, :, :], b2[:, :].unsqueeze(1).broadcast_to([P, NT, F]),
                                          ALU.add).then_inc(b2_done, 1)
                        dve.wait_ge(b2_done, 1)
                        inputs(0, 0)
                        inputs(0, 1)
                        outputs(0, 0)
                        with dve.Fori(1, NCH // 2) as j:
                            inputs(j, 0)
                            outputs(j - 1, 1)
                            inputs(j, 1)
                            outputs(j, 0)
                        outputs(NCH // 2 - 1, 1)

                    @block.tensor
                    def _(pe):
                        pe.wait_ge(wl, 4 * 16)

                        def one(j, q):
                            c = j * 2 + q
                            pe.wait_ge(u, c * 2 + 2)
                            for h, (first, count) in enumerate(sets):
                                wait(pe, aT_done, c * 2 + h - 1)
                                pe.sem_inc(pe_passed, 1)
                                for k in range(count):
                                    tr = pe.transpose(bank[h][0:F, k * P:k * P + P], U[:, q, first + k, :],
                                                      ident[:, :])
                                tr.then_inc(t_done, 1)
                            for h, (first, count) in enumerate(sets):
                                pe.wait_ge(aT_done, c * 2 + h + 1)
                                wait(pe, hid_done, c * 2 + h - 1)
                                pe.sem_inc(pe_passed, 1)
                                pe.matmul(bank[2 + h][0:F, 0:count * P], W1[:, :], aT[:, h, 0:count * P],
                                          start=True, stop=True).then_inc(h_done, 1)
                            for h, (first, count) in enumerate(sets):
                                pe.wait_ge(hid_done, c * 2 + h + 1)
                                wait(pe, x_done, c * 2 + h - 1)
                                for k in range(count):
                                    mm = pe.matmul(bank[4 + h][:, k * F:k * F + F], hid[:, h, k * P:k * P + P],
                                                   W2[:, :], start=True, stop=True)
                                mm.then_inc(o_done, 1)
                        chunks(pe, one)

                    @block.scalar
                    def _(act):
                        act.wait_ge(wl, 4 * 16)

                        def one(j, q):
                            c = j * 2 + q
                            for h, (first, count) in enumerate(sets):
                                act.wait_ge(t_done, c * 2 + h + 1)
                                wait(act, h_done, c * 2 + h - 1)
                                act.activation(aT[:, h, 0:count * P], bank[h][0:F, 0:count * P], ACT.Copy
                                               ).then_inc(aT_done, 1)
                            for h, (first, count) in enumerate(sets):
                                act.wait_ge(h_done, c * 2 + h + 1)
                                wait(act, o_done, c * 2 + h - 1)
                                act.activation(hid[:, h, 0:count * P], bank[2 + h][0:F, 0:count * P], ACT.Relu,
                                               bias=b1[:, :]).then_inc(hid_done, 1)
                        chunks(act, one)

        relational()
        norm(1, htab[0], negative=True)
        pna_edges()
        pna_nodes()
        norm(2, htab[1], await_table=False)
        place_first_rows()
        sum_edges()
        add_tables()
        norm(3, htab[2])
        gine_edges()
        gine_nodes()

        stored = sem("stored")
        with nc.Block() as block:
            @block.sync
            def _(sp):
                sp.dma_start(out, X[:, :, :]).then_inc(stored, 16)
                sp.wait_ge(stored, 16)


def kernel(x, src, dst, edge_attr_32, edge_type_9, L0_gnn_weights, L0_gnn_biases, L1_gnn_W, L1_gnn_b,
           L1_gnn_gamma, L1_gnn_beta, L3_gnn_We, L3_gnn_be, L3_gnn_W1, L3_gnn_b1, L3_gnn_W2, L3_gnn_b2):
    import numpy as np
    import concourse.bacc as bacc
    from concourse.bass_utils import run_bass_kernel_spmd

    def edges(a, fill):
        a = np.asarray(a)
        a = np.concatenate([a, np.full(EPAD - EDGES, fill, a.dtype)])
        return a.reshape(TILES, P).T

    dst = np.asarray(dst)
    type_flat = np.concatenate([np.asarray(edge_type_9), np.zeros(EPAD - EDGES, np.int32)])
    dst_flat = np.concatenate([dst, np.full(EPAD - EDGES, LAST, dst.dtype)])
    head = np.concatenate([dst_flat[::P], np.full(13 * P - TILES, LAST, dst.dtype)]).reshape(13, P).T
    before = np.concatenate([np.full(1, -1, dst.dtype), dst_flat[:-1]])
    x_pad = np.concatenate([np.asarray(x), np.zeros((NPAD - NODES, F), np.float32)])
    attr = np.concatenate([np.asarray(edge_attr_32), np.zeros((EPAD - EDGES, EDGE_F), np.float32)])
    w0 = np.asarray(L0_gnn_weights)[2].transpose(1, 0, 2).reshape(F, 2 * REL * F)
    b0 = np.asarray(L0_gnn_biases)[2].reshape(1, 2 * REL * F)
    w1 = np.asarray(L1_gnn_W).reshape(3, 2, P, F).transpose(2, 1, 0, 3).reshape(P, 2, 3 * F)

    def rows(v):
        return np.broadcast_to(np.asarray(v).reshape(1, F), (P, F))

    arrays = {
        "x3": x_pad.reshape(NT, P, F).transpose(1, 0, 2),
        "srcT": edges(src, LAST), "dstT": edges(dst, LAST), "dstprevT": before.reshape(TILES, P).T,
        "typeT": edges(edge_type_9, 0), "typeM": type_flat.reshape(P, TILES),
        "dstM": dst_flat.reshape(TILES, P), "heads": head,
        "attrT": attr.T,
        "w0": np.concatenate([w0, b0]), "w1": w1, "b1r": rows(L1_gnn_b), "gam": rows(L1_gnn_gamma),
        "bet": rows(L1_gnn_beta), "weT": np.asarray(L3_gnn_We).T, "bec": np.asarray(L3_gnn_be).reshape(F, 1),
        "g1T": np.asarray(L3_gnn_W1).T, "g1b": np.asarray(L3_gnn_b1).reshape(F, 1),
        "g2T": np.asarray(L3_gnn_W2).T, "g2b": rows(L3_gnn_b2),
    }
    arrays = {n: np.ascontiguousarray(a) for n, a in arrays.items()}
    nc = bacc.Bacc("TRN2", target_bir_lowering=False, num_devices=1)
    args = [nc.dram_tensor(n, a.shape, mybir.dt.from_np(a.dtype), kind="ExternalInput").ap()
            for n, a in arrays.items()]
    out = nc.dram_tensor("out", (P, NT, F), FP32, kind="ExternalOutput").ap()
    build(nc, *args, out)
    r = run_bass_kernel_spmd(nc, [arrays], core_ids=[0])
    return r.results[0]["out"].transpose(1, 0, 2).reshape(NPAD, F)[:NODES]
```
